# Optimizing a Trainium2 kernel written in Bass

```python
import numpy as np
import jax
import jax.numpy as jnp

def _softmax(x, axis=-1):
    return jax.nn.softmax(x, axis=axis)

def _gelu(x):
    return jax.nn.gelu(x, approximate=True)

def _silu(x):
    return jax.nn.silu(x)

def _sigmoid(x):
    return jax.nn.sigmoid(x)

def _layernorm(x, axis=-1, eps=1e-05):
    m = jnp.mean(x, axis=axis, keepdims=True)
    v = jnp.var(x, axis=axis, keepdims=True)
    return (x - m) / jnp.sqrt(v + eps)

def _scatter_add(tgt, idx, src, axis=0):
    return tgt.at[idx].add(src)

def _segment_sum(src, seg, n):
    return jax.ops.segment_sum(src, seg, n)
kernel_name = 'mk_gnn_preln_d4_gnn_r64_bc1cad'

def setup_inputs(seed: int=0):
    np.random.seed(seed)
    _w = jnp.asarray

    def _rec_inputs():
        import jax
        import jax.numpy as jnp
        _gk = jax.random.key(seed)
        x = -0.000202 + 1 * jax.random.normal(jax.random.fold_in(_gk, 1), (50000, 64), jnp.float32)
        src = jax.random.randint(jax.random.fold_in(_gk, 2), (25000,), 0, 50000, jnp.int32)
        dst = jax.random.randint(jax.random.fold_in(_gk, 3), (25000,), 0, 50000, jnp.int32)
        _o = jnp.argsort(dst, stable=True)
        src = src[_o]
        dst = dst[_o]
        edge_type_8 = jax.random.randint(jax.random.fold_in(_gk, 13), (25000,), 0, 8, jnp.int32)
        edge_weight = -1.20086e-11 + 0.13101 * jax.random.normal(jax.random.fold_in(_gk, 14), (25000,), jnp.float32)
        return (x, src, dst, edge_type_8, edge_weight)
    x, src, dst, edge_type_8, edge_weight = _rec_inputs()

    def _L0_gnn_setup():
        import jax, jax.numpy as jnp
        import numpy as np
        N_NODES = 100000
        N_EDGES = 25000
        IN_DIM = 64
        OUT_DIM = 64
        key = jax.random.key(seed)
        k_x, k_e, k_wm, k_bm, k_wu, k_bu = jax.random.split(key, 6)
        x = jax.random.normal(k_x, (N_NODES, IN_DIM), dtype=jnp.float32)
        edge_index = jax.random.randint(k_e, (2, N_EDGES), 0, N_NODES, dtype=jnp.int64)
        lim_m = 1.0 / np.sqrt(2 * IN_DIM)
        lim_u = 1.0 / np.sqrt(IN_DIM + OUT_DIM)
        W_msg = jax.random.uniform(k_wm, (2 * IN_DIM, OUT_DIM), jnp.float32, -lim_m, lim_m)
        b_msg = jax.random.uniform(k_bm, (OUT_DIM,), jnp.float32, -lim_m, lim_m)
        W_upd = jax.random.uniform(k_wu, (IN_DIM + OUT_DIM, OUT_DIM), jnp.float32, -lim_u, lim_u)
        b_upd = jax.random.uniform(k_bu, (OUT_DIM,), jnp.float32, -lim_u, lim_u)
        return {'x': x, 'edge_index': edge_index, 'W_msg': W_msg, 'b_msg': b_msg, 'W_upd': W_upd, 'b_upd': b_upd}
    _L0_gnn_all = _L0_gnn_setup()
    _L0_gnn_in = {k: v for k, v in _L0_gnn_all.items() if k in ('W_msg', 'b_msg', 'W_upd', 'b_upd')}
    del _L0_gnn_all

    def _L1_gnn_setup():
        import jax, jax.numpy as jnp
        import numpy as np
        N_NODES = 100000
        N_EDGES = 15625
        IN_DIM = 64
        OUT_DIM = 64
        key = jax.random.key(seed)
        k1, k2, k3, k4, k5 = jax.random.split(key, 5)
        x = jax.random.normal(k1, (N_NODES, IN_DIM), dtype=jnp.float32)
        edge_index = jax.random.randint(k2, (2, N_EDGES), 0, N_NODES, dtype=jnp.int64)
        bound = 1.0 / np.sqrt(IN_DIM)
        W = jax.random.uniform(k3, (OUT_DIM, IN_DIM), minval=-bound, maxval=bound, dtype=jnp.float32)
        b = jax.random.uniform(k4, (OUT_DIM,), minval=-bound, maxval=bound, dtype=jnp.float32)
        return {'x': x, 'edge_index': edge_index, 'W': W, 'b': b}
    _L1_gnn_all = _L1_gnn_setup()
    _L1_gnn_in = {k: v for k, v in _L1_gnn_all.items() if k in ('W', 'b')}
    del _L1_gnn_all

    def _L2_gnn_setup():
        import jax, jax.numpy as jnp
        import numpy as np
        N, E, HID, NH, HD, NET = (50000, 12500, 64, 4, 16, 8)

        def _layer_norm(x, g, b, eps=1e-05):
            m = jnp.mean(x, axis=-1, keepdims=True)
            v = jnp.mean((x - m) ** 2, axis=-1, keepdims=True)
            return (x - m) * jax.lax.rsqrt(v + eps) * g + b
        key = jax.random.key(seed)
        ks = jax.random.split(key, 32)
        rn = lambda k, shape, s=0.05: jax.random.normal(k, shape, jnp.float32) * s
        return {'node_embeddings': jax.random.normal(ks[0], (N, HID), jnp.float32), 'edge_index': jax.random.randint(ks[1], (2, E), 0, N), 'edge_type': jax.random.randint(ks[2], (E,), 0, NET), 'task_embedding': jax.random.normal(ks[3], (HID,), jnp.float32), 'Wq': rn(ks[4], (HID, HID)), 'bq': jnp.zeros((HID,), jnp.float32), 'Wk': rn(ks[5], (HID, HID)), 'bk': jnp.zeros((HID,), jnp.float32), 'Wv': rn(ks[6], (HID, HID)), 'bv': jnp.zeros((HID,), jnp.float32), 'ek_tab': rn(ks[7], (NET, HID)), 'ev_tab': rn(ks[8], (NET, HID)), 'es_tab': rn(ks[9], (NET, NH)), 'eg_tab': jnp.exp(rn(ks[10], (NET, NH), 0.1)), 'Wo': rn(ks[11], (HID, HID)), 'bo': jnp.zeros((HID,), jnp.float32), 'ln1_g': jnp.ones((HID,), jnp.float32), 'ln1_b': jnp.zeros((HID,), jnp.float32), 'W1': rn(ks[12], (HID, 2 * HID)), 'b1': jnp.zeros((2 * HID,), jnp.float32), 'W2': rn(ks[13], (2 * HID, HID)), 'b2': jnp.zeros((HID,), jnp.float32), 'ln2_g': jnp.ones((HID,), jnp.float32), 'ln2_b': jnp.zeros((HID,), jnp.float32), 'Wf': rn(ks[14], (HID, 2 * HID)), 'bf': jnp.zeros((2 * HID,), jnp.float32)}
    _L2_gnn_all = _L2_gnn_setup()
    _L2_gnn_in = {k: v for k, v in _L2_gnn_all.items() if k in ('task_embedding', 'Wq', 'bq', 'Wk', 'bk', 'Wv', 'bv', 'ek_tab', 'ev_tab', 'es_tab', 'eg_tab', 'Wo', 'bo', 'ln1_g', 'ln1_b', 'W1', 'b1', 'W2', 'b2', 'ln2_g', 'ln2_b', 'Wf', 'bf')}
    del _L2_gnn_all

    def _L3_gnn_setup():
        import jax, jax.numpy as jnp
        import numpy as np
        N = 50000
        C = 64
        E_OFF = 12500
        N_SUB = 4
        M_TERMS = 20

        def _expm_multiply(x, edge_src, edge_dst, edge_w, t):
            n = x.shape[0]
            scale = -(t[0] / N_SUB)

            def A_apply(v):
                return scale * jax.ops.segment_sum(edge_w[:, None] * v[edge_dst], edge_src, num_segments=n)
            ks = jnp.arange(1, M_TERMS + 1, dtype=x.dtype)

            def substep(v, _):

                def taylor(carry, k):
                    term, acc = carry
                    term = A_apply(term) / k
                    return ((term, acc + term), None)
                (_, acc), _ = jax.lax.scan(taylor, (v, v), ks)
                return (acc, None)
            out, _ = jax.lax.scan(substep, x, None, length=N_SUB)
            return out
        key = jax.random.key(seed)
        k1, k2, k3, k4, k5 = jax.random.split(key, 5)
        src = jax.random.randint(k1, (E_OFF,), 0, N)
        dst = jax.random.randint(k2, (E_OFF,), 0, N)
        w = jax.random.uniform(k3, (E_OFF,), dtype=jnp.float32) / 16.0
        deg = jax.ops.segment_sum(w, src, num_segments=N)
        edge_src = jnp.concatenate([src, jnp.arange(N, dtype=src.dtype)])
        edge_dst = jnp.concatenate([dst, jnp.arange(N, dtype=dst.dtype)])
        edge_w = jnp.concatenate([-w, deg])
        x = jax.random.normal(k4, (N, C), dtype=jnp.float32)
        t = jax.random.uniform(k5, (1,), dtype=jnp.float32) * 0.2 + 1e-08
        return {'x': x, 'edge_src': edge_src, 'edge_dst': edge_dst, 'edge_w': edge_w, 't': t}
    _L3_gnn_all = _L3_gnn_setup()
    _L3_gnn_in = {k: v for k, v in _L3_gnn_all.items() if k in ('t',)}
    del _L3_gnn_all
    return {'x': x, 'src': src, 'dst': dst, 'edge_type_8': edge_type_8, 'edge_weight': edge_weight, 'L0_gnn_W_msg': _L0_gnn_in['W_msg'], 'L0_gnn_b_msg': _L0_gnn_in['b_msg'], 'L0_gnn_W_upd': _L0_gnn_in['W_upd'], 'L0_gnn_b_upd': _L0_gnn_in['b_upd'], 'L1_gnn_W': _L1_gnn_in['W'], 'L1_gnn_b': _L1_gnn_in['b'], 'L2_gnn_task_embedding': _L2_gnn_in['task_embedding'], 'L2_gnn_Wq': _L2_gnn_in['Wq'], 'L2_gnn_bq': _L2_gnn_in['bq'], 'L2_gnn_Wk': _L2_gnn_in['Wk'], 'L2_gnn_bk': _L2_gnn_in['bk'], 'L2_gnn_Wv': _L2_gnn_in['Wv'], 'L2_gnn_bv': _L2_gnn_in['bv'], 'L2_gnn_ek_tab': _L2_gnn_in['ek_tab'], 'L2_gnn_ev_tab': _L2_gnn_in['ev_tab'], 'L2_gnn_es_tab': _L2_gnn_in['es_tab'], 'L2_gnn_eg_tab': _L2_gnn_in['eg_tab'], 'L2_gnn_Wo': _L2_gnn_in['Wo'], 'L2_gnn_bo': _L2_gnn_in['bo'], 'L2_gnn_ln1_g': _L2_gnn_in['ln1_g'], 'L2_gnn_ln1_b': _L2_gnn_in['ln1_b'], 'L2_gnn_W1': _L2_gnn_in['W1'], 'L2_gnn_b1': _L2_gnn_in['b1'], 'L2_gnn_W2': _L2_gnn_in['W2'], 'L2_gnn_b2': _L2_gnn_in['b2'], 'L2_gnn_ln2_g': _L2_gnn_in['ln2_g'], 'L2_gnn_ln2_b': _L2_gnn_in['ln2_b'], 'L2_gnn_Wf': _L2_gnn_in['Wf'], 'L2_gnn_bf': _L2_gnn_in['bf'], 'L3_gnn_t': _L3_gnn_in['t']}

def reference(x, src, dst, edge_type_8, edge_weight, L0_gnn_W_msg, L0_gnn_b_msg, L0_gnn_W_upd, L0_gnn_b_upd, L1_gnn_W, L1_gnn_b, L2_gnn_task_embedding, L2_gnn_Wq, L2_gnn_bq, L2_gnn_Wk, L2_gnn_bk, L2_gnn_Wv, L2_gnn_bv, L2_gnn_ek_tab, L2_gnn_ev_tab, L2_gnn_es_tab, L2_gnn_eg_tab, L2_gnn_Wo, L2_gnn_bo, L2_gnn_ln1_g, L2_gnn_ln1_b, L2_gnn_W1, L2_gnn_b1, L2_gnn_W2, L2_gnn_b2, L2_gnn_ln2_g, L2_gnn_ln2_b, L2_gnn_Wf, L2_gnn_bf, L3_gnn_t):
    import jax
    import jax.numpy as jnp

    def _L0_gnn_ref(x, edge_index, W_msg, b_msg, W_upd, b_upd):
        import jax, jax.numpy as jnp
        import numpy as np
        N_NODES = 100000
        N_EDGES = 25000
        IN_DIM = 64
        OUT_DIM = 64
        num_nodes = x.shape[0]
        source, target = (edge_index[0], edge_index[1])
        edge_feats = jnp.concatenate([x[source], x[target]], axis=-1)
        messages = jax.nn.relu(edge_feats @ W_msg + b_msg)
        agg_sum = jax.ops.segment_sum(messages, target, num_segments=num_nodes)
        counts = jax.ops.segment_sum(jnp.ones_like(target, dtype=x.dtype), target, num_segments=num_nodes)
        aggregated = agg_sum / jnp.clip(counts, 1.0, None)[:, None]
        updated = jax.nn.relu(jnp.concatenate([x, aggregated], axis=-1) @ W_upd + b_upd)
        return updated

    def _L1_gnn_ref(x, edge_index, W, b):
        import jax, jax.numpy as jnp
        import numpy as np
        N_NODES = 100000
        N_EDGES = 15625
        IN_DIM = 64
        OUT_DIM = 64
        num_nodes = x.shape[0]
        source, target = (edge_index[0], edge_index[1])
        deg = jax.ops.segment_sum(jnp.ones_like(target, dtype=x.dtype), target, num_segments=num_nodes)
        deg = jnp.maximum(deg, 1.0)
        deg_inv_sqrt = deg ** (-0.5)
        norm = deg_inv_sqrt[source] * deg_inv_sqrt[target]
        messages = x[source] * norm[:, None]
        aggregated = jax.ops.segment_sum(messages, target, num_segments=num_nodes)
        aggregated = aggregated + x
        return aggregated @ W.T + b

    def _L2_gnn_ref(node_embeddings, edge_index, edge_type, task_embedding, Wq, bq, Wk, bk, Wv, bv, ek_tab, ev_tab, es_tab, eg_tab, Wo, bo, ln1_g, ln1_b, W1, b1, W2, b2, ln2_g, ln2_b, Wf, bf):
        import jax, jax.numpy as jnp
        import numpy as np
        N, E, HID, NH, HD, NET = (50000, 12500, 64, 4, 16, 8)

        def _layer_norm(x, g, b, eps=1e-05):
            m = jnp.mean(x, axis=-1, keepdims=True)
            v = jnp.mean((x - m) ** 2, axis=-1, keepdims=True)
            return (x - m) * jax.lax.rsqrt(v + eps) * g + b
        n = node_embeddings.shape[0]
        nh = es_tab.shape[1]
        hd = node_embeddings.shape[1] // nh
        scale = 1.0 / hd ** 0.5
        src, dst = (edge_index[0], edge_index[1])
        q = (node_embeddings @ Wq + bq).reshape(n, nh, hd)
        k = (node_embeddings @ Wk + bk).reshape(n, nh, hd)
        v = (node_embeddings @ Wv + bv).reshape(n, nh, hd)
        e_k = ek_tab[edge_type].reshape(-1, nh, hd)
        e_v = ev_tab[edge_type].reshape(-1, nh, hd)
        logits = jnp.sum(q[dst] * (k[src] + e_k), axis=-1) * scale + es_tab[edge_type]
        logits = logits + jnp.clip(jnp.log(eg_tab[edge_type]), -10.0, 10.0)
        mx = jax.ops.segment_max(logits, dst, num_segments=n)
        mx = jnp.where(jnp.isinf(mx), 0.0, mx)
        ex = jnp.exp(logits - mx[dst])
        sums = jax.ops.segment_sum(ex, dst, num_segments=n)
        attn = ex / jnp.maximum(sums[dst], 1e-12)
        msg = (v[src] + e_v) * attn[..., None]
        agg = jax.ops.segment_sum(msg.reshape(-1, nh * hd), dst, num_segments=n)
        agg = agg @ Wo + bo
        gb = task_embedding @ Wf + bf
        gamma, beta = (gb[:nh * hd], gb[nh * hd:])
        agg = agg * (1.0 + 0.5 * jnp.tanh(gamma))[None, :] + beta[None, :]
        x = _layer_norm(node_embeddings + agg, ln1_g, ln1_b)
        h = jax.nn.gelu(x @ W1 + b1, approximate=False) @ W2 + b2
        return _layer_norm(x + h, ln2_g, ln2_b)

    def _L3_gnn_ref(x, edge_src, edge_dst, edge_w, t):
        import jax, jax.numpy as jnp
        import numpy as np
        N = 50000
        C = 64
        E_OFF = 12500
        N_SUB = 4
        M_TERMS = 20

        def _expm_multiply(x, edge_src, edge_dst, edge_w, t):
            n = x.shape[0]
            scale = -(t[0] / N_SUB)

            def A_apply(v):
                return scale * jax.ops.segment_sum(edge_w[:, None] * v[edge_dst], edge_src, num_segments=n)
            ks = jnp.arange(1, M_TERMS + 1, dtype=x.dtype)

            def substep(v, _):

                def taylor(carry, k):
                    term, acc = carry
                    term = A_apply(term) / k
                    return ((term, acc + term), None)
                (_, acc), _ = jax.lax.scan(taylor, (v, v), ks)
                return (acc, None)
            out, _ = jax.lax.scan(substep, x, None, length=N_SUB)
            return out
        t = jnp.clip(t, 1e-08)
        return _expm_multiply(x, edge_src, edge_dst, edge_w, t)
    edge_index = jnp.stack([src, dst])
    h = jnp.maximum(_layernorm(x, axis=-1), 0.0)
    x = x + _L0_gnn_ref(h, edge_index, L0_gnn_W_msg, L0_gnn_b_msg, L0_gnn_W_upd, L0_gnn_b_upd)
    h = jnp.maximum(_layernorm(x, axis=-1), 0.0)
    x = x + _L1_gnn_ref(h, edge_index, L1_gnn_W, L1_gnn_b)
    h = jnp.maximum(_layernorm(x, axis=-1), 0.0)
    x = x + _L2_gnn_ref(h, edge_index, edge_type_8, L2_gnn_task_embedding, L2_gnn_Wq, L2_gnn_bq, L2_gnn_Wk, L2_gnn_bk, L2_gnn_Wv, L2_gnn_bv, L2_gnn_ek_tab, L2_gnn_ev_tab, L2_gnn_es_tab, L2_gnn_eg_tab, L2_gnn_Wo, L2_gnn_bo, L2_gnn_ln1_g, L2_gnn_ln1_b, L2_gnn_W1, L2_gnn_b1, L2_gnn_W2, L2_gnn_b2, L2_gnn_ln2_g, L2_gnn_ln2_b, L2_gnn_Wf, L2_gnn_bf)
    h = jnp.maximum(_layernorm(x, axis=-1), 0.0)
    x = x + _L3_gnn_ref(h, src, dst, edge_weight, L3_gnn_t)
    return x

_drawn_inputs = setup_inputs


def setup_inputs(seed=0):
    import zlib

    import numpy as np

    out = dict(_drawn_inputs(seed))
    spreads = {'L2_gnn_bq': (0.0, 2.0),
     'L2_gnn_bk': (0.0, 2.0),
     'L2_gnn_bv': (0.0, 0.513),
     'L2_gnn_bo': (0.0, 0.1),
     'L2_gnn_ln1_g': (1.0, 0.2),
     'L2_gnn_ln1_b': (0.0, 0.1),
     'L2_gnn_b1': (0.0, 0.619),
     'L2_gnn_b2': (0.0, 0.1),
     'L2_gnn_ln2_g': (1.0, 0.2),
     'L2_gnn_ln2_b': (0.0, 0.1),
     'L2_gnn_bf': (0.0, 0.1)}
    factors = {'edge_weight': 64.0,
     'L0_gnn_b_msg': 8.0,
     'L2_gnn_Wq': 66.046,
     'L2_gnn_Wk': 67.954,
     'L2_gnn_ek_tab': 200.0,
     'L2_gnn_ev_tab': 7.522,
     'L2_gnn_es_tab': 200.0,
     'L2_gnn_eg_tab': 200.0}
    for name, (base, spread) in spreads.items():
        noise = np.random.default_rng([zlib.crc32(name.encode()), seed]).standard_normal(out[name].shape)
        drawn = base * np.exp(spread * noise) if base else spread * noise
        out[name] = jnp.asarray(drawn.astype(out[name].dtype))
    for name, factor in factors.items():
        out[name] = (out[name] * factor).astype(out[name].dtype)
    return out
```

```python
import numpy as np
import concourse.bass as bass
from concourse import mybir
from contextlib import ExitStack

F32 = mybir.dt.float32
BF16 = mybir.dt.bfloat16
I32 = mybir.dt.int32
ALU = mybir.AluOpType
ACT = mybir.ActivationFunctionType
AX = mybir.AxisListType

P = 128
NODES, EDGES, C = 50000, 25000, 64
NH, HD, NET, FF = 4, 16, 8, 128
G = 28
J = 4
SUPER = -(-NODES // (P * G))
NP = SUPER * P * G
SUBS = G // J
CH = P * J
CHUNKS = 2 * -(-EDGES // (2 * CH))
EP = CHUNKS * CH
EPS = 1e-5
FAR = 1 << 17
NEG = -1e30
CV = C + NH
N_SUB, M_TERMS = 4, 20
STEPS = N_SUB * M_TERMS
SPARE = 2 * CH


def step_ratios():
    once = [1] * (M_TERMS + 1)
    for j in range(M_TERMS, 0, -1):
        once[j - 1] = once[j] * j
    poly = [1]
    for _ in range(N_SUB):
        new = [0] * (len(poly) + M_TERMS)
        for a, x in enumerate(poly):
            for b, y in enumerate(once):
                new[a + b] += x * y
        poly = new
    return [poly[k] / poly[k - 1] for k in range(1, len(poly))]


class Net:
    pass


def stage_semaphore(nc, ctx, name):
    s = nc.alloc_semaphore(name)
    ctx.callback(nc.clear_and_free_semaphores, [s])
    return s


def allocate(nc, ctx, net):
    def sb(name, shape, dt=F32):
        return ctx.enter_context(nc.sbuf_tensor(name, shape, dt))
    net.ident = sb("ident", [P, P])
    net.identb = sb("identb", [P, P], BF16)
    net.negidentb = sb("negidentb", [P, P], BF16)
    net.ones = sb("ones", [1, P])
    net.eps = sb("eps", [P, 1])
    net.iota8 = sb("iota8", [P, J, NET])
    net.w_msg = sb("w_msg", [P, C])
    net.b_msg = sb("b_msg", [C, 1])
    net.w_upd = sb("w_upd", [P, C])
    net.b_upd = sb("b_upd", [1, C])
    net.w_lin = sb("w_lin", [C, C])
    net.b_lin = sb("b_lin", [1, C])
    net.wq = sb("wq", [P, C])
    net.wk = sb("wk", [C, C])
    net.wv = sb("wv", [C, CV])
    net.tab_q = sb("tab_q", [NET, C])
    net.tab_k = sb("tab_k", [NET, C])
    net.tab_v = sb("tab_v", [NET, CV])
    net.tab_l = sb("tab_l", [NET, CV])
    net.head_sum = sb("head_sum", [C, CV])
    net.w_out = sb("w_out", [C, C])
    net.b_out = sb("b_out", [1, C])
    net.w1 = sb("w1", [C, FF])
    net.b1 = sb("b1", [FF, 1])
    net.w2 = sb("w2", [FF, C])
    net.b2 = sb("b2", [1, C])
    net.norms = sb("norms", [P, 4, C])


def prepare(nc, net):
    d = net.dram
    with ExitStack() as ctx:
        ctx.callback(nc.all_engine_barrier)
        def sb(name, shape, dt=F32):
            return ctx.enter_context(nc.sbuf_tensor(name, shape, dt))

        def sem(name):
            return stage_semaphore(nc, ctx, name)
        zeros = sb("zeros", [P, G * (C + 1)])
        task = sb("task", [C, 1])
        wf = sb("wf", [C, 2 * C])
        bf_row = sb("bf_row", [1, 2 * C])
        bo_row = sb("bo_row", [1, C])
        wo = sb("wo", [C, C])
        ek = sb("ek", [NET, C])
        bk = sb("bk", [NET, C])
        ev = sb("ev", [NET, C])
        bv = sb("bv", [NET, C])
        es = sb("es", [NET, NH])
        eg = sb("eg", [NET, NH])
        leg = sb("leg", [NET, NH])
        gb = sb("gb", [1, 2 * C])
        gate = sb("gate", [1, C])
        gated = sb("gated", [1, C])
        ps = ctx.enter_context(nc.psum_tensor("ps_gate", [P, 512], F32))
        ps2 = ctx.enter_context(nc.psum_tensor("ps_gate2", [P, 512], F32))
        loaded = sem("weights_loaded")
        cleared = sem("tables_cleared")
        zero_ready = sem("zero_ready")
        film_done = sem("film_done")
        gb_ready = sem("gb_ready")
        tanh_done = sem("tanh_done")
        gate_ready = sem("gate_ready")
        spread_done = sem("spread_done")
        log_done = sem("log_done")
        with nc.Block() as block:
            loads = [
                (net.ident[:, :], d["c_ident"][:, :]), (net.ones[:, :], d["c_ones"][:, :]),
                (net.iota8[:, :, :], d["c_iota8"][:, :, :]), (net.head_sum[:, :], d["c_head_sum"][:, :]),
                (net.w_msg[:, :], d["L0_gnn_W_msg"][:, :]), (net.b_msg[:, :], d["L0_gnn_b_msg"][:, None]),
                (net.w_upd[:, :], d["L0_gnn_W_upd"][:, :]), (net.b_upd[:, :], d["L0_gnn_b_upd"][None, :]),
                (net.w_lin[:, :], d["L1_gnn_WT"][:, :]), (net.b_lin[:, :], d["L1_gnn_b"][None, :]),
                (net.wq[C:, :], d["L2_gnn_Wq"][:, :]), (net.wk[:, :], d["L2_gnn_Wk"][:, :]),
                (net.wv[:, 0:C], d["L2_gnn_Wv"][:, :]),
                (net.tab_q[:, :], d["L2_gnn_bq"][None, :].to_broadcast([NET, C])),
                (bk[:, :], d["L2_gnn_bk"][None, :].to_broadcast([NET, C])),
                (bv[:, :], d["L2_gnn_bv"][None, :].to_broadcast([NET, C])),
                (ek[:, :], d["L2_gnn_ek_tab"][:, :]), (ev[:, :], d["L2_gnn_ev_tab"][:, :]),
                (es[:, :], d["L2_gnn_es_tab"][:, :]), (eg[:, :], d["L2_gnn_eg_tab"][:, :]),
                (task[:, :], d["L2_gnn_task_embedding"][:, None]), (wf[:, :], d["L2_gnn_Wf"][:, :]),
                (bf_row[:, :], d["L2_gnn_bf"][None, :]), (bo_row[:, :], d["L2_gnn_bo"][None, :]),
                (wo[:, :], d["L2_gnn_Wo"][:, :]),
                (net.w1[:, :], d["L2_gnn_W1"][:, :]), (net.b1[:, :], d["L2_gnn_b1"][:, None]),
                (net.w2[:, :], d["L2_gnn_W2"][:, :]), (net.b2[:, :], d["L2_gnn_b2"][None, :]),
                (net.norms[:, 0, :], d["L2_gnn_ln1_g"][None, :].to_broadcast([P, C])),
                (net.norms[:, 1, :], d["L2_gnn_ln1_b"][None, :].to_broadcast([P, C])),
                (net.norms[:, 2, :], d["L2_gnn_ln2_g"][None, :].to_broadcast([P, C])),
                (net.norms[:, 3, :], d["L2_gnn_ln2_b"][None, :].to_broadcast([P, C])),
            ]
            all_loaded = 16 * len(loads)

            @block.sync
            def _(sp):
                for dst, src in loads:
                    sp.dma_start(dst, src).then_inc(loaded, 16)
                sp.wait_ge(zero_ready, 1)
                for table in (net.agg0, net.agg1, net.agg2, net.term[1]):
                    wide = table.shape[1]
                    for i in range(SUPER):
                        rows = table[i * P * G:(i + 1) * P * G, :].rearrange("(p g) c -> p (g c)", p=P)
                        sp.dma_start(rows, zeros[:, 0:G * wide]).then_inc(cleared, 16)
                for table in (net.out, *net.term):
                    wide = table.shape[1]
                    rows = table[NP:NP + SPARE, :].rearrange("(p g) c -> p (g c)", p=P)
                    sp.dma_start(rows, zeros[:, 0:SPARE // P * wide]).then_inc(cleared, 16)
                sp.wait_ge(cleared, (4 * SUPER + 3) * 16)

            @block.tensor
            def _(pe):
                pe.wait_ge(loaded, all_loaded)
                nc.tensor.matmul(ps[0:1, 0:2 * C], task[:, :], wf[:, :], start=True, stop=True).then_inc(film_done, 1)
                pe.wait_ge(gate_ready, 1)
                nc.tensor.matmul(ps2[0:C, 0:C], net.ones[0:1, 0:C], gate[:, :], start=True, stop=True).then_inc(spread_done, 1)

            @block.scalar
            def _(act):
                act.wait_ge(gb_ready, 1)
                nc.scalar.activation(gate[:, :], gb[:, 0:C], ACT.Tanh).then_inc(tanh_done, 1)
                act.wait_ge(loaded, all_loaded)
                nc.scalar.activation(leg[:, :], eg[:, :], ACT.Ln).then_inc(log_done, 1)

            @block.vector
            def _(v):
                nc.vector.memset(zeros[:, :], 0.0).then_inc(zero_ready, 1)
                v.wait_ge(loaded, all_loaded)
                nc.vector.tensor_copy(net.identb[:, :], net.ident[:, :])
                nc.vector.tensor_scalar(net.negidentb[:, :], net.ident[:, :], NEG, None, ALU.mult)
                nc.vector.memset(net.wv[:, C:CV], 0.0)
                nc.vector.memset(net.eps[:, :], EPS)
                nc.vector.memset(net.tab_v[:, C:CV], 1.0)
                nc.vector.tensor_tensor(net.tab_k[:, :], ek[:, :], bk[:, :], ALU.add)
                nc.vector.tensor_tensor(net.tab_v[:, 0:C], ev[:, :], bv[:, :], ALU.add)
                v.wait_ge(film_done, 1)
                nc.vector.tensor_tensor(gb[:, :], ps[0:1, 0:2 * C], bf_row[:, :], ALU.add).then_inc(gb_ready, 1)
                v.wait_ge(tanh_done, 1)
                nc.vector.tensor_scalar(gate[:, :], gate[:, :], 0.5, 1.0, ALU.mult, ALU.add).then_inc(gate_ready, 1)
                v.drain()
                nc.vector.tensor_tensor(gated[:, :], bo_row[:, :], gate[:, :], ALU.mult)
                v.drain()
                nc.vector.tensor_tensor(net.b_out[:, :], gated[:, :], gb[:, C:2 * C], ALU.add)
                v.wait_ge(spread_done, 1)
                nc.vector.tensor_tensor(net.w_out[:, :], wo[:, :], ps2[0:C, 0:C], ALU.mult)
                v.wait_ge(log_done, 1)
                nc.vector.tensor_scalar(leg[:, :], leg[:, :], -10.0, 10.0, ALU.max, ALU.min)
                v.drain()
                nc.vector.tensor_tensor(es[:, :], es[:, :], leg[:, :], ALU.add)
                v.drain()
                nc.vector.tensor_copy(net.tab_l[:, 0:C].rearrange("e (h d) -> e h d", d=HD),
                                      es[:, :].unsqueeze(2).to_broadcast([NET, NH, HD]))
                nc.vector.tensor_copy(net.tab_l[:, C:CV], es[:, :])


def rows_of(table, chunk, rows, lo=0, hi=None):
    return table[bass.ds(chunk * (P * rows), P * rows), :].rearrange("(p g) c -> p g c", p=P)


def first_norm(nc, net):
    with ExitStack() as ctx:
        ctx.callback(nc.all_engine_barrier)
        def sb(name, shape, dt=F32):
            return ctx.enter_context(nc.sbuf_tensor(name, shape, dt))

        def sem(name):
            return stage_semaphore(nc, ctx, name)
        X = [sb(f"n_x{s}", [P, G, C]) for s in range(2)]
        XC = [sb(f"n_xc{s}", [P, G, C]) for s in range(2)]
        SQ = [sb(f"n_sq{s}", [P, G, C]) for s in range(2)]
        H = [sb(f"n_h{s}", [P, G, C]) for s in range(2)]
        mean = [sb(f"n_mean{s}", [P, G]) for s in range(2)]
        rstd = [sb(f"n_rstd{s}", [P, G]) for s in range(2)]
        loaded = [sem(f"n_loaded{s}") for s in range(2)]
        stored = [sem(f"n_stored{s}") for s in range(2)]
        centred, squared, var_ready, rstd_ready, normed, relu_done = (
            sem(f"n_{x}") for x in ("centred", "squared", "var_ready", "rstd_ready", "normed", "relu_done"))
        with nc.Block() as block:
            @block.sync
            def _(sp):
                for s in range(2):
                    sp.dma_start(X[s][:, :, :], rows_of(net.x_in, s, G)).then_inc(loaded[s], 16)
                with sp.Fori(1, SUPER // 2) as t:
                    for s in range(2):
                        sp.wait_ge(centred, 2 * t + s - 1)
                        sp.dma_start(X[s][:, :, :], rows_of(net.x_in, 2 * t + s, G)).then_inc(loaded[s], 16)

            @block.vector
            def _(v):
                with v.Fori(0, SUPER // 2) as t:
                    for s in range(2):
                        v.wait_ge(loaded[s], 16 * t + 16)
                        nc.vector.tensor_reduce(mean[s][:, :], X[s][:, :, :], AX.X, ALU.add)
                        v.drain()
                        nc.vector.tensor_scalar(mean[s][:, :], mean[s][:, :], 1.0 / C, None, ALU.mult)
                        v.drain()
                        nc.vector.tensor_tensor(XC[s][:, :, :], X[s][:, :, :],
                                                mean[s][:, :].unsqueeze(2).to_broadcast([P, G, C]),
                                                ALU.subtract).then_inc(centred, 1)
                    for s in range(2):
                        v.wait_ge(squared, 2 * t + s + 1)
                        nc.vector.tensor_reduce(rstd[s][:, :], SQ[s][:, :, :], AX.X, ALU.add).then_inc(var_ready, 1)
                    for s in range(2):
                        v.wait_ge(rstd_ready, 2 * t + s + 1)
                        nc.vector.reciprocal(rstd[s][:, :], rstd[s][:, :])
                        v.drain()
                        v.wait_ge(stored[s], 16 * t)
                        nc.vector.tensor_tensor(H[s][:, :, :], XC[s][:, :, :],
                                                rstd[s][:, :].unsqueeze(2).to_broadcast([P, G, C]),
                                                ALU.mult).then_inc(normed, 1)

            @block.scalar
            def _(act):
                with act.Fori(0, SUPER // 2) as t:
                    for s in range(2):
                        act.wait_ge(centred, 2 * t + s + 1)
                        nc.scalar.activation(SQ[s][:, :, :], XC[s][:, :, :], ACT.Square, scale=C ** -0.5).then_inc(squared, 1)
                    for s in range(2):
                        act.wait_ge(var_ready, 2 * t + s + 1)
                        nc.scalar.activation(rstd[s][:, :], rstd[s][:, :], ACT.Sqrt, bias=net.eps[:, :]).then_inc(rstd_ready, 1)
                    for s in range(2):
                        act.wait_ge(normed, 2 * t + s + 1)
                        nc.scalar.activation(H[s][:, :, :], H[s][:, :, :], ACT.Relu).then_inc(relu_done, 1)
                        act.wait_ge(relu_done, 2 * t + s + 1)
                        act.dma_start(rows_of(net.h0, 2 * t + s, G), H[s][:, :, :]).then_inc(stored[s], 16)
                for s in range(2):
                    act.wait_ge(stored[s], 16 * (SUPER // 2))


def edge_sums(nc, net, layer):
    two = layer != 1
    table = (net.h0, net.h1d, net.h2)[layer]
    agg = (net.agg0, net.agg1, net.agg2)[layer]
    wide = C + 1 if layer == 1 else C
    rows = (C + 1, C, CV)[layer]
    outw = (C + 1, C, C)[layer]
    n_gather = 8 if two else 4
    n = f"e{layer}_"
    with ExitStack() as ctx:
        ctx.callback(nc.all_engine_barrier)
        def sb(name, shape, dt=F32):
            return ctx.enter_context(nc.sbuf_tensor(n + name, shape, dt))

        def ps(name):
            return ctx.enter_context(nc.psum_tensor(n + name, [P, 512], F32))

        def sem(name):
            return stage_semaphore(nc, ctx, n + name)
        src = [sb(f"src{s}", [P, J], I32) for s in range(2)]
        dst = [sb(f"dst{s}", [P, J + 2], I32) for s in range(2)]
        etype = [sb(f"etype{s}", [P, J], I32) for s in range(2)]
        keep = [sb(f"keep{s}", [P, J], BF16) for s in range(2)]
        fresh = [sb(f"fresh{s}", [P, J], BF16) for s in range(2)]
        same = [sb(f"same{s}", [P, J]) for s in range(2)]
        end = [sb(f"end{s}", [P, J], I32) for s in range(2)]
        ends = [sb(f"ends{s}", [P, J, 2 * wide if two else wide]) for s in range(2)]
        out = [sb(f"out{s}", [P, J, outw]) for s in range(2)]
        scan = [sb(f"scan{s}", [rows, CH]) for s in range(2)]
        feat = sb("feat", [P if two else C, CH])
        msg = sb("msg", [rows, CH])
        y = sb("y", [P, J, C])
        pt = ps("pt")
        pk = ps("pk")
        pm = ps("pm")
        pr = ps("pr")
        loaded = [sem(f"loaded{s}") for s in range(2)]
        gathered = [sem(f"gathered{s}") for s in range(2)]
        scattered = [sem(f"scattered{s}") for s in range(2)]
        names = ("flags", "y_ready", "turned", "kept", "feat_ready", "msg_mm", "msg_ready", "scanned", "back", "out_ready",
                 "pool_turn", "pe_turn")
        (flags, y_ready, turned, kept, feat_ready, msg_mm, msg_ready, scanned, back, out_ready, pool_turn,
         pe_turn) = map(sem, names)
        if layer == 2:
            onehot = sb("onehot", [P, J, NET])
            oht = sb("oht", [NET, CH])
            qs = sb("qs", [C, CH])
            prod = sb("prod", [C, CH])
            mx = [sb(f"mx{s}", [CV, CH + 1]) for s in range(2)]
            lm = sb("lm", [CV, CH])
            dm = sb("dm", [CV, CH])
            pexp = sb("pexp", [CV, CH])
            rexp = sb("rexp", [CV, CH])
            negs = sb("negs", [CV, CH])
            dsum = sb("dsum", [P, J, NH])
            pq, pkk, pl, pg = ps("pq"), ps("pkk"), ps("pl"), ps("pg")
            (onehot_ready, oht_mm, oht_ready, q_ready, prod_ready, logits, lm_ready, p_ready, dm_ready, r_ready,
             q_copied) = map(sem, (
                 "onehot_ready", "oht_mm", "oht_ready", "q_ready", "prod_ready", "logits", "lm_ready", "p_ready", "dm_ready",
                 "r_ready", "q_copied"))

        edge_src = net.src.rearrange("(n p j) -> n p j", p=P, j=J)
        edge_typ = net.etype.rearrange("(n p j) -> n p j", p=P, j=J)

        def dst_rows(c):
            first = net.dst_ext[bass.ds(c * CH, CH)].rearrange("(p j) -> p j", j=J)
            last = net.dst_ext[bass.ds(c * CH + J, CH)].rearrange("(p j) -> p j", j=J)
            return first, last[:, 0:2]

        n_loads = 4 if layer == 2 else 3
        with nc.Block() as block:
            @block.sync
            def _(sp):
                def load(c, s):
                    first, last = dst_rows(c)
                    sp.dma_start(src[s][:, :], edge_src[c, :, :] if isinstance(c, int) else edge_src[bass.ds(c, 1), :, :].rearrange("o p j -> (o p) j")).then_inc(loaded[s], 16)
                    sp.dma_start(dst[s][:, 0:J], first).then_inc(loaded[s], 16)
                    sp.dma_start(dst[s][:, J:J + 2], last).then_inc(loaded[s], 16)
                    if layer == 2:
                        sp.dma_start(etype[s][:, :], edge_typ[c, :, :] if isinstance(c, int) else edge_typ[bass.ds(c, 1), :, :].rearrange("o p j -> (o p) j")).then_inc(loaded[s], 16)
                for s in range(2):
                    load(s, s)
                with sp.Fori(1, CHUNKS // 2) as t:
                    for s in range(2):
                        sp.wait_ge(gathered[s], 16 * n_gather * t)
                        sp.wait_ge(flags, 2 * t + s - 1)
                        if layer == 2:
                            sp.wait_ge(onehot_ready, 2 * t + s - 1)
                        load(2 * t + s, s)

            @block.gpsimd
            def _(pool):
                def gather(t, s):
                    pool.wait_ge(loaded[s], 16 * n_loads * (t + 1))
                    pool.wait_ge(turned if two else y_ready, 2 * t + s + 1)
                    pool.sem_inc(pool_turn, 1)
                    for j in range(J):
                        pool.indirect_dma_start(ends[s][:, j, 0:wide], None, table[:, :],
                                                bass.IndirectOffsetOnAxis(ap=src[s][:, j:j + 1], axis=0)).then_inc(gathered[s], 16)
                        if two:
                            pool.indirect_dma_start(ends[s][:, j, wide:2 * wide], None, table[:, :],
                                                    bass.IndirectOffsetOnAxis(ap=dst[s][:, 1 + j:2 + j], axis=0)).then_inc(gathered[s], 16)

                def scatter(t, s):
                    pool.wait_ge(out_ready, 2 * t + s + 1)
                    pool.sem_inc(pool_turn, 1)
                    for j in range(J):
                        pool.indirect_dma_start(agg[:, :], bass.IndirectOffsetOnAxis(ap=end[s][:, j:j + 1], axis=0),
                                                out[s][:, j, :], None, bounds_check=NP - 1, oob_is_err=False).then_inc(scattered[s], 16)
                gather(0, 0)
                with pool.Fori(0, CHUNKS // 2 - 1) as t:
                    gather(t, 1)
                    scatter(t, 0)
                    gather(t + 1, 0)
                    scatter(t, 1)
                last = CHUNKS // 2 - 1
                gather(last, 1)
                scatter(last, 0)
                scatter(last, 1)
                for s in range(2):
                    pool.wait_ge(scattered[s], 16 * J * (CHUNKS // 2))

            @block.vector
            def _(v):
                nc.vector.memset(scan[1][:, :], 0.0)
                if layer == 0:
                    nc.vector.memset(msg[C:C + 1, :], 1.0)
                if layer == 2:
                    nc.vector.memset(mx[1][:, :], 0.0)
                if layer == 1:
                    for _ in range(2):
                        v.sem_inc(y_ready, 1)
                v.drain()

                def make_flags(t, s):
                    v.wait_ge(loaded[s], 16 * n_loads * (t + 1))
                    v.wait_ge(scattered[s], 16 * J * t)
                    nc.vector.tensor_tensor(keep[s][:, :], dst[s][:, 1:J + 1], dst[s][:, 0:J], ALU.is_equal)
                    if layer == 2:
                        nc.vector.tensor_tensor(fresh[s][:, :], dst[s][:, 1:J + 1], dst[s][:, 0:J], ALU.not_equal)
                    nc.vector.tensor_tensor(same[s][:, :], dst[s][:, 1:J + 1], dst[s][:, 2:J + 2], ALU.is_equal)
                    v.drain()
                    nc.vector.scalar_tensor_tensor(end[s][:, :], same[s][:, :], float(FAR), dst[s][:, 1:J + 1],
                                                   ALU.mult, ALU.add).then_inc(flags, 1)

                def sums(t, s):
                    k = 2 * t + s + 1
                    if layer == 1:
                        v.wait_ge(gathered[s], 16 * n_gather * (t + 1))
                        v.wait_ge(turned, k - 1)
                        nc.vector.tensor_tensor(y[:, :, :], ends[s][:, :, 0:C],
                                                ends[s][:, :, C:C + 1].to_broadcast([P, J, C]), ALU.mult).then_inc(y_ready, 1)
                    if layer == 2:
                        v.wait_ge(oht_mm, k - 1)
                        nc.vector.tensor_tensor(onehot[:, :, :], etype[s][:, :].unsqueeze(2).to_broadcast([P, J, NET]),
                                                net.iota8[:, :, :], ALU.is_equal).then_inc(onehot_ready, 1)
                        v.wait_ge(q_copied, k)
                        v.wait_ge(q_ready, k)
                        nc.vector.tensor_tensor(prod[:, :], qs[:, :], pkk[0:C, :], ALU.mult).then_inc(prod_ready, 1)
                        v.wait_ge(kept, k)
                        nc.vector.tensor_copy(negs[:, :], pg[0:CV, :])
                        nc.vector.tensor_copy(mx[s][:, 0:1], mx[1 - s][:, CH:CH + 1])
                        v.drain()
                        v.wait_ge(logits, k)
                        nc.vector.tensor_tensor_scan(mx[s][:, 1:CH + 1], negs[:, :], pl[0:CV, :], mx[1 - s][:, CH:CH + 1],
                                                     ALU.add, ALU.max)
                        v.drain()
                        nc.vector.tensor_tensor(lm[:, :], pl[0:CV, :], mx[s][:, 1:CH + 1], ALU.subtract).then_inc(lm_ready, 1)
                        nc.vector.tensor_tensor(dm[:, :], negs[:, :], mx[s][:, 0:CH], ALU.add)
                        v.drain()
                        nc.vector.tensor_tensor(dm[:, :], dm[:, :], mx[s][:, 1:CH + 1], ALU.subtract).then_inc(dm_ready, 1)
                        v.wait_ge(p_ready, k)
                        nc.vector.tensor_tensor(msg[:, :], pexp[:, :], pm[0:CV, :], ALU.mult)
                        v.drain()
                        v.wait_ge(r_ready, k)
                        v.wait_ge(back, k - 1)
                        nc.vector.tensor_tensor_scan(scan[s][:, :], rexp[:, :], msg[:, :], scan[1 - s][:, CH - 1:CH],
                                                     ALU.mult, ALU.add).then_inc(scanned, 1)
                    else:
                        v.wait_ge(msg_ready, k)
                        v.wait_ge(kept, k)
                        nc.vector.tensor_tensor_scan(scan[s][:, :], pk[0:rows, :], msg[:, :], scan[1 - s][:, CH - 1:CH],
                                                     ALU.mult, ALU.add).then_inc(scanned, 1)
                    v.wait_ge(back, k)
                    sums_rows = pr[:, 0:J * rows].rearrange("p (j c) -> p j c", c=rows)
                    if layer == 2:
                        nc.vector.tensor_scalar(dsum[:, :, :], sums_rows[:, :, C:CV], 1e-12, None, ALU.max)
                        v.drain()
                        nc.vector.reciprocal(dsum[:, :, :], dsum[:, :, :])
                        v.drain()
                        for j in range(J):
                            last = nc.vector.tensor_tensor(
                                out[s][:, j, :].rearrange("p (h d) -> p h d", d=HD),
                                sums_rows[:, j, 0:C].rearrange("p (h d) -> p h d", d=HD),
                                dsum[:, j, :].unsqueeze(2).to_broadcast([P, NH, HD]), ALU.mult)
                        last.then_inc(out_ready, 1)
                    else:
                        nc.vector.tensor_copy(out[s][:, :, :], sums_rows).then_inc(out_ready, 1)

                with v.Fori(0, CHUNKS // 2) as t:
                    for s in range(2):
                        make_flags(t, s)
                        sums(t, s)

            @block.tensor
            def _(pe):
                if two:
                    for _ in range(2):
                        pe.sem_inc(turned, 1)
                with pe.Fori(0, CHUNKS // 2) as t:
                    for s in range(2):
                        k = 2 * t + s + 1
                        if two:
                            pe.wait_ge(gathered[s], 16 * n_gather * (t + 1))
                            pe.wait_ge(feat_ready, k - 1)
                            pe.sem_inc(pe_turn, 1)
                            for j in range(J):
                                last = nc.tensor.transpose(pt[:, j:CH:J], ends[s][:, j, :], net.ident[:, :])
                        else:
                            pe.wait_ge(y_ready, k + 2)
                            pe.wait_ge(feat_ready, k - 1)
                            pe.sem_inc(pe_turn, 1)
                            for j in range(J):
                                last = nc.tensor.transpose(pt[0:C, j:CH:J], y[:, j, :], net.ident[:, :])
                        last.then_inc(turned, 1)
                        pe.wait_ge(flags, k)
                        pe.wait_ge(scanned, k - 1)
                        if layer == 2:
                            for j in range(J):
                                last = nc.tensor.matmul(pg[0:CV, j:CH:J], fresh[s][:, j:j + 1].to_broadcast([P, CV]),
                                                        net.negidentb[:, :], start=True, stop=True)
                            last.then_inc(kept, 1)
                            pe.wait_ge(onehot_ready, k)
                            pe.sem_inc(pe_turn, 1)
                            for j in range(J):
                                last = nc.tensor.transpose(pk[0:NET, j:CH:J], onehot[:, j, :], net.ident[:, :])
                            last.then_inc(oht_mm, 1)
                            pe.wait_ge(oht_ready, k)
                            pe.wait_ge(feat_ready, k)
                            pe.sem_inc(pe_turn, 1)
                            nc.tensor.matmul(pq[0:C, :], net.wq[C:P, :], feat[C:P, :], start=True, stop=False)
                            nc.tensor.matmul(pq[0:C, :], net.tab_q[:, :], oht[:, :], start=False, stop=True)
                            nc.tensor.matmul(pkk[0:C, :], net.wk[:, :], feat[0:C, :], start=True, stop=False)
                            nc.tensor.matmul(pkk[0:C, :], net.tab_k[:, :], oht[:, :], start=False, stop=True).then_inc(q_ready, 1)
                            nc.tensor.matmul(pm[0:CV, :], net.wv[:, :], feat[0:C, :], start=True, stop=False)
                            nc.tensor.matmul(pm[0:CV, :], net.tab_v[:, :], oht[:, :], start=False, stop=True)
                            pe.wait_ge(prod_ready, k)
                            nc.tensor.matmul(pl[0:CV, :], net.head_sum[:, :], prod[:, :], start=True, stop=False)
                            nc.tensor.matmul(pl[0:CV, :], net.tab_l[:, :], oht[:, :], start=False, stop=True).then_inc(logits, 1)
                        else:
                            for j in range(J):
                                last = nc.tensor.matmul(pk[0:rows, j:CH:J], keep[s][:, j:j + 1].to_broadcast([P, rows]),
                                                        net.identb[:, :], start=True, stop=True)
                            last.then_inc(kept, 1)
                            if layer == 0:
                                pe.wait_ge(feat_ready, k)
                                nc.tensor.matmul(pm[0:C, :], net.w_msg[:, :], feat[:, :], start=True, stop=True).then_inc(msg_mm, 1)
                        pe.wait_ge(scanned, k)
                        pe.wait_ge(out_ready, k - 1)
                        pe.sem_inc(pe_turn, 1)
                        for j in range(J):
                            last = nc.tensor.transpose(pr[:, j * rows:(j + 1) * rows], scan[s][:, j:CH:J], net.ident[0:rows, 0:rows])
                        last.then_inc(back, 1)

            @block.scalar
            def _(act):
                with act.Fori(0, CHUNKS // 2) as t:
                    for s in range(2):
                        k = 2 * t + s + 1
                        if layer == 0:
                            act.wait_ge(turned, k + 2)
                            nc.scalar.activation(feat[:, :], pt[:, :], ACT.Copy).then_inc(feat_ready, 1)
                            act.wait_ge(msg_mm, k)
                            act.wait_ge(scanned, k - 1)
                            nc.scalar.activation(msg[0:C, :], pm[0:C, :], ACT.Relu, bias=net.b_msg[:, :]).then_inc(msg_ready, 1)
                        elif layer == 1:
                            act.wait_ge(turned, k)
                            act.wait_ge(scanned, k - 1)
                            nc.scalar.activation(msg[:, :], pt[0:C, :], ACT.Copy)
                            act.drain()
                            act.sem_inc(feat_ready, 1)
                            act.sem_inc(msg_ready, 1)
                        else:
                            act.wait_ge(turned, k + 2)
                            nc.scalar.activation(feat[:, :], pt[:, :], ACT.Copy).then_inc(feat_ready, 1)
                            act.wait_ge(oht_mm, k)
                            act.wait_ge(logits, k - 1)
                            nc.scalar.activation(oht[:, :], pk[0:NET, :], ACT.Copy).then_inc(oht_ready, 1)
                            act.wait_ge(q_ready, k)
                            nc.scalar.activation(qs[:, :], pq[0:C, :], ACT.Copy).then_inc(q_copied, 1)
                            act.wait_ge(lm_ready, k)
                            nc.scalar.activation(pexp[:, :], lm[:, :], ACT.Exp).then_inc(p_ready, 1)
                            act.wait_ge(dm_ready, k)
                            nc.scalar.activation(rexp[:, :], dm[:, :], ACT.Exp).then_inc(r_ready, 1)


def node_update(nc, net, layer):
    n = f"u{layer}_"
    feats = P if layer == 0 else C
    aggw = C + 1 if layer == 0 else C
    hw = C + 1 if layer == 1 else C
    with ExitStack() as ctx:
        ctx.callback(nc.all_engine_barrier)
        def sb(name, shape, dt=F32):
            return ctx.enter_context(nc.sbuf_tensor(n + name, shape, dt))

        def ps(name):
            return ctx.enter_context(nc.psum_tensor(n + name, [P, 512], F32))

        def sem(name):
            return stage_semaphore(nc, ctx, n + name)
        X = [sb(f"x{s}", [P, G, C]) for s in range(2)]
        A = [sb(f"a{s}", [P, G, aggw]) for s in range(2)]
        Z = [sb(f"z{s}", [P, G, P if layer == 0 else hw]) for s in range(2)]
        H = [sb(f"h{s}", [P, G, C if layer == 1 else C + 1]) for s in range(2)]
        XC = sb("xc", [P, G, C])
        SQ = sb("sq", [P, G, C])
        mean = sb("mean", [P, G])
        rstd = sb("rstd", [P, G])
        zt = [sb(f"zt{b}", [feats, CH]) for b in range(2)]
        pt = [ps(f"pt{b}") for b in range(2)]
        po = [ps(f"po{b}") for b in range(2)]
        loaded = [sem(f"loaded{s}") for s in range(2)]
        stored = [sem(f"stored{s}") for s in range(2)]
        names = ("z_ready", "turned", "zt_ready", "mm_done", "evacuated", "centred", "squared", "var_ready", "rstd_ready",
                 "normed", "relu_done", "deg_ready", "dinv_ready", "tail_ready", "pe_turn")
        (z_ready, turned, zt_ready, mm_done, evacuated, centred, squared, var_ready, rstd_ready, normed, relu_done,
         deg_ready, dinv_ready, tail_ready, pe_turn) = map(sem, names)
        if layer == 2:
            T = sb("t", [P, G, C])
            u = [sb(f"u{b}", [FF, CH]) for b in range(2)]
            pf = [ps(f"pf{b}") for b in range(2)]
            up_done, gelu_done, t_ready = map(sem, ("up_done", "gelu_done", "t_ready"))
        bias = (net.b_upd, net.b_lin, net.b_out)[layer]
        weight = (net.w_upd, net.w_lin, net.w_out)[layer]
        x_in = (net.x_in, net.x1, net.x2)[layer]
        h_in = (net.h0, net.h1d, net.h2)[layer]
        agg = (net.agg0, net.agg1, net.agg2)[layer]
        x_out = (net.x1, net.x2, net.out)[layer]
        h_out = (net.h1d, net.h2, net.term[0])[layer]
        MM = 2 if layer == 2 else 1
        NORMS = 3 if layer == 2 else 1

        def b_of(s, i):
            return (s * SUBS + i) % 2
        with nc.Block() as block:
            @block.sync
            def _(sp):
                def load(c, s):
                    sp.dma_start(X[s][:, :, :], rows_of(x_in, c, G)).then_inc(loaded[s], 16)
                    sp.dma_start(A[s][:, :, :], rows_of(agg, c, G)).then_inc(loaded[s], 16)
                    sp.dma_start(Z[s][:, :, 0:hw], rows_of(h_in, c, G)).then_inc(loaded[s], 16)
                for s in range(2):
                    load(s, s)
                with sp.Fori(1, SUPER // 2) as t:
                    for s in range(2):
                        sp.wait_ge(stored[s], 32 * t)
                        load(2 * t + s, s)

            @block.tensor
            def _(pe):
                with pe.Fori(0, SUPER // 2) as t:
                    for s in range(2):
                        k = 2 * t + s
                        for m in range(MM):
                            if m == 0:
                                pe.wait_ge(z_ready, k + 1)
                            else:
                                pe.wait_ge(t_ready, k + 1)

                            def turn(i):
                                q = (k * MM + m) * SUBS + i
                                pe.wait_ge(zt_ready, q)
                                pe.sem_inc(pe_turn, 1)
                                source = Z[s] if layer < 2 else (A[s] if m == 0 else T)
                                for j in range(J):
                                    last = nc.tensor.transpose(pt[i % 2][0:feats, j * P:(j + 1) * P],
                                                               source[:, i * J + j, 0:feats], net.ident[:, :])
                                last.then_inc(turned, 1)

                            def project(i):
                                q = (k * MM + m) * SUBS + i
                                pe.wait_ge(zt_ready, q + 1)
                                pe.wait_ge(evacuated, q)
                                pe.sem_inc(pe_turn, 1)
                                lhs, w, b = zt[i % 2], weight, bias
                                if m == 1:
                                    nc.tensor.matmul(pf[i % 2][:, :], net.w1[:, :], zt[i % 2][:, :], start=True, stop=True).then_inc(up_done, 1)
                                    pe.wait_ge(gelu_done, k * SUBS + i + 1)
                                    lhs, w, b = u[i % 2], net.w2, net.b2
                                for j in range(J):
                                    nc.tensor.matmul(po[i % 2][:, j * C:(j + 1) * C], lhs[:, j * P:(j + 1) * P], w[:, :], start=True, stop=False)
                                    last = nc.tensor.matmul(po[i % 2][:, j * C:(j + 1) * C], net.ones[:, :], b[:, :], start=False, stop=True)
                                last.then_inc(mm_done, 1)
                            for i in range(SUBS):
                                turn(i)
                                project(i)

            @block.scalar
            def _(act):
                with act.Fori(0, SUPER // 2) as t:
                    for s in range(2):
                        k = 2 * t + s

                        def square(r):
                            act.wait_ge(centred, NORMS * k + r + 1)
                            nc.scalar.activation(SQ[:, :, :], XC[:, :, :], ACT.Square, scale=C ** -0.5).then_inc(squared, 1)
                            act.wait_ge(var_ready, NORMS * k + r + 1)
                            nc.scalar.activation(rstd[:, :], rstd[:, :], ACT.Sqrt, bias=net.eps[:, :]).then_inc(rstd_ready, 1)
                        if layer == 0:
                            act.wait_ge(deg_ready, k + 1)
                            nc.scalar.activation(H[s][:, :, C:C + 1], A[s][:, :, C:C + 1], ACT.Sqrt).then_inc(dinv_ready, 1)
                        for m in range(MM):
                            for i in range(SUBS):
                                q = (k * MM + m) * SUBS + i
                                act.wait_ge(turned, q + 1)
                                act.wait_ge(mm_done, q)
                                nc.scalar.activation(zt[i % 2][:, :], pt[i % 2][0:feats, :], ACT.Copy).then_inc(zt_ready, 1)
                                if m == 1:
                                    act.wait_ge(up_done, k * SUBS + i + 1)
                                    nc.scalar.activation(u[i % 2][:, :], pf[i % 2][:, :], ACT.Gelu, bias=net.b1[:, :]).then_inc(gelu_done, 1)
                            square(m)
                        if layer == 2:
                            square(2)
                        act.wait_ge(normed, k + 1)
                        nc.scalar.activation(H[s][:, :, 0:C], H[s][:, :, 0:C], ACT.Relu).then_inc(relu_done, 1)
                        act.wait_ge(relu_done, k + 1)
                        act.dma_start(rows_of(h_out, k, G), H[s][:, :, :]).then_inc(stored[s], 16)
                        if layer == 2:
                            act.wait_ge(tail_ready, k + 1)
                        act.dma_start(rows_of(x_out, k, G), X[s][:, :, :]).then_inc(stored[s], 16)
                for s in range(2):
                    act.wait_ge(stored[s], 32 * (SUPER // 2))

            @block.vector
            def _(v):
                def spread(x):
                    return x.unsqueeze(2).to_broadcast([P, G, C])

                def norm(x, y, k, r):
                    nc.vector.tensor_reduce(mean[:, :], x, AX.X, ALU.add)
                    v.drain()
                    nc.vector.tensor_scalar(mean[:, :], mean[:, :], 1.0 / C, None, ALU.mult)
                    v.drain()
                    nc.vector.tensor_tensor(XC[:, :, :], x, spread(mean[:, :]), ALU.subtract).then_inc(centred, 1)
                    v.wait_ge(squared, NORMS * k + r + 1)
                    nc.vector.tensor_reduce(rstd[:, :], SQ[:, :, :], AX.X, ALU.add).then_inc(var_ready, 1)
                    v.wait_ge(rstd_ready, NORMS * k + r + 1)
                    nc.vector.reciprocal(rstd[:, :], rstd[:, :])
                    v.drain()
                    return nc.vector.tensor_tensor(y, XC[:, :, :], spread(rstd[:, :]), ALU.mult)

                def affine(y, r):
                    v.drain()
                    nc.vector.tensor_tensor(y, y, net.norms[:, 2 * r, :].unsqueeze(1).to_broadcast([P, G, C]), ALU.mult)
                    v.drain()
                    return nc.vector.tensor_tensor(y, y, net.norms[:, 2 * r + 1, :].unsqueeze(1).to_broadcast([P, G, C]), ALU.add)

                with v.Fori(0, SUPER // 2) as t:
                    for s in range(2):
                        k = 2 * t + s
                        v.wait_ge(loaded[s], 48 * (t + 1))
                        if layer == 0:
                            nc.vector.tensor_scalar(A[s][:, :, C:C + 1], A[s][:, :, C:C + 1], 1.0, None, ALU.max).then_inc(deg_ready, 1)
                            v.drain()
                            nc.vector.reciprocal(rstd[:, :], A[s][:, :, C])
                            v.wait_ge(dinv_ready, k + 1)
                            nc.vector.reciprocal(H[s][:, :, C:C + 1], H[s][:, :, C:C + 1])
                            v.drain()
                            nc.vector.tensor_tensor(Z[s][:, :, C:P], A[s][:, :, 0:C], spread(rstd[:, :]), ALU.mult).then_inc(z_ready, 1)
                        elif layer == 1:
                            nc.vector.tensor_tensor(A[s][:, :, :], A[s][:, :, :], Z[s][:, :, C:C + 1].to_broadcast([P, G, C]), ALU.mult)
                            v.drain()
                            nc.vector.tensor_tensor(Z[s][:, :, 0:C], Z[s][:, :, 0:C], A[s][:, :, :], ALU.add).then_inc(z_ready, 1)
                        else:
                            v.sem_inc(z_ready, 1)
                        for m in range(MM):
                            for i in range(SUBS):
                                q = (k * MM + m) * SUBS + i
                                rows = slice(i * J, (i + 1) * J)
                                got = po[i % 2][:, 0:J * C].rearrange("p (j c) -> p j c", c=C)
                                v.wait_ge(mm_done, q + 1)
                                if layer == 0:
                                    nc.vector.scalar_tensor_tensor(X[s][:, rows, :], got, 0.0, X[s][:, rows, :], ALU.max, ALU.add).then_inc(evacuated, 1)
                                elif layer == 1:
                                    nc.vector.tensor_tensor(X[s][:, rows, :], got, X[s][:, rows, :], ALU.add).then_inc(evacuated, 1)
                                elif m == 0:
                                    nc.vector.tensor_tensor(T[:, rows, :], got, Z[s][:, rows, :], ALU.add).then_inc(evacuated, 1)
                                else:
                                    nc.vector.tensor_tensor(T[:, rows, :], got, T[:, rows, :], ALU.add).then_inc(evacuated, 1)
                            v.drain()
                            if layer == 2:
                                norm(T[:, :, :], T[:, :, :], k, m)
                                last = affine(T[:, :, :], m)
                                if m == 0:
                                    last.then_inc(t_ready, 1)
                        if layer == 2:
                            v.drain()
                            nc.vector.tensor_tensor(X[s][:, :, :], X[s][:, :, :], T[:, :, :], ALU.add)
                            nc.vector.memset(H[s][:, :, C:C + 1], 0.0)
                            v.drain()
                        norm(X[s][:, :, :], H[s][:, :, 0:C], k, NORMS - 1).then_inc(normed, 1)
                        if layer == 2:
                            v.wait_ge(relu_done, k + 1)
                            nc.vector.tensor_tensor(X[s][:, :, :], X[s][:, :, :], H[s][:, :, 0:C], ALU.add).then_inc(tail_ready, 1)


T_ALL = EP // P
BLOCK = 10
DIGITS = 256
LIST_SPARE = 1 + EP + J
LIST_ROWS = LIST_SPARE + SPARE


def sort_by_source(nc, net):
    with ExitStack() as ctx:
        ctx.callback(nc.all_engine_barrier)
        def sb(name, shape, dt=F32):
            return ctx.enter_context(nc.sbuf_tensor("s_" + name, shape, dt))

        def sem(name):
            return stage_semaphore(nc, ctx, "s_" + name)
        before_f = sb("before_f", [P, P])
        before = sb("before", [P, P], BF16)
        all_ones = sb("all_ones", [P, P], BF16)
        iota_f = sb("iota_f", [P, DIGITS])
        iota = sb("iota", [P, DIGITS], BF16)
        zero_row = sb("zero_row", [P, DIGITS], BF16)
        columns = [sb("col_src", [P, T_ALL], I32), sb("col_dst", [P, T_ALL], I32), sb("col_weight", [P, T_ALL])]
        rec = sb("rec", [P, T_ALL, 4], I32)
        part = sb("part", [P, T_ALL], I32)
        digit = sb("digit", [P, T_ALL])
        lane = sb("lane", [P, BLOCK])
        hots = [sb(f"hots{b}", [P, DIGITS], BF16) for b in range(4)]
        picked = sb("picked", [P, DIGITS])
        start_at = [sb(f"start_at{b}", [P, DIGITS]) for b in range(2)]
        rank = sb("rank", [P, BLOCK])
        ri = sb("ri", [P, BLOCK], I32)
        lo7 = sb("lo7", [P, BLOCK], I32)
        hi7 = sb("hi7", [P, BLOCK], I32)
        place = [sb(f"place{b}", [P, BLOCK], I32) for b in range(2)]
        recs = [sb(f"recs{b}", [P, BLOCK, 4], I32) for b in range(2)]
        none = sb("none", [1, 4], I32)
        blank = sb("blank", [P, 4 * T_ALL], I32)
        acc = [ctx.enter_context(nc.psum_tensor(f"s_acc{d}", [P, 512], F32)) for d in range(2)]
        within = ctx.enter_context(nc.psum_tensor("s_within", [P, 512], F32))
        names = ("loaded", "made", "hot", "freed", "counted", "ranked", "placed", "pool_turn", "reloaded", "filled", "summed", "based")
        (loaded, made, hot, freed, counted, ranked, placed, pool_turn, reloaded, filled, summed, based) = map(sem, names)
        scattered = [sem(f"scattered{b}") for b in range(2)]
        rounds = T_ALL // (2 * BLOCK)
        with nc.Block() as block:
            @block.sync
            def _(sp):
                sp.dma_start(before_f[:, :], net.dram["c_before"][:, :]).then_inc(loaded, 16)
                sp.dma_start(iota_f[:, :], net.dram["c_iota256"][:, :]).then_inc(loaded, 16)
                for tile, col in zip(columns, (net.src, net.dst_ext[1:1 + EP], net.dram["weight"])):
                    sp.dma_start(tile[:, :], col.rearrange("(p t) -> p t", p=P)).then_inc(loaded, 16)
                sp.wait_ge(made, 1)
                for n in range(2):
                    sp.dma_start(net.lists[n][0:1, :], none[:, :]).then_inc(filled, 16)
                    sp.dma_start(net.lists[n][1 + EP:1 + EP + J, :], blank[0:J, 0:4]).then_inc(filled, 16)
                sp.dma_start(net.lists[1][1:1 + EP, :].rearrange("(p t) c -> p (t c)", p=P), blank[:, :]).then_inc(filled, 16)
                for b in range(2):
                    sp.wait_ge(scattered[b], 16 * BLOCK * rounds)
                sp.dma_start(rec[:, :, :].rearrange("p t c -> p (t c)"),
                             net.half_sorted.rearrange("(p t) c -> p (t c)", p=P)).then_inc(reloaded, 16)
                sp.wait_ge(filled, 5 * 16)

            @block.vector
            def _(v):
                nc.vector.memset(none[:, :], -1)
                v.drain()
                nc.vector.memset(blank[:, :], 0).then_inc(made, 1)
                nc.vector.memset(all_ones[:, :], 1.0)
                nc.vector.memset(zero_row[:, :], 0.0)
                nc.vector.memset(rec[:, :, :], 0)
                v.wait_ge(loaded, 5 * 16)
                nc.vector.tensor_copy(before[:, :], before_f[:, :])
                nc.vector.tensor_copy(iota[:, :], iota_f[:, :])
                v.drain()
                for c in range(2):
                    nc.vector.tensor_copy(rec[:, :, c], columns[c][:, :])
                nc.vector.tensor_scalar(rec[:, :, 2], columns[2][:, :].bitcast(I32), 0, None, ALU.bitwise_or).then_inc(made, 1)
                v.drain()
                for d in range(2):
                    if d == 1:
                        v.wait_ge(reloaded, 16)
                    nc.vector.tensor_scalar(part[:, :], rec[:, :, 0], 255 if d == 0 else 8, None,
                                            ALU.bitwise_and if d == 0 else ALU.logical_shift_right)
                    v.drain()
                    nc.vector.tensor_copy(digit[:, :], part[:, :])
                    v.drain()
                    with v.Fori(0, rounds) as t:
                        for s in range(2):
                            nc.vector.tensor_copy(lane[:, :], digit[:, bass.ds(BLOCK * (2 * t + s), BLOCK)])
                            v.drain()
                            for q in range(BLOCK):
                                n = s * BLOCK + q
                                v.wait_ge(freed, T_ALL * d + 2 * BLOCK * t + n + 1)
                                nc.vector.tensor_scalar(hots[n % 4][:, :], iota[:, :], lane[:, q:q + 1], None, ALU.is_gt).then_inc(hot, 1)
                            v.drain()
                    v.wait_ge(freed, T_ALL * (d + 1) + 4)
                    with v.Fori(0, rounds) as t:
                        for s in range(2):
                            nc.vector.tensor_copy(lane[:, :], digit[:, bass.ds(BLOCK * (2 * t + s), BLOCK)])
                            v.drain()

                            def one_hot(q):
                                n = s * BLOCK + q
                                nc.vector.tensor_scalar(hots[n % 4][:, :], iota[:, :], lane[:, q:q + 1], None, ALU.is_equal).then_inc(hot, 1)
                            one_hot(0)
                            for q in range(BLOCK):
                                n = s * BLOCK + q
                                if q + 1 < BLOCK:
                                    one_hot(q + 1)
                                v.wait_ge(counted, T_ALL * d + 2 * BLOCK * t + n + 1)
                                nc.vector.tensor_tensor_reduce(out=picked[:, :], in0=within[:, 0:DIGITS], in1=hots[n % 4][:, :],
                                                               scale=1.0, scalar=0.0, op0=ALU.mult, op1=ALU.add,
                                                               accum_out=rank[:, q:q + 1]).then_inc(ranked, 1)
                            v.drain()
                            v.wait_ge(scattered[s], 16 * BLOCK * (rounds * d + t))
                            nc.vector.tensor_scalar(recs[s][:, :, :], rec[:, bass.ds(BLOCK * (2 * t + s), BLOCK), :], 0, None, ALU.bitwise_or)
                            if d == 0:
                                nc.vector.tensor_copy(ri[:, :], rank[:, :])
                                v.drain()
                                nc.vector.tensor_scalar(lo7[:, :], ri[:, :], P - 1, None, ALU.bitwise_and)
                                nc.vector.tensor_scalar(hi7[:, :], ri[:, :], 7, None, ALU.logical_shift_right)
                                v.drain()
                                nc.vector.scalar_tensor_tensor(place[s][:, :], lo7[:, :], float(T_ALL), hi7[:, :], ALU.mult, ALU.add).then_inc(placed, 1)
                            else:
                                nc.vector.tensor_scalar(place[s][:, :], rank[:, :], 1.0, None, ALU.add).then_inc(placed, 1)
                            v.drain()

            @block.tensor
            def _(pe):
                for _ in range(4):
                    pe.sem_inc(freed, 1)
                pe.wait_ge(made, 2)
                for d in range(2):
                    nc.tensor.matmul(acc[0][:, 0:DIGITS], all_ones[:, :], zero_row[:, :], start=True, stop=False)
                    with pe.Fori(0, rounds) as t:
                        for n in range(2 * BLOCK):
                            pe.wait_ge(hot, 2 * T_ALL * d + 2 * BLOCK * t + n + 1)
                            nc.tensor.matmul(acc[0][:, 0:DIGITS], all_ones[:, :], hots[n % 4][:, :], start=False, stop=False).then_inc(freed, 1)
                    nc.tensor.matmul(acc[0][:, 0:DIGITS], all_ones[:, :], zero_row[:, :], start=False, stop=True).then_inc(summed, 1)
                    with pe.Fori(0, rounds) as t:
                        for n in range(2 * BLOCK):
                            m = T_ALL * d + 2 * BLOCK * t + n
                            pe.wait_ge(hot, T_ALL * (2 * d + 1) + 2 * BLOCK * t + n + 1)
                            pe.wait_ge(based, m + d + 1)
                            nc.tensor.matmul(acc[n % 2][:, 0:DIGITS], net.ident[:, :], start_at[n % 2][:, :], start=True, stop=False)
                            nc.tensor.matmul(acc[n % 2][:, 0:DIGITS], all_ones[:, :], hots[n % 4][:, :], start=False, stop=True).then_inc(summed, 1)
                            pe.wait_ge(ranked, m)
                            nc.tensor.matmul(within[:, 0:DIGITS], net.ident[:, :], start_at[n % 2][:, :], start=True, stop=False)
                            nc.tensor.matmul(within[:, 0:DIGITS], before[:, :], hots[n % 4][:, :], start=False, stop=True).then_inc(counted, 1)

            @block.scalar
            def _(act):
                for d in range(2):
                    if d:
                        act.wait_ge(based, (T_ALL + 1) * d)
                    act.wait_ge(summed, (T_ALL + 1) * d + 1)
                    nc.scalar.activation(start_at[0][:, :], acc[0][:, 0:DIGITS], ACT.Copy).then_inc(based, 1)
                    with act.Fori(0, rounds) as t:
                        for n in range(2 * BLOCK):
                            m = T_ALL * d + 2 * BLOCK * t + n
                            act.wait_ge(summed, m + d + 2)
                            act.wait_ge(counted, m)
                            nc.scalar.activation(start_at[(n + 1) % 2][:, :], acc[n % 2][:, 0:DIGITS], ACT.Copy).then_inc(based, 1)

            @block.gpsimd
            def _(pool):
                for d in range(2):
                    table = (net.half_sorted, net.lists[0])[d]
                    with pool.Fori(0, rounds) as t:
                        for s in range(2):
                            pool.wait_ge(placed, 2 * rounds * d + 2 * t + s + 1)
                            pool.sem_inc(pool_turn, 1)
                            for q in range(BLOCK):
                                pool.indirect_dma_start(table[:, :], bass.IndirectOffsetOnAxis(ap=place[s][:, q:q + 1], axis=0),
                                                        recs[s][:, q, :], None).then_inc(scattered[s], 16)
                for s in range(2):
                    pool.wait_ge(scattered[s], 2 * 16 * BLOCK * rounds)


def diffuse(nc, net):
    W = C + 1
    with ExitStack() as ctx:
        ctx.callback(nc.all_engine_barrier)
        def sb(name, shape, dt=F32):
            return ctx.enter_context(nc.sbuf_tensor("d_" + name, shape, dt))

        def ps(name):
            return ctx.enter_context(nc.psum_tensor("d_" + name, [P, 512], F32))

        def sem(name):
            return stage_semaphore(nc, ctx, "d_" + name)
        before_f = sb("before_f", [P, P])
        before = sb("before", [P, P], BF16)
        all_ones = sb("all_ones", [P, P], BF16)
        ratios = sb("ratios", [P, STEPS])
        tcol = sb("tcol", [P, 1])
        pos0 = sb("pos0", [P, J + 2])
        node_spare = sb("node_spare", [P, J])
        list_spare = sb("list_spare", [P, J])
        step = sb("step", [P, 1])
        last_step = sb("last_step", [P, 1])
        next_step = sb("next_step", [P, 1])
        coef = sb("coef", [P, 1])
        base = sb("base", [P, 1])
        have = sb("have", [P, 1])
        passed = sb("passed", [P, 1])
        have_i = sb("have_i", [P, 1], I32)
        rec = sb("rec", [P, J + 2, 4], I32)
        inside = sb("inside", [P, J + 2])
        srcs = sb("srcs", [P, J + 2])
        keep = sb("keep", [P, J], BF16)
        is_end = sb("is_end", [P, J])
        end_f = sb("end_f", [P, J])
        end = sb("end", [P, J], I32)
        near = sb("near", [P, J, W])
        nonzero = sb("nonzero", [P, J, C])
        live = sb("live", [P, J])
        liveb = sb("liveb", [P, J], BF16)
        some = sb("some", [P, J])
        wl = sb("wl", [P, J])
        prod = sb("prod", [P, J, W])
        turned = sb("turned_sb", [W, CH])
        scan = sb("scan", [W, CH])
        carry = sb("carry", [W, 1])
        out = sb("out", [P, J, W])
        counts = sb("counts", [P, 2 * J])
        ahead = sb("ahead", [P, 2])
        upto = sb("upto", [P, J])
        place_f = sb("place_f", [P, J])
        place = sb("place", [P, J], I32)
        pt, pk, pr, pc = ps("pt"), ps("pk"), ps("pr"), ps("pc")
        names = ("loaded", "set_up", "counted_in", "rec_loaded", "gathered", "ready", "spread", "moved", "scanned", "back",
                 "out_ready", "placed", "stored", "passed_on", "stepped", "turn_pool", "turn_pe", "seen", "step_turn")
        (loaded, set_up, counted_in, rec_loaded, gathered, ready, spread, moved, scanned, back,
         out_ready, placed, stored, passed_on, stepped, turn_pool, turn_pe, seen, step_turn) = map(sem, names)

        def chunks_of(engine):
            n = engine.value_load(have_i[0:1, 0:1], min_val=0, max_val=EP)
            return engine.snap((n + (CH - 1)) >> 9, min_val=0, max_val=CHUNKS)

        def steps(engine, name, body):
            done = engine.alloc_register(f"done_{name}")
            engine.reg_mov(done, 0)
            with engine.Fori(0, STEPS // 2) as t:
                for parity in (1, 0):
                    engine.wait_ge(stepped, 2 * t + 2 - parity)
                    engine.sem_inc(step_turn, 1)
                    chunks = chunks_of(engine)
                    with engine.If(chunks > 0):
                        with engine.Fori(0, chunks) as c:
                            k = engine.snap(done, min_val=0, max_val=STEPS * CHUNKS)
                            body(parity, c, k)
                            engine.reg_add(done, done, 1)
                    engine.sem_inc(seen, 1)
            return done

        with nc.Block() as block:
            @block.sync
            def _(sp):
                for dst, src in ((before_f, "c_before"), (ratios, "c_ratios"), (pos0, "c_pos0"),
                                 (node_spare, "c_node_spare"), (list_spare, "c_list_spare")):
                    sp.dma_start(dst[:, :], net.dram[src][:, :]).then_inc(loaded, 16)
                sp.dma_start(tcol[:, :], net.dram["L3_gnn_t"][None, :].to_broadcast([P, 1])).then_inc(loaded, 16)

                def chunk(parity, c, k):
                    sp.wait_ge(passed_on, k * (16 * J))
                    rows = net.lists[1 - parity]
                    sp.dma_start(rec[:, 0:J, :], rows[bass.ds(c * CH, CH), :].rearrange("(p j) c -> p j c", j=J)).then_inc(rec_loaded, 16)
                    sp.dma_start(rec[:, J:J + 2, :], rows[bass.ds(c * CH + J, CH), :].rearrange("(p j) c -> p j c", j=J)[:, 0:2, :]).then_inc(rec_loaded, 16)
                steps(sp, "sp", chunk)

            @block.gpsimd
            def _(pool):
                def chunk(parity, c, k):
                    pool.wait_ge(rec_loaded, k * 32 + 32)
                    pool.sem_inc(turn_pool, 1)
                    for j in range(J):
                        pool.indirect_dma_start(near[:, j, :], None, net.term[1 - parity][:, :],
                                                bass.IndirectOffsetOnAxis(ap=rec[:, 1 + j, 1:2], axis=0)).then_inc(gathered, 16)
                    pool.wait_ge(placed, k + 1)
                    pool.sem_inc(turn_pool, 1)
                    for j in range(J):
                        pool.indirect_dma_start(net.lists[parity][:, :], bass.IndirectOffsetOnAxis(ap=place[:, j:j + 1], axis=0),
                                                rec[:, 1 + j, :], None).then_inc(passed_on, 16)
                    pool.wait_ge(out_ready, k + 1)
                    pool.sem_inc(turn_pool, 1)
                    for j in range(J):
                        pool.indirect_dma_start(net.term[parity][:, :], bass.IndirectOffsetOnAxis(ap=end[:, j:j + 1], axis=0),
                                                out[:, j, :], None).then_inc(stored, 16)
                        pool.indirect_dma_start(net.out[:, :], bass.IndirectOffsetOnAxis(ap=end[:, j:j + 1], axis=0),
                                                out[:, j, 0:C], None, compute_op=ALU.add).then_inc(stored, 16)
                    pool.wait_ge(stored, (k + 1) * (32 * J))
                    pool.wait_ge(passed_on, (k + 1) * (16 * J))
                    pool.sem_inc(turn_pool, 1)
                steps(pool, "pool", chunk)

            @block.tensor
            def _(pe):
                pe.wait_ge(set_up, 1)

                def chunk(parity, c, k):
                    pe.wait_ge(ready, k + 1)
                    pe.sem_inc(turn_pe, 1)
                    nc.tensor.matmul(pc[:, 0:J], before[:, :], liveb[:, :], start=True, stop=True)
                    nc.tensor.matmul(pc[:, J:2 * J], all_ones[:, :], liveb[:, :], start=True, stop=True)
                    for j in range(J):
                        nc.tensor.matmul(pk[0:W, j:CH:J], keep[:, j:j + 1].to_broadcast([P, W]), net.identb[:, :], start=True, stop=True)
                    for j in range(J):
                        last = nc.tensor.transpose(pt[0:W, j:CH:J], prod[:, j, :], net.ident[:, :])
                    last.then_inc(spread, 1)
                    pe.wait_ge(scanned, k + 1)
                    pe.sem_inc(turn_pe, 1)
                    for j in range(J):
                        last = nc.tensor.transpose(pr[:, j * W:(j + 1) * W], scan[:, j:CH:J], net.ident[0:W, 0:W])
                    last.then_inc(back, 1)
                steps(pe, "pe", chunk)

            @block.scalar
            def _(act):
                def chunk(parity, c, k):
                    act.wait_ge(spread, k + 1)
                    nc.scalar.activation(turned[:, :], pt[0:W, :], ACT.Copy).then_inc(moved, 1)
                steps(act, "act", chunk)

            @block.vector
            def _(v):
                v.wait_ge(loaded, 6 * 16)
                nc.vector.tensor_copy(before[:, :], before_f[:, :])
                nc.vector.memset(all_ones[:, :], 1.0)
                nc.vector.memset(carry[:, :], 0.0)
                nc.vector.tensor_scalar(tcol[:, :], tcol[:, :], 1e-8, -1.0 / N_SUB, ALU.max, ALU.mult)
                nc.vector.memset(last_step[:, :], 0.0)
                nc.vector.memset(step[:, :], 1.0)
                nc.vector.memset(next_step[:, :], 2.0)
                nc.vector.memset(base[:, :], 0.0)
                nc.vector.memset(passed[:, :], 0.0)
                nc.vector.memset(have[:, :], float(EDGES))
                nc.vector.memset(have_i[:, :], EDGES)
                v.drain()
                nc.vector.tensor_scalar(ratios[:, :], ratios[:, :], tcol[:, :], None, ALU.mult).then_inc(set_up, 1)
                v.drain()
                done = v.alloc_register("done_v")
                v.reg_mov(done, 0)
                with v.Fori(0, STEPS // 2) as t:
                    for parity in (1, 0):
                        nc.vector.tensor_copy(coef[:, :], ratios[:, bass.ds(2 * t + (1 - parity), 1)])
                        v.drain()
                        v.sem_inc(stepped, 1)
                        chunks = chunks_of(v)
                        with v.If(chunks > 0):
                            with v.Fori(0, chunks) as c:
                                k = v.snap(done, min_val=0, max_val=STEPS * CHUNKS)
                                v.wait_ge(rec_loaded, k * 32 + 32)
                                nc.vector.tensor_scalar(inside[:, :], pos0[:, :], base[:, :], have[:, :], ALU.add, ALU.is_lt)
                                v.drain()
                                nc.vector.scalar_tensor_tensor(srcs[:, :], rec[:, :, 0], 1.0, inside[:, :], ALU.add, ALU.mult)
                                v.drain()
                                nc.vector.tensor_tensor(keep[:, :], srcs[:, 1:J + 1], srcs[:, 0:J], ALU.is_equal)
                                nc.vector.tensor_tensor(is_end[:, :], srcs[:, 1:J + 1], srcs[:, 2:J + 2], ALU.not_equal)
                                nc.vector.tensor_scalar(end_f[:, :], srcs[:, 1:J + 1], -1.0, None, ALU.add)
                                v.drain()
                                nc.vector.tensor_tensor(end_f[:, :], end_f[:, :], node_spare[:, :], ALU.subtract)
                                nc.vector.tensor_tensor(is_end[:, :], is_end[:, :], inside[:, 1:J + 1], ALU.mult)
                                v.drain()
                                nc.vector.tensor_tensor(end_f[:, :], end_f[:, :], is_end[:, :], ALU.mult)
                                v.drain()
                                nc.vector.tensor_tensor(end[:, :], end_f[:, :], node_spare[:, :], ALU.add)
                                v.wait_ge(gathered, k * (16 * J) + 16 * J)
                                nc.vector.tensor_scalar(nonzero[:, :, :], near[:, :, 0:C], 0.0, None, ALU.not_equal)
                                nc.vector.tensor_scalar(live[:, :], near[:, :, C], last_step[:, :], None, ALU.is_equal)
                                v.drain()
                                nc.vector.tensor_reduce(some[:, :], nonzero[:, :, :], AX.X, ALU.max)
                                nc.vector.tensor_tensor(live[:, :], live[:, :], inside[:, 1:J + 1], ALU.mult)
                                v.drain()
                                nc.vector.tensor_tensor(live[:, :], live[:, :], some[:, :], ALU.mult)
                                v.drain()
                                nc.vector.tensor_copy(liveb[:, :], live[:, :])
                                nc.vector.scalar_tensor_tensor(wl[:, :], rec[:, 1:J + 1, 2].bitcast(F32), coef[:, :], live[:, :], ALU.mult, ALU.mult)
                                nc.vector.tensor_copy(prod[:, :, C], live[:, :])
                                v.drain()
                                nc.vector.tensor_tensor(prod[:, :, 0:C], near[:, :, 0:C], wl[:, :].unsqueeze(2).to_broadcast([P, J, C]),
                                                        ALU.mult).then_inc(ready, 1)
                                v.wait_ge(moved, k + 1)
                                nc.vector.tensor_tensor_scan(scan[:, :], pk[0:W, :], turned[:, :], carry[:, :], ALU.mult, ALU.add).then_inc(scanned, 1)
                                nc.vector.tensor_copy(counts[:, :], pc[:, 0:2 * J])
                                nc.vector.tensor_tensor_scan(upto[:, :], all_ones[:, 0:J], live[:, :], 0.0, ALU.mult, ALU.add)
                                v.drain()
                                nc.vector.tensor_copy(carry[:, :], scan[:, CH - 1:CH])
                                nc.vector.tensor_reduce(ahead[:, :], counts[:, :].rearrange("p (a j) -> p a j", a=2), AX.X, ALU.add)
                                nc.vector.tensor_tensor(upto[:, :], upto[:, :], live[:, :], ALU.subtract)
                                v.drain()
                                nc.vector.tensor_scalar(place_f[:, :], upto[:, :], ahead[:, 0:1], passed[:, :], ALU.add, ALU.add)
                                v.drain()
                                nc.vector.scalar_tensor_tensor(place_f[:, :], place_f[:, :], 1.0, list_spare[:, :], ALU.add, ALU.subtract)
                                nc.vector.tensor_tensor(passed[:, :], passed[:, :], ahead[:, 1:2], ALU.add)
                                nc.vector.tensor_scalar(base[:, :], base[:, :], float(CH), None, ALU.add)
                                v.drain()
                                nc.vector.tensor_tensor(place_f[:, :], place_f[:, :], live[:, :], ALU.mult)
                                v.drain()
                                nc.vector.tensor_tensor(place[:, :], place_f[:, :], list_spare[:, :], ALU.add).then_inc(placed, 1)
                                v.wait_ge(back, k + 1)
                                sums = pr[:, 0:J * W].rearrange("p (j c) -> p j c", c=W)
                                nc.vector.tensor_scalar(out[:, :, C], sums[:, :, C], 0.0, next_step[:, :], ALU.is_gt, ALU.mult)
                                nc.vector.tensor_copy(out[:, :, 0:C], sums[:, :, 0:C])
                                v.drain()
                                nc.vector.tensor_scalar(out[:, :, C], out[:, :, C], -1.0, None, ALU.add).then_inc(out_ready, 1)
                                v.wait_ge(stored, (k + 1) * (32 * J))
                                v.wait_ge(passed_on, (k + 1) * (16 * J))
                                v.reg_add(done, done, 1)
                        v.wait_ge(seen, 4 * (2 * t + (2 - parity)))
                        nc.vector.tensor_copy(have[:, :], passed[:, :])
                        nc.vector.tensor_copy(have_i[:, :], passed[:, :])
                        for x in (last_step, step, next_step):
                            nc.vector.tensor_scalar(x[:, :], x[:, :], 1.0, None, ALU.add)
                        nc.vector.memset(base[:, :], 0.0)
                        v.drain()
                        nc.vector.memset(passed[:, :], 0.0)
                        v.drain()


INPUTS = ["x", "src", "dst", "edge_type_8", "edge_weight", "L0_gnn_W_msg", "L0_gnn_b_msg", "L0_gnn_W_upd", "L0_gnn_b_upd",
          "L1_gnn_W", "L1_gnn_b", "L2_gnn_task_embedding", "L2_gnn_Wq", "L2_gnn_bq", "L2_gnn_Wk", "L2_gnn_bk", "L2_gnn_Wv",
          "L2_gnn_bv", "L2_gnn_ek_tab", "L2_gnn_ev_tab", "L2_gnn_es_tab", "L2_gnn_eg_tab", "L2_gnn_Wo", "L2_gnn_bo",
          "L2_gnn_ln1_g", "L2_gnn_ln1_b", "L2_gnn_W1", "L2_gnn_b1", "L2_gnn_W2", "L2_gnn_b2", "L2_gnn_ln2_g",
          "L2_gnn_ln2_b", "L2_gnn_Wf", "L2_gnn_bf", "L3_gnn_t"]


def host_layout(inputs):
    a = {k: np.ascontiguousarray(np.asarray(inputs[k])) for k in INPUTS}
    pad = EP - EDGES
    o = {k: v for k, v in a.items() if k not in ("x", "src", "dst", "edge_type_8", "edge_weight", "L1_gnn_W")}
    o["L1_gnn_WT"] = np.ascontiguousarray(a["L1_gnn_W"].T)
    o["x"] = np.concatenate([a["x"], np.zeros((NP - NODES, C), np.float32)])
    psrc = (NODES + np.arange(pad) % 128).astype(np.int32)
    pdst = np.full(pad, NP - 1, np.int32)
    o["src"] = np.concatenate([a["src"], psrc])
    one = np.full(1, -1, np.int32)
    o["dst_ext"] = np.concatenate([one, a["dst"], pdst, one, one, one])
    o["etype"] = np.concatenate([a["edge_type_8"], np.zeros(pad, np.int32)])
    o["weight"] = np.concatenate([a["edge_weight"], np.zeros(pad, np.float32)])
    o["c_before"] = np.triu(np.ones((P, P), np.float32), 1)
    o["c_iota256"] = np.broadcast_to(np.arange(DIGITS, dtype=np.float32), (P, DIGITS)).copy()
    o["c_ratios"] = np.broadcast_to(np.array(step_ratios(), np.float32), (P, STEPS)).copy()
    row = (np.arange(P)[:, None] * J + np.arange(J)[None, :]).astype(np.float32)
    o["c_pos0"] = (np.arange(P)[:, None] * J + np.arange(-1, J + 1)[None, :]).astype(np.float32)
    o["c_node_spare"] = row + np.float32(NP)
    o["c_list_spare"] = row + np.float32(LIST_SPARE)
    o["c_ident"] = np.eye(P, dtype=np.float32)
    o["c_ones"] = np.ones((1, P), np.float32)
    o["c_iota8"] = np.broadcast_to(np.arange(NET, dtype=np.float32), (P, J, NET)).copy()
    head = np.arange(C) // HD
    o["c_head_sum"] = np.where(head[:, None] == np.concatenate([head, np.arange(NH)])[None, :], HD ** -0.5, 0.0).astype(np.float32)
    return o


def program(nc, dram, out):
    net = Net()
    net.dram = dram
    net.x_in, net.src, net.dst_ext, net.etype, net.out = dram["x"], dram["src"], dram["dst_ext"], dram["etype"], out

    def table(name, rows, cols, dt=F32):
        return nc.dram_tensor(name, [rows, cols], dt, kind="Internal").ap()
    net.h0 = table("h0", NP, C)
    net.h1d = table("h1d", NP, C + 1)
    net.h2 = table("h2", NP, C)
    net.x1 = table("x1", NP, C)
    net.x2 = table("x2", NP, C)
    net.agg0 = table("agg0", NP, C + 1)
    net.agg1 = table("agg1", NP, C)
    net.agg2 = table("agg2", NP, C)
    net.term = [table(f"term{p}", NP + SPARE, C + 1) for p in range(2)]
    net.half_sorted = table("half_sorted", EP, 4, I32)
    net.lists = [table(f"list{p}", LIST_ROWS, 4, I32) for p in range(2)]
    with ExitStack() as ctx:
        allocate(nc, ctx, net)
        prepare(nc, net)
        sort_by_source(nc, net)
        first_norm(nc, net)
        for layer in range(3):
            edge_sums(nc, net, layer)
            node_update(nc, net, layer)
        diffuse(nc, net)


def kernel(**inputs):
    import concourse.bacc as bacc
    from concourse.bass_utils import run_bass_kernel_spmd
    nc = bacc.Bacc("TRN2", target_bir_lowering=False, num_devices=1)
    arrays = {f"in_{k}": v for k, v in host_layout(inputs).items()}
    dram = {k[3:]: nc.dram_tensor(k, v.shape, mybir.dt.from_np(v.dtype), kind="ExternalInput").ap() for k, v in arrays.items()}
    out = nc.dram_tensor("out", [NP + SPARE, C], F32, kind="ExternalOutput").ap()
    program(nc, dram, out)
    r = run_bass_kernel_spmd(nc, [arrays], core_ids=[0])
    return r.results[0]["out"][:NODES]
```

```python
import numpy as np
import concourse.bass as bass
from concourse import mybir
from contextlib import ExitStack

F32 = mybir.dt.float32
BF16 = mybir.dt.bfloat16
I32 = mybir.dt.int32
ALU = mybir.AluOpType
ACT = mybir.ActivationFunctionType
AX = mybir.AxisListType

P = 128
NODES, EDGES, C = 50000, 25000, 64
NH, HD, NET, FF = 4, 16, 8, 128
G = 28
J = 4
SUPER = -(-NODES // (P * G))
NP = SUPER * P * G
SUBS = G // J
CH = P * J
CHUNKS = 2 * -(-EDGES // (2 * CH))
EP = CHUNKS * CH
EPS = 1e-5
FAR = 1 << 17
NEG = -1e30
CV = C + NH
N_SUB, M_TERMS = 4, 20
STEPS = N_SUB * M_TERMS
SPARE = 2 * CH


def step_ratios():
    once = [1] * (M_TERMS + 1)
    for j in range(M_TERMS, 0, -1):
        once[j - 1] = once[j] * j
    poly = [1]
    for _ in range(N_SUB):
        new = [0] * (len(poly) + M_TERMS)
        for a, x in enumerate(poly):
            for b, y in enumerate(once):
                new[a + b] += x * y
        poly = new
    return [poly[k] / poly[k - 1] for k in range(1, len(poly))]


class Net:
    pass


def stage_semaphore(nc, ctx, name):
    s = nc.alloc_semaphore(name)
    ctx.callback(nc.clear_and_free_semaphores, [s])
    return s


def allocate(nc, ctx, net):
    def sb(name, shape, dt=F32):
        return ctx.enter_context(nc.sbuf_tensor(name, shape, dt))
    net.ident = sb("ident", [P, P])
    net.identb = sb("identb", [P, P], BF16)
    net.negidentb = sb("negidentb", [P, P], BF16)
    net.ones = sb("ones", [1, P])
    net.eps = sb("eps", [P, 1])
    net.iota8 = sb("iota8", [P, J, NET])
    net.w_msg = sb("w_msg", [P, C])
    net.b_msg = sb("b_msg", [C, 1])
    net.w_upd = sb("w_upd", [P, C])
    net.w_lin = sb("w_lin", [P, P])
    net.wq = sb("wq", [P, C])
    net.wk = sb("wk", [C, C])
    net.wv = sb("wv", [C, CV])
    net.tab_q = sb("tab_q", [NET, C])
    net.tab_k = sb("tab_k", [NET, C])
    net.tab_v = sb("tab_v", [NET, CV])
    net.tab_l = sb("tab_l", [NET, CV])
    net.head_sum = sb("head_sum", [C, CV])
    net.w_out = sb("w_out", [P, P])
    net.w1 = sb("w1", [P, FF])
    net.b1 = sb("b1", [FF, 1])
    net.w2 = sb("w2", [FF, C])
    net.norms = sb("norms", [P, 4, C])
    net.bias_parts = sb("bias_parts", [3, 4, J, C], BF16)
    net.ones3 = sb("ones3", [3, P], BF16)


def prepare(nc, net):
    d = net.dram
    with ExitStack() as ctx:
        ctx.callback(nc.all_engine_barrier)
        def sb(name, shape, dt=F32):
            return ctx.enter_context(nc.sbuf_tensor(name, shape, dt))

        def sem(name):
            return stage_semaphore(nc, ctx, name)
        zeros = sb("zeros", [P, G * (C + 1)])
        task = sb("task", [C, 1])
        wf = sb("wf", [C, 2 * C])
        bf_row = sb("bf_row", [1, 2 * C])
        bo_row = sb("bo_row", [1, C])
        wo = sb("wo", [P, C])
        g1 = sb("g1", [P, 1])
        a1 = sb("a1", [C, 1])
        a1_row = sb("a1_row", [1, C])
        rows = sb("rows", [1, 4, C])
        rest = sb("rest", [1, 4, C])
        parts = [sb(f"part{i}", [1, 4, C], BF16) for i in range(3)]
        repeated = [sb(f"repeated{i}", [1, 4, J, C], BF16) for i in range(3)]
        ek = sb("ek", [NET, C])
        bk = sb("bk", [NET, C])
        ev = sb("ev", [NET, C])
        bv = sb("bv", [NET, C])
        es = sb("es", [NET, NH])
        eg = sb("eg", [NET, NH])
        leg = sb("leg", [NET, NH])
        gb = sb("gb", [1, 2 * C])
        gate = sb("gate", [1, C])
        gated = sb("gated", [1, C])
        ps = ctx.enter_context(nc.psum_tensor("ps_gate", [P, 512], F32))
        ps2 = ctx.enter_context(nc.psum_tensor("ps_gate2", [P, 512], F32))
        ps3 = ctx.enter_context(nc.psum_tensor("ps_up_bias", [P, 512], F32))
        loaded = sem("weights_loaded")
        parts_ready = sem("parts_ready")
        parts_placed = sem("parts_placed")
        cleared = sem("tables_cleared")
        zero_ready = sem("zero_ready")
        corners_clear = sem("corners_clear")
        film_done = sem("film_done")
        up_bias_done = sem("up_bias_done")
        gb_ready = sem("gb_ready")
        tanh_done = sem("tanh_done")
        gate_ready = sem("gate_ready")
        spread_done = sem("spread_done")
        log_done = sem("log_done")
        with nc.Block() as block:
            loads = [
                (net.ident[:, :], d["c_ident"][:, :]), (net.ones[:, :], d["c_ones"][:, :]),
                (net.iota8[:, :, :], d["c_iota8"][:, :, :]), (net.head_sum[:, :], d["c_head_sum"][:, :]),
                (net.w_msg[:, :], d["L0_gnn_W_msg"][:, :]), (net.b_msg[:, :], d["L0_gnn_b_msg"][:, None]),
                (net.w_upd[:, :], d["L0_gnn_W_upd"][:, :]), (rows[:, 0, :], d["L0_gnn_b_upd"][None, :]),
                (net.w_lin[0:C, 0:C], d["L1_gnn_WT"][:, :]), (net.w_lin[C:P, C:P], d["L1_gnn_WT"][:, :]),
                (rows[:, 1, :], d["L1_gnn_b"][None, :]),
                (net.wq[C:, :], d["L2_gnn_Wq"][:, :]), (net.wk[:, :], d["L2_gnn_Wk"][:, :]),
                (net.wv[:, 0:C], d["L2_gnn_Wv"][:, :]),
                (net.tab_q[:, :], d["L2_gnn_bq"][None, :].to_broadcast([NET, C])),
                (bk[:, :], d["L2_gnn_bk"][None, :].to_broadcast([NET, C])),
                (bv[:, :], d["L2_gnn_bv"][None, :].to_broadcast([NET, C])),
                (ek[:, :], d["L2_gnn_ek_tab"][:, :]), (ev[:, :], d["L2_gnn_ev_tab"][:, :]),
                (es[:, :], d["L2_gnn_es_tab"][:, :]), (eg[:, :], d["L2_gnn_eg_tab"][:, :]),
                (task[:, :], d["L2_gnn_task_embedding"][:, None]), (wf[:, :], d["L2_gnn_Wf"][:, :]),
                (bf_row[:, :], d["L2_gnn_bf"][None, :]), (bo_row[:, :], d["L2_gnn_bo"][None, :]),
                (wo[0:C, :], d["L2_gnn_Wo"][:, :]), (wo[C:P, :], d["L2_gnn_Wo"][:, :]),
                (net.w1[0:C, :], d["L2_gnn_W1"][:, :]), (net.w1[C:P, :], d["L2_gnn_W1"][:, :]),
                (g1[0:C, :], d["L2_gnn_ln1_g"][:, None]), (g1[C:P, :], d["L2_gnn_ln1_g"][:, None]),
                (a1[:, :], d["L2_gnn_ln1_b"][:, None]), (a1_row[:, :], d["L2_gnn_ln1_b"][None, :]),
                (net.b1[:, :], d["L2_gnn_b1"][:, None]),
                (net.w2[:, :], d["L2_gnn_W2"][:, :]), (rows[:, 3, :], d["L2_gnn_b2"][None, :]),
                (net.norms[:, 0, :], d["L2_gnn_ln1_g"][None, :].to_broadcast([P, C])),
                (net.norms[:, 1, :], d["L2_gnn_ln1_b"][None, :].to_broadcast([P, C])),
                (net.norms[:, 2, :], d["L2_gnn_ln2_g"][None, :].to_broadcast([P, C])),
                (net.norms[:, 3, :], d["L2_gnn_ln2_b"][None, :].to_broadcast([P, C])),
            ]
            all_loaded = 16 * len(loads)

            @block.sync
            def _(sp):
                sp.wait_ge(corners_clear, 1)
                for dst, src in loads:
                    sp.dma_start(dst, src).then_inc(loaded, 16)
                sp.wait_ge(zero_ready, 1)
                for table in (net.agg0, net.agg1, net.agg2, net.term[1]):
                    wide = table.shape[1]
                    for i in range(SUPER):
                        rows = table[i * P * G:(i + 1) * P * G, :].rearrange("(p g) c -> p (g c)", p=P)
                        sp.dma_start(rows, zeros[:, 0:G * wide]).then_inc(cleared, 16)
                for table in (net.out, *net.term):
                    wide = table.shape[1]
                    rows = table[NP:NP + SPARE, :].rearrange("(p g) c -> p (g c)", p=P)
                    sp.dma_start(rows, zeros[:, 0:SPARE // P * wide]).then_inc(cleared, 16)
                sp.wait_ge(parts_ready, 1)
                for i in range(3):
                    sp.dma_start(net.bias_parts[i:i + 1, :, :, :], repeated[i][:, :, :, :]).then_inc(parts_placed, 16)
                sp.wait_ge(parts_placed, 3 * 16)
                sp.wait_ge(cleared, (4 * SUPER + 3) * 16)

            @block.tensor
            def _(pe):
                pe.wait_ge(loaded, all_loaded)
                nc.tensor.matmul(ps[0:1, 0:2 * C], task[:, :], wf[:, :], start=True, stop=True).then_inc(film_done, 1)
                nc.tensor.matmul(ps3[:, 0:1], net.w1[0:C, :], a1[:, :], start=True, stop=True).then_inc(up_bias_done, 1)
                pe.wait_ge(gate_ready, 1)
                nc.tensor.matmul(ps2[:, 0:C], net.ones[:, :], gate[:, :], start=True, stop=True).then_inc(spread_done, 1)

            @block.scalar
            def _(act):
                act.wait_ge(gb_ready, 1)
                nc.scalar.activation(gate[:, :], gb[:, 0:C], ACT.Tanh).then_inc(tanh_done, 1)
                act.wait_ge(loaded, all_loaded)
                nc.scalar.activation(leg[:, :], eg[:, :], ACT.Ln).then_inc(log_done, 1)

            @block.vector
            def _(v):
                nc.vector.memset(net.w_lin[:, :], 0.0)
                nc.vector.memset(net.w_out[:, :], 0.0)
                nc.vector.memset(net.ones3[:, :], 1.0)
                v.drain()
                v.sem_inc(corners_clear, 1)
                nc.vector.memset(zeros[:, :], 0.0).then_inc(zero_ready, 1)
                v.wait_ge(loaded, all_loaded)
                nc.vector.tensor_copy(net.identb[:, :], net.ident[:, :])
                nc.vector.tensor_scalar(net.negidentb[:, :], net.ident[:, :], NEG, None, ALU.mult)
                nc.vector.memset(net.wv[:, C:CV], 0.0)
                nc.vector.memset(net.eps[:, :], EPS)
                nc.vector.memset(net.tab_v[:, C:CV], 1.0)
                nc.vector.tensor_tensor(net.tab_k[:, :], ek[:, :], bk[:, :], ALU.add)
                nc.vector.tensor_tensor(net.tab_v[:, 0:C], ev[:, :], bv[:, :], ALU.add)
                v.wait_ge(film_done, 1)
                nc.vector.tensor_tensor(gb[:, :], ps[0:1, 0:2 * C], bf_row[:, :], ALU.add).then_inc(gb_ready, 1)
                v.wait_ge(tanh_done, 1)
                nc.vector.tensor_scalar(gate[:, :], gate[:, :], 0.5, 1.0, ALU.mult, ALU.add).then_inc(gate_ready, 1)
                v.drain()
                nc.vector.tensor_tensor(gated[:, :], bo_row[:, :], gate[:, :], ALU.mult)
                v.drain()
                nc.vector.tensor_tensor(rows[:, 2, :], gated[:, :], gb[:, C:2 * C], ALU.add)
                nc.vector.tensor_tensor(rows[:, 3, :], rows[:, 3, :], a1_row[:, :], ALU.add)
                v.wait_ge(up_bias_done, 1)
                nc.vector.tensor_tensor(net.b1[:, :], net.b1[:, :], ps3[:, 0:1], ALU.add)
                nc.vector.tensor_scalar(net.w1[:, :], net.w1[:, :], g1[:, :], None, ALU.mult)
                v.wait_ge(spread_done, 1)
                for half in (slice(0, C), slice(C, P)):
                    nc.vector.tensor_tensor(net.w_out[half, half], wo[half, :], ps2[half, 0:C], ALU.mult)
                left = rows
                for i in range(3):
                    v.drain()
                    nc.vector.tensor_copy(parts[i][:, :, :], left[:, :, :])
                    v.drain()
                    nc.vector.tensor_copy(repeated[i][:, :, :, :], parts[i][:, :, :].unsqueeze(2).to_broadcast([1, 4, J, C]))
                    nc.vector.tensor_tensor(rest[:, :, :], left[:, :, :], parts[i][:, :, :], ALU.subtract)
                    left = rest
                v.drain()
                v.sem_inc(parts_ready, 1)
                v.wait_ge(log_done, 1)
                nc.vector.tensor_scalar(leg[:, :], leg[:, :], -10.0, 10.0, ALU.max, ALU.min)
                v.drain()
                nc.vector.tensor_tensor(es[:, :], es[:, :], leg[:, :], ALU.add)
                v.drain()
                nc.vector.tensor_copy(net.tab_l[:, 0:C].rearrange("e (h d) -> e h d", d=HD),
                                      es[:, :].unsqueeze(2).to_broadcast([NET, NH, HD]))
                nc.vector.tensor_copy(net.tab_l[:, C:CV], es[:, :])


def rows_of(table, chunk, rows, lo=0, hi=None):
    return table[bass.ds(chunk * (P * rows), P * rows), :].rearrange("(p g) c -> p g c", p=P)


def first_norm(nc, net):
    with ExitStack() as ctx:
        ctx.callback(nc.all_engine_barrier)
        def sb(name, shape, dt=F32):
            return ctx.enter_context(nc.sbuf_tensor(name, shape, dt))

        def sem(name):
            return stage_semaphore(nc, ctx, name)
        X = [sb(f"n_x{s}", [P, G, C]) for s in range(2)]
        XC = [sb(f"n_xc{s}", [P, G, C]) for s in range(2)]
        SQ = [sb(f"n_sq{s}", [P, G, C]) for s in range(2)]
        H = [sb(f"n_h{s}", [P, G, C]) for s in range(2)]
        mean = [sb(f"n_mean{s}", [P, G]) for s in range(2)]
        rstd = [sb(f"n_rstd{s}", [P, G]) for s in range(2)]
        loaded = [sem(f"n_loaded{s}") for s in range(2)]
        stored = [sem(f"n_stored{s}") for s in range(2)]
        centred, squared, var_ready, rstd_ready, normed = (
            sem(f"n_{x}") for x in ("centred", "squared", "var_ready", "rstd_ready", "normed"))
        with nc.Block() as block:
            @block.sync
            def _(sp):
                for s in range(2):
                    sp.dma_start(X[s][:, :, :], rows_of(net.x_in, s, G)).then_inc(loaded[s], 16)
                with sp.Fori(1, SUPER // 2) as t:
                    for s in range(2):
                        sp.wait_ge(centred, 2 * t + s - 1)
                        sp.dma_start(X[s][:, :, :], rows_of(net.x_in, 2 * t + s, G)).then_inc(loaded[s], 16)

            @block.vector
            def _(v):
                with v.Fori(0, SUPER // 2) as t:
                    for s in range(2):
                        v.wait_ge(loaded[s], 16 * t + 16)
                        nc.vector.tensor_reduce(mean[s][:, :], X[s][:, :, :], AX.X, ALU.add)
                        v.drain()
                        nc.vector.tensor_scalar(mean[s][:, :], mean[s][:, :], 1.0 / C, None, ALU.mult)
                        v.drain()
                        nc.vector.tensor_tensor(XC[s][:, :, :], X[s][:, :, :],
                                                mean[s][:, :].unsqueeze(2).to_broadcast([P, G, C]),
                                                ALU.subtract).then_inc(centred, 1)
                    for s in range(2):
                        v.wait_ge(squared, 2 * t + s + 1)
                        nc.vector.tensor_reduce(rstd[s][:, :], SQ[s][:, :, :], AX.X, ALU.add).then_inc(var_ready, 1)
                    for s in range(2):
                        v.wait_ge(rstd_ready, 2 * t + s + 1)
                        nc.vector.reciprocal(rstd[s][:, :], rstd[s][:, :])
                        v.drain()
                        v.wait_ge(stored[s], 16 * t)
                        nc.vector.scalar_tensor_tensor(H[s][:, :, :], XC[s][:, :, :], 0.0,
                                                       rstd[s][:, :].unsqueeze(2).to_broadcast([P, G, C]),
                                                       ALU.max, ALU.mult).then_inc(normed, 1)

            @block.scalar
            def _(act):
                with act.Fori(0, SUPER // 2) as t:
                    for s in range(2):
                        act.wait_ge(centred, 2 * t + s + 1)
                        nc.scalar.activation(SQ[s][:, :, :], XC[s][:, :, :], ACT.Square, scale=C ** -0.5).then_inc(squared, 1)
                    for s in range(2):
                        act.wait_ge(var_ready, 2 * t + s + 1)
                        nc.scalar.activation(rstd[s][:, :], rstd[s][:, :], ACT.Sqrt, bias=net.eps[:, :]).then_inc(rstd_ready, 1)
                    for s in range(2):
                        act.wait_ge(normed, 2 * t + s + 1)
                        act.dma_start(rows_of(net.h0, 2 * t + s, G), H[s][:, :, :]).then_inc(stored[s], 16)
                for s in range(2):
                    act.wait_ge(stored[s], 16 * (SUPER // 2))


def edge_sums(nc, net, layer):
    two = layer != 1
    table = (net.h0, net.h1d, net.h2)[layer]
    agg = (net.agg0, net.agg1, net.agg2)[layer]
    wide = C + 1 if layer == 1 else C
    rows = (C + 1, C, CV)[layer]
    outw = (C + 1, C, C)[layer]
    n_gather = 8 if two else 4
    n = f"e{layer}_"
    with ExitStack() as ctx:
        ctx.callback(nc.all_engine_barrier)
        def sb(name, shape, dt=F32):
            return ctx.enter_context(nc.sbuf_tensor(n + name, shape, dt))

        def ps(name):
            return ctx.enter_context(nc.psum_tensor(n + name, [P, 512], F32))

        def sem(name):
            return stage_semaphore(nc, ctx, n + name)
        src = [sb(f"src{s}", [P, J], I32) for s in range(2)]
        dst = [sb(f"dst{s}", [P, J + 2], I32) for s in range(2)]
        etype = [sb(f"etype{s}", [P, J], I32) for s in range(2)]
        keep = [sb(f"keep{s}", [P, J], BF16) for s in range(2)]
        fresh = [sb(f"fresh{s}", [P, J], BF16) for s in range(2)]
        same = [sb(f"same{s}", [P, J]) for s in range(2)]
        end = [sb(f"end{s}", [P, J], I32) for s in range(2)]
        ends = [sb(f"ends{s}", [P, J, 2 * wide if two else wide]) for s in range(2)]
        out = [sb(f"out{s}", [P, J, outw]) for s in range(2)]
        scan = [sb(f"scan{s}", [rows, CH]) for s in range(2)]
        feat = sb("feat", [P if two else C, CH])
        msg = sb("msg", [rows, CH])
        y = sb("y", [P, J, C])
        pt = ps("pt")
        pk = ps("pk")
        pm = ps("pm")
        pr = ps("pr")
        loaded = [sem(f"loaded{s}") for s in range(2)]
        gathered = [sem(f"gathered{s}") for s in range(2)]
        scattered = [sem(f"scattered{s}") for s in range(2)]
        names = ("flags", "y_ready", "turned", "kept", "feat_ready", "msg_mm", "msg_ready", "scanned", "back", "out_ready",
                 "pool_turn", "pe_turn")
        (flags, y_ready, turned, kept, feat_ready, msg_mm, msg_ready, scanned, back, out_ready, pool_turn,
         pe_turn) = map(sem, names)
        if layer == 2:
            onehot = sb("onehot", [P, J, NET])
            oht = sb("oht", [NET, CH])
            qs = sb("qs", [C, CH])
            prod = sb("prod", [C, CH])
            mx = [sb(f"mx{s}", [CV, CH + 1]) for s in range(2)]
            lm = sb("lm", [CV, CH])
            dm = sb("dm", [CV, CH])
            pexp = sb("pexp", [CV, CH])
            rexp = sb("rexp", [CV, CH])
            negs = sb("negs", [CV, CH])
            dsum = sb("dsum", [P, J, NH])
            pq, pkk, pl, pg = ps("pq"), ps("pkk"), ps("pl"), ps("pg")
            (onehot_ready, oht_mm, oht_ready, q_ready, prod_ready, logits, lm_ready, p_ready, dm_ready, r_ready,
             q_copied) = map(sem, (
                 "onehot_ready", "oht_mm", "oht_ready", "q_ready", "prod_ready", "logits", "lm_ready", "p_ready", "dm_ready",
                 "r_ready", "q_copied"))

        edge_src = net.src.rearrange("(n p j) -> n p j", p=P, j=J)
        edge_typ = net.etype.rearrange("(n p j) -> n p j", p=P, j=J)

        def dst_rows(c):
            first = net.dst_ext[bass.ds(c * CH, CH)].rearrange("(p j) -> p j", j=J)
            last = net.dst_ext[bass.ds(c * CH + J, CH)].rearrange("(p j) -> p j", j=J)
            return first, last[:, 0:2]

        n_loads = 4 if layer == 2 else 3
        with nc.Block() as block:
            @block.sync
            def _(sp):
                def load(c, s):
                    first, last = dst_rows(c)
                    sp.dma_start(src[s][:, :], edge_src[c, :, :] if isinstance(c, int) else edge_src[bass.ds(c, 1), :, :].rearrange("o p j -> (o p) j")).then_inc(loaded[s], 16)
                    sp.dma_start(dst[s][:, 0:J], first).then_inc(loaded[s], 16)
                    sp.dma_start(dst[s][:, J:J + 2], last).then_inc(loaded[s], 16)
                    if layer == 2:
                        sp.dma_start(etype[s][:, :], edge_typ[c, :, :] if isinstance(c, int) else edge_typ[bass.ds(c, 1), :, :].rearrange("o p j -> (o p) j")).then_inc(loaded[s], 16)
                for s in range(2):
                    load(s, s)
                with sp.Fori(1, CHUNKS // 2) as t:
                    for s in range(2):
                        sp.wait_ge(gathered[s], 16 * n_gather * t)
                        sp.wait_ge(flags, 2 * t + s - 1)
                        if layer == 2:
                            sp.wait_ge(onehot_ready, 2 * t + s - 1)
                        load(2 * t + s, s)

            @block.gpsimd
            def _(pool):
                def gather(t, s):
                    pool.wait_ge(loaded[s], 16 * n_loads * (t + 1))
                    pool.wait_ge(turned if two else y_ready, 2 * t + s + 1)
                    pool.sem_inc(pool_turn, 1)
                    for j in range(J):
                        pool.indirect_dma_start(ends[s][:, j, 0:wide], None, table[:, :],
                                                bass.IndirectOffsetOnAxis(ap=src[s][:, j:j + 1], axis=0)).then_inc(gathered[s], 16)
                        if two:
                            pool.indirect_dma_start(ends[s][:, j, wide:2 * wide], None, table[:, :],
                                                    bass.IndirectOffsetOnAxis(ap=dst[s][:, 1 + j:2 + j], axis=0)).then_inc(gathered[s], 16)

                def scatter(t, s):
                    pool.wait_ge(out_ready, 2 * t + s + 1)
                    pool.sem_inc(pool_turn, 1)
                    for j in range(J):
                        pool.indirect_dma_start(agg[:, :], bass.IndirectOffsetOnAxis(ap=end[s][:, j:j + 1], axis=0),
                                                out[s][:, j, :], None, bounds_check=NP - 1, oob_is_err=False).then_inc(scattered[s], 16)
                gather(0, 0)
                with pool.Fori(0, CHUNKS // 2 - 1) as t:
                    gather(t, 1)
                    scatter(t, 0)
                    gather(t + 1, 0)
                    scatter(t, 1)
                last = CHUNKS // 2 - 1
                gather(last, 1)
                scatter(last, 0)
                scatter(last, 1)
                for s in range(2):
                    pool.wait_ge(scattered[s], 16 * J * (CHUNKS // 2))

            @block.vector
            def _(v):
                nc.vector.memset(scan[1][:, :], 0.0)
                if layer == 0:
                    nc.vector.memset(msg[C:C + 1, :], 1.0)
                if layer == 2:
                    nc.vector.memset(mx[1][:, :], 0.0)
                if layer == 1:
                    for _ in range(2):
                        v.sem_inc(y_ready, 1)
                v.drain()

                def make_flags(t, s):
                    v.wait_ge(loaded[s], 16 * n_loads * (t + 1))
                    v.wait_ge(scattered[s], 16 * J * t)
                    nc.vector.tensor_tensor(keep[s][:, :], dst[s][:, 1:J + 1], dst[s][:, 0:J], ALU.is_equal)
                    if layer == 2:
                        nc.vector.tensor_tensor(fresh[s][:, :], dst[s][:, 1:J + 1], dst[s][:, 0:J], ALU.not_equal)
                    nc.vector.tensor_tensor(same[s][:, :], dst[s][:, 1:J + 1], dst[s][:, 2:J + 2], ALU.is_equal)
                    v.drain()
                    nc.vector.scalar_tensor_tensor(end[s][:, :], same[s][:, :], float(FAR), dst[s][:, 1:J + 1],
                                                   ALU.mult, ALU.add).then_inc(flags, 1)

                def sums(t, s):
                    k = 2 * t + s + 1
                    if layer == 1:
                        v.wait_ge(gathered[s], 16 * n_gather * (t + 1))
                        v.wait_ge(turned, k - 1)
                        nc.vector.tensor_tensor(y[:, :, :], ends[s][:, :, 0:C],
                                                ends[s][:, :, C:C + 1].to_broadcast([P, J, C]), ALU.mult).then_inc(y_ready, 1)
                    if layer == 2:
                        v.wait_ge(oht_mm, k - 1)
                        nc.vector.tensor_tensor(onehot[:, :, :], etype[s][:, :].unsqueeze(2).to_broadcast([P, J, NET]),
                                                net.iota8[:, :, :], ALU.is_equal).then_inc(onehot_ready, 1)
                        v.wait_ge(q_copied, k)
                        v.wait_ge(q_ready, k)
                        nc.vector.tensor_tensor(prod[:, :], qs[:, :], pkk[0:C, :], ALU.mult).then_inc(prod_ready, 1)
                        v.wait_ge(kept, k)
                        nc.vector.tensor_copy(negs[:, :], pg[0:CV, :])
                        nc.vector.tensor_copy(mx[s][:, 0:1], mx[1 - s][:, CH:CH + 1])
                        v.drain()
                        v.wait_ge(logits, k)
                        nc.vector.tensor_tensor_scan(mx[s][:, 1:CH + 1], negs[:, :], pl[0:CV, :], mx[1 - s][:, CH:CH + 1],
                                                     ALU.add, ALU.max)
                        v.drain()
                        nc.vector.tensor_tensor(lm[:, :], pl[0:CV, :], mx[s][:, 1:CH + 1], ALU.subtract).then_inc(lm_ready, 1)
                        nc.vector.tensor_tensor(dm[:, :], negs[:, :], mx[s][:, 0:CH], ALU.add)
                        v.drain()
                        nc.vector.tensor_tensor(dm[:, :], dm[:, :], mx[s][:, 1:CH + 1], ALU.subtract).then_inc(dm_ready, 1)
                        v.wait_ge(p_ready, k)
                        nc.vector.tensor_tensor(msg[:, :], pexp[:, :], pm[0:CV, :], ALU.mult)
                        v.drain()
                        v.wait_ge(r_ready, k)
                        v.wait_ge(back, k - 1)
                        nc.vector.tensor_tensor_scan(scan[s][:, :], rexp[:, :], msg[:, :], scan[1 - s][:, CH - 1:CH],
                                                     ALU.mult, ALU.add).then_inc(scanned, 1)
                    else:
                        v.wait_ge(msg_ready, k)
                        v.wait_ge(kept, k)
                        nc.vector.tensor_tensor_scan(scan[s][:, :], pk[0:rows, :], msg[:, :], scan[1 - s][:, CH - 1:CH],
                                                     ALU.mult, ALU.add).then_inc(scanned, 1)
                    v.wait_ge(back, k)
                    sums_rows = pr[:, 0:J * rows].rearrange("p (j c) -> p j c", c=rows)
                    if layer == 2:
                        nc.vector.tensor_scalar(dsum[:, :, :], sums_rows[:, :, C:CV], 1e-12, None, ALU.max)
                        v.drain()
                        nc.vector.reciprocal(dsum[:, :, :], dsum[:, :, :])
                        v.drain()
                        for j in range(J):
                            last = nc.vector.tensor_tensor(
                                out[s][:, j, :].rearrange("p (h d) -> p h d", d=HD),
                                sums_rows[:, j, 0:C].rearrange("p (h d) -> p h d", d=HD),
                                dsum[:, j, :].unsqueeze(2).to_broadcast([P, NH, HD]), ALU.mult)
                        last.then_inc(out_ready, 1)
                    else:
                        nc.vector.tensor_copy(out[s][:, :, :], sums_rows).then_inc(out_ready, 1)

                with v.Fori(0, CHUNKS // 2) as t:
                    for s in range(2):
                        make_flags(t, s)
                        sums(t, s)

            @block.tensor
            def _(pe):
                if two:
                    for _ in range(2):
                        pe.sem_inc(turned, 1)
                with pe.Fori(0, CHUNKS // 2) as t:
                    for s in range(2):
                        k = 2 * t + s + 1
                        if two:
                            pe.wait_ge(gathered[s], 16 * n_gather * (t + 1))
                            pe.wait_ge(feat_ready, k - 1)
                            pe.sem_inc(pe_turn, 1)
                            for j in range(J):
                                last = nc.tensor.transpose(pt[:, j:CH:J], ends[s][:, j, :], net.ident[:, :])
                        else:
                            pe.wait_ge(y_ready, k + 2)
                            pe.wait_ge(feat_ready, k - 1)
                            pe.sem_inc(pe_turn, 1)
                            for j in range(J):
                                last = nc.tensor.transpose(pt[0:C, j:CH:J], y[:, j, :], net.ident[:, :])
                        last.then_inc(turned, 1)
                        pe.wait_ge(flags, k)
                        pe.wait_ge(scanned, k - 1)
                        if layer == 2:
                            for j in range(J):
                                last = nc.tensor.matmul(pg[0:CV, j:CH:J], fresh[s][:, j:j + 1].to_broadcast([P, CV]),
                                                        net.negidentb[:, :], start=True, stop=True)
                            last.then_inc(kept, 1)
                            pe.wait_ge(onehot_ready, k)
                            pe.sem_inc(pe_turn, 1)
                            for j in range(J):
                                last = nc.tensor.transpose(pk[0:NET, j:CH:J], onehot[:, j, :], net.ident[:, :])
                            last.then_inc(oht_mm, 1)
                            pe.wait_ge(oht_ready, k)
                            pe.wait_ge(feat_ready, k)
                            pe.sem_inc(pe_turn, 1)
                            nc.tensor.matmul(pq[0:C, :], net.wq[C:P, :], feat[C:P, :], start=True, stop=False)
                            nc.tensor.matmul(pq[0:C, :], net.tab_q[:, :], oht[:, :], start=False, stop=True)
                            nc.tensor.matmul(pkk[0:C, :], net.wk[:, :], feat[0:C, :], start=True, stop=False)
                            nc.tensor.matmul(pkk[0:C, :], net.tab_k[:, :], oht[:, :], start=False, stop=True).then_inc(q_ready, 1)
                            nc.tensor.matmul(pm[0:CV, :], net.wv[:, :], feat[0:C, :], start=True, stop=False)
                            nc.tensor.matmul(pm[0:CV, :], net.tab_v[:, :], oht[:, :], start=False, stop=True)
                            pe.wait_ge(prod_ready, k)
                            nc.tensor.matmul(pl[0:CV, :], net.head_sum[:, :], prod[:, :], start=True, stop=False)
                            nc.tensor.matmul(pl[0:CV, :], net.tab_l[:, :], oht[:, :], start=False, stop=True).then_inc(logits, 1)
                        else:
                            for j in range(J):
                                last = nc.tensor.matmul(pk[0:rows, j:CH:J], keep[s][:, j:j + 1].to_broadcast([P, rows]),
                                                        net.identb[:, :], start=True, stop=True)
                            last.then_inc(kept, 1)
                            if layer == 0:
                                pe.wait_ge(feat_ready, k)
                                nc.tensor.matmul(pm[0:C, :], net.w_msg[:, :], feat[:, :], start=True, stop=True).then_inc(msg_mm, 1)
                        pe.wait_ge(scanned, k)
                        pe.wait_ge(out_ready, k - 1)
                        pe.sem_inc(pe_turn, 1)
                        for j in range(J):
                            last = nc.tensor.transpose(pr[:, j * rows:(j + 1) * rows], scan[s][:, j:CH:J], net.ident[0:rows, 0:rows])
                        last.then_inc(back, 1)

            @block.scalar
            def _(act):
                with act.Fori(0, CHUNKS // 2) as t:
                    for s in range(2):
                        k = 2 * t + s + 1
                        if layer == 0:
                            act.wait_ge(turned, k + 2)
                            nc.scalar.activation(feat[:, :], pt[:, :], ACT.Copy).then_inc(feat_ready, 1)
                            act.wait_ge(msg_mm, k)
                            act.wait_ge(scanned, k - 1)
                            nc.scalar.activation(msg[0:C, :], pm[0:C, :], ACT.Relu, bias=net.b_msg[:, :]).then_inc(msg_ready, 1)
                        elif layer == 1:
                            act.wait_ge(turned, k)
                            act.wait_ge(scanned, k - 1)
                            nc.scalar.activation(msg[:, :], pt[0:C, :], ACT.Copy)
                            act.drain()
                            act.sem_inc(feat_ready, 1)
                            act.sem_inc(msg_ready, 1)
                        else:
                            act.wait_ge(turned, k + 2)
                            nc.scalar.activation(feat[:, :], pt[:, :], ACT.Copy).then_inc(feat_ready, 1)
                            act.wait_ge(oht_mm, k)
                            act.wait_ge(logits, k - 1)
                            nc.scalar.activation(oht[:, :], pk[0:NET, :], ACT.Copy).then_inc(oht_ready, 1)
                            act.wait_ge(q_ready, k)
                            nc.scalar.activation(qs[:, :], pq[0:C, :], ACT.Copy).then_inc(q_copied, 1)
                            act.wait_ge(lm_ready, k)
                            nc.scalar.activation(pexp[:, :], lm[:, :], ACT.Exp).then_inc(p_ready, 1)
                            act.wait_ge(dm_ready, k)
                            nc.scalar.activation(rexp[:, :], dm[:, :], ACT.Exp).then_inc(r_ready, 1)


def node_update(nc, net, layer):
    n = f"u{layer}_"
    TURNS = J if layer == 0 else J // 2
    aggw = C + 1 if layer == 0 else C
    hw = C + 1 if layer == 1 else C
    with ExitStack() as ctx:
        ctx.callback(nc.all_engine_barrier)
        def sb(name, shape, dt=F32):
            return ctx.enter_context(nc.sbuf_tensor(n + name, shape, dt))

        def ps(name):
            return ctx.enter_context(nc.psum_tensor(n + name, [P, 512], F32))

        def sem(name):
            return stage_semaphore(nc, ctx, n + name)
        X = [sb(f"x{s}", [P, G, C]) for s in range(2)]
        A = [sb(f"a{s}", [P, G, aggw]) for s in range(2)]
        Z = [sb(f"z{s}", [P, G, P if layer == 0 else hw]) for s in range(2)]
        T = [sb(f"t{s}", [P, G, C]) for s in range(2)]
        H = [sb(f"h{s}", [P, G, C if layer == 1 else C + 1]) for s in range(2)]
        chains = 2 if layer == 2 else 1
        XC = [sb(f"xc{n}", [P, G, C]) for n in range(chains)]
        SQ = [sb(f"sq{n}", [P, G, C]) for n in range(chains)]
        mean = [sb(f"mean{n}", [P, G]) for n in range(chains)]
        rstd = [sb(f"rstd{n}", [P, G]) for n in range(chains)]
        centred, squared, var_ready, rstd_ready = (
            [sem(f"{x}{n}") for n in range(chains)] for x in ("centred", "squared", "var_ready", "rstd_ready"))
        zt = [sb(f"zt{b}", [P, TURNS * P]) for b in range(2)]
        pt = [ps(f"pt{b}") for b in range(2)]
        po = [ps(f"po{b}") for b in range(2)]
        loaded = [sem(f"loaded{s}") for s in range(2)]
        stored_x = [sem(f"stored_x{s}") for s in range(2)]
        stored_h = [sem(f"stored_h{s}") for s in range(2)]
        names = ("z_ready", "turned", "zt_ready", "mm_done", "evacuated", "inputs_used", "normed", "pe_turn")
        (z_ready, turned, zt_ready, mm_done, evacuated, inputs_used, normed, pe_turn) = map(sem, names)
        if layer == 0:
            inv_count = [sb(f"inv_count{s}", [P, G]) for s in range(2)]
            dinv = [sb(f"dinv{s}", [P, G]) for s in range(2)]
            deg_ready, dinv_ready = map(sem, ("deg_ready", "dinv_ready"))
        if layer == 2:
            Y = [sb(f"y{s}", [P, G, C]) for s in range(2)]
            TG = [sb(f"tg{s}", [P, G, C]) for s in range(2)]
            u = [sb(f"u{b}", [FF, 2, CH // 2]) for b in range(2)]
            pf = [ctx.enter_context(nc.psum_tensor(f"{n}pf{b}", [P, 2, 512], F32)) for b in range(2)]
            loaded_x = [sem(f"loaded_x{s}") for s in range(2)]
            up_done, gelu_done, t_ready, tg_ready, xa_ready, tail_ready = map(
                sem, ("up_done", "gelu_done", "t_ready", "tg_ready", "xa_ready", "tail_ready"))
        weight = (net.w_upd, net.w_lin, net.w_out)[layer]
        x_in = (net.x_in, net.x1, net.x2)[layer]
        h_in = (net.h0, net.h1d, net.h2)[layer]
        agg = (net.agg0, net.agg1, net.agg2)[layer]
        x_out = (net.x1, net.x2, net.out)[layer]
        h_out = (net.h1d, net.h2, net.term[0])[layer]
        LAST = SUPER - 1
        in_loads = 2 if layer == 2 else 3

        def at(t, d):
            return 2 * t + d, d % 2, t + d // 2

        def attend_phase(j):
            return (2 * j[0] - 1, 1)

        def mlp_phase(j):
            return (2 * j[0] + 2, 0)
        FIRST_PHASE, LAST_PHASE = (0, 0), (2 * LAST + 1, 1)

        with nc.Block() as block:
            @block.sync
            def _(sp):
                def load(c):
                    number, s, _ = c
                    sp.dma_start(A[s][:, :, :], rows_of(agg, number, G)).then_inc(loaded[s], 16)
                    sp.dma_start(Z[s][:, :, 0:hw], rows_of(h_in, number, G)).then_inc(loaded[s], 16)
                    if layer < 2:
                        sp.dma_start(X[s][:, :, :], rows_of(x_in, number, G)).then_inc(loaded[s], 16)

                def load_x(c):
                    number, s, _ = c
                    sp.dma_start(X[s][:, :, :], rows_of(x_in, number, G)).then_inc(loaded_x[s], 16)

                def store_x(c, tile):
                    number, s, _ = c
                    sp.dma_start(rows_of(x_out, number, G), tile[s][:, :, :]).then_inc(stored_x[s], 16)
                load(at(0, 0))
                load(at(0, 1))

                def store_h(c):
                    number, s, _ = c
                    sp.dma_start(rows_of(h_out, number, G), H[s][:, :, :]).then_inc(stored_h[s], 16)
                if layer < 2:
                    def step(c, after=None, before=None):
                        sp.wait_ge(inputs_used, c[0] + 1)
                        if after is not None:
                            load(after)
                        store_x(c, T)
                        if before is not None:
                            sp.wait_ge(normed, before[0] + 1)
                            store_h(before)
                    step(at(0, 0), at(0, 2))
                    step(at(0, 1), at(0, 3), at(0, 0))
                    with sp.Fori(0, SUPER // 2 - 2) as t:
                        for d in (2, 3):
                            step(at(t, d), at(t, d + 2), at(t, d - 1))
                    for d in (LAST - 1, LAST):
                        step(at(0, d), None, at(0, d - 1))
                    sp.wait_ge(normed, SUPER)
                    store_h(at(0, LAST))
                else:
                    load_x(at(0, 0))
                    load_x(at(0, 1))
                    for d in range(2):
                        sp.wait_ge(inputs_used, d + 1)
                        load(at(0, d + 2))

                    def swap_x(t, d):
                        sp.wait_ge(tail_ready, at(t, d)[0] + 1)
                        store_h(at(t, d))
                        store_x(at(t, d), X)
                        sp.wait_ge(stored_x[d % 2], 16 * (at(t, d)[2] + 1))
                        load_x(at(t, d + 2))
                    with sp.Fori(0, SUPER // 2 - 2) as t:
                        for d in range(2):
                            sp.wait_ge(inputs_used, at(t, d + 2)[0] + 1)
                            load(at(t, d + 4))
                            swap_x(t, d)
                    for d in (LAST - 3, LAST - 2):
                        swap_x(0, d)
                    for d in (LAST - 1, LAST):
                        sp.wait_ge(tail_ready, d + 1)
                        store_h(at(0, d))
                        store_x(at(0, d), X)
                for s in range(2):
                    sp.wait_ge(stored_x[s], 16 * (SUPER // 2))
                    sp.wait_ge(stored_h[s], 16 * (SUPER // 2))

            @block.tensor
            def _(pe):
                def turn(source, phase, i, start):
                    q, b = phase[0] * SUBS + i, (phase[1] + i) % 2
                    if not start or i > 1:
                        pe.wait_ge(zt_ready, q - 1)
                    pe.sem_inc(pe_turn, 1)
                    per = J // TURNS
                    for n in range(TURNS):
                        first = i * J + n * per
                        last = nc.tensor.transpose(pt[b][:, n * P:(n + 1) * P],
                                                   source[:, first:first + per, :].rearrange("p j c -> p (j c)"), net.ident[:, :])
                    last.then_inc(turned, 1)

                def set_bias(b, which):
                    nc.tensor.matmul(po[b][:, 0:J * C], net.ones3[:, :],
                                     net.bias_parts[:, which, :, :].rearrange("k j c -> k (j c)"), start=True, stop=False)

                def products(source, phase, start=False):
                    turn(source, phase, 0, start)
                    for i in range(SUBS):
                        q, b = phase[0] * SUBS + i, (phase[1] + i) % 2
                        if i + 1 < SUBS:
                            turn(source, phase, i + 1, start)
                        pe.wait_ge(zt_ready, q + 1)
                        if not start or i > 1:
                            pe.wait_ge(evacuated, q - 1)
                        pe.sem_inc(pe_turn, 1)
                        width = J * C // TURNS
                        set_bias(b, layer)
                        for n in range(TURNS):
                            last = nc.tensor.matmul(po[b][:, n * width:(n + 1) * width], zt[b][:, n * P:(n + 1) * P], weight[:, :],
                                                    start=False, stop=n == TURNS - 1)
                        last.then_inc(mm_done, 1)

                def mlp(c, phase):
                    number, s, _ = c
                    pe.wait_ge(t_ready, number + 1)

                    def up(i):
                        b = (phase[1] + i) % 2
                        pe.wait_ge(zt_ready, phase[0] * SUBS + i + 1)
                        pe.sem_inc(pe_turn, 1)
                        for half in range(2):
                            lanes = slice(half * C, (half + 1) * C)
                            last = nc.tensor.matmul(pf[b][:, half, 0:CH // 2], net.w1[lanes, :], zt[b][lanes, :], start=True, stop=True)
                        last.then_inc(up_done, 1)

                    def down(i):
                        b = (phase[1] + i) % 2
                        pe.wait_ge(gelu_done, number * SUBS + i + 1)
                        pe.wait_ge(evacuated, phase[0] * SUBS + i - 1)
                        pe.sem_inc(pe_turn, 1)
                        set_bias(b, 3)
                        for j in range(J):
                            half, pair = j % 2, j // 2
                            last = nc.tensor.matmul(po[b][:, j * C:(j + 1) * C], u[b][:, half, pair * P:(pair + 1) * P], net.w2[:, :],
                                                    start=False, stop=j == J - 1)
                        last.then_inc(mm_done, 1)
                    turn(T[s], phase, 0, False)
                    turn(T[s], phase, 1, False)
                    up(0)
                    for i in range(SUBS):
                        if i + 1 < SUBS:
                            up(i + 1)
                        if i + 2 < SUBS:
                            turn(T[s], phase, i + 2, False)
                        down(i)
                if layer < 2:
                    def step(c, start=False):
                        pe.wait_ge(z_ready, c[0] + 1)
                        products((Z if layer == 0 else A)[c[1]], (c[0], c[1]), start)
                    step(at(0, 0), True)
                    with pe.Fori(0, SUPER // 2 - 1) as t:
                        step(at(t, 1))
                        step(at(t, 2))
                    step(at(0, LAST))
                else:
                    def attend(c, phase, start=False):
                        pe.wait_ge(loaded[c[1]], 16 * in_loads * (c[2] + 1))
                        products(A[c[1]], phase, start)
                    attend(at(0, 0), FIRST_PHASE, True)
                    attend(at(0, 1), attend_phase(at(0, 1)))
                    mlp(at(0, 0), mlp_phase(at(0, 0)))
                    with pe.Fori(0, SUPER // 2 - 1) as t:
                        for d in (2, 3):
                            attend(at(t, d), attend_phase(at(t, d)))
                            mlp(at(t, d - 1), mlp_phase(at(t, d - 1)))
                    mlp(at(0, LAST), LAST_PHASE)

            @block.scalar
            def _(act):
                def copy(phase, i, start, after_up=False):
                    q, b = phase[0] * SUBS + i, (phase[1] + i) % 2
                    act.wait_ge(turned, q + 1)
                    if not after_up and (not start or i > 1):
                        act.wait_ge(mm_done, q - 1)
                    nc.scalar.activation(zt[b][:, :], pt[b][:, 0:TURNS * P], ACT.Copy).then_inc(zt_ready, 1)

                def gelu(c, phase, i):
                    q, b = phase[0] * SUBS + i, (phase[1] + i) % 2
                    act.wait_ge(up_done, c[0] * SUBS + i + 1)
                    act.wait_ge(mm_done, q - 1)
                    nc.scalar.activation(u[b][:, :, :], pf[b][:, :, 0:CH // 2], ACT.Gelu, bias=net.b1[:, :]).then_inc(gelu_done, 1)

                def square(r, n=0):
                    act.wait_ge(centred[n], r + 1)
                    nc.scalar.activation(SQ[n][:, :, :], XC[n][:, :, :], ACT.Square, scale=C ** -0.5).then_inc(squared[n], 1)

                def root(r, n=0):
                    act.wait_ge(var_ready[n], r + 1)
                    nc.scalar.activation(rstd[n][:, :], rstd[n][:, :], ACT.Sqrt, bias=net.eps[:, :]).then_inc(rstd_ready[n], 1)

                def degree_root(c):
                    act.wait_ge(deg_ready, c[0] + 1)
                    nc.scalar.activation(dinv[c[1]][:, :], dinv[c[1]][:, :], ACT.Sqrt).then_inc(dinv_ready, 1)
                if layer < 2:
                    def step(c, before=None, after=None):
                        for i in range(SUBS):
                            copy((c[0], c[1]), i, before is None)
                            if before is not None:
                                if i == 2:
                                    square(before[0])
                                elif i == 4:
                                    root(before[0])
                            if layer == 0 and after is not None and i == 5:
                                degree_root(after)
                    if layer == 0:
                        degree_root(at(0, 0))
                    step(at(0, 0), after=at(0, 1))
                    with act.Fori(0, SUPER // 2 - 1) as t:
                        for d in (1, 2):
                            step(at(t, d), at(t, d - 1), at(t, d + 1))
                    step(at(0, LAST), at(0, LAST - 1))
                    square(LAST)
                    root(LAST)
                else:
                    def attend(phase, start=False, y=None):
                        for i in range(SUBS):
                            if phase is not None:
                                copy(phase, i, start)
                            if y is not None and i == 3:
                                square(2 * y[0], 1)
                            elif y is not None and i == 6:
                                root(2 * y[0], 1)

                    def mlp(c, phase, t=None, y=None):
                        if c is not None:
                            copy(phase, 0, False)
                        for i in range(SUBS):
                            if c is not None:
                                if i + 1 < SUBS:
                                    copy(phase, i + 1, False, i + 1 > 1)
                                gelu(c, phase, i)
                            if t is not None and i == 2:
                                square(t[0])
                            elif y is not None and i == 5:
                                square(2 * y[0] + 1, 1)
                        if t is not None:
                            root(t[0])
                        if y is not None:
                            root(2 * y[0] + 1, 1)
                    attend(FIRST_PHASE, True)
                    mlp(None, None, t=at(0, 0))
                    attend(attend_phase(at(0, 1)))
                    mlp(at(0, 0), mlp_phase(at(0, 0)), t=at(0, 1))
                    for d in (2, 3):
                        attend(attend_phase(at(0, d)), y=at(0, d - 2))
                        mlp(at(0, d - 1), mlp_phase(at(0, d - 1)), at(0, d), at(0, d - 2))
                    with act.Fori(0, SUPER // 2 - 2) as t:
                        for d in (4, 5):
                            attend(attend_phase(at(t, d)), y=at(t, d - 2))
                            mlp(at(t, d - 1), mlp_phase(at(t, d - 1)), at(t, d), at(t, d - 2))
                    attend(None, y=at(0, LAST - 1))
                    mlp(at(0, LAST), LAST_PHASE, y=at(0, LAST - 1))
                    attend(None, y=at(0, LAST))
                    mlp(None, None, y=at(0, LAST))

            @block.vector
            def _(v):
                def spread(x):
                    return x.unsqueeze(2).to_broadcast([P, G, C])

                def channels(x):
                    return x.unsqueeze(1).to_broadcast([P, G, C])

                def total(x, n=0):
                    nc.vector.tensor_reduce(mean[n][:, :], x, AX.X, ALU.add)

                def centre(x, n=0):
                    v.drain()
                    nc.vector.tensor_scalar(mean[n][:, :], mean[n][:, :], 1.0 / C, None, ALU.mult)
                    v.drain()
                    nc.vector.tensor_tensor(XC[n][:, :, :], x, spread(mean[n][:, :]), ALU.subtract).then_inc(centred[n], 1)

                def variance(r, n=0):
                    v.wait_ge(squared[n], r + 1)
                    nc.vector.tensor_reduce(rstd[n][:, :], SQ[n][:, :, :], AX.X, ALU.add).then_inc(var_ready[n], 1)

                def scale(y, r, n=0, relu=False):
                    v.wait_ge(rstd_ready[n], r + 1)
                    nc.vector.reciprocal(rstd[n][:, :], rstd[n][:, :])
                    v.drain()
                    if relu:
                        return nc.vector.scalar_tensor_tensor(y, XC[n][:, :, :], 0.0, spread(rstd[n][:, :]), ALU.max, ALU.mult)
                    return nc.vector.tensor_tensor(y, XC[n][:, :, :], spread(rstd[n][:, :]), ALU.mult)

                def evacuate(c, phase, i, m):
                    q, b, s = phase[0] * SUBS + i, (phase[1] + i) % 2, c[1]
                    rows = slice(i * J, (i + 1) * J)
                    got = po[b][:, 0:J * C].rearrange("p (j c) -> p j c", c=C)
                    v.wait_ge(mm_done, q + 1)
                    if layer == 0:
                        nc.vector.scalar_tensor_tensor(T[s][:, rows, :], got, 0.0, X[s][:, rows, :], ALU.max, ALU.add).then_inc(evacuated, 1)
                    elif layer == 1:
                        nc.vector.tensor_tensor(T[s][:, rows, :], got, X[s][:, rows, :], ALU.add).then_inc(evacuated, 1)
                    elif m == 0:
                        nc.vector.tensor_tensor(T[s][:, rows, :], got, Z[s][:, rows, :], ALU.add).then_inc(evacuated, 1)
                    else:
                        nc.vector.tensor_tensor(Y[s][:, rows, :], got, TG[s][:, rows, :], ALU.add).then_inc(evacuated, 1)

                def counts(c):
                    number, s, h = c
                    v.wait_ge(loaded[s], 16 * in_loads * (h + 1))
                    nc.vector.tensor_scalar(dinv[s][:, :], A[s][:, :, C], 1.0, None, ALU.max)
                    v.drain()
                    nc.vector.reciprocal(inv_count[s][:, :], dinv[s][:, :]).then_inc(deg_ready, 1)

                def roots(c):
                    v.wait_ge(dinv_ready, c[0] + 1)
                    nc.vector.reciprocal(dinv[c[1]][:, :], dinv[c[1]][:, :])

                if layer < 2:
                    def norm_step(c, i):
                        number, s, h = c
                        if i == 0:
                            total(T[s][:, :, :])
                            if layer == 0:
                                v.wait_ge(stored_h[s], 16 * h)
                                nc.vector.tensor_copy(H[s][:, :, C], dinv[s][:, :])
                        elif i == 1:
                            centre(T[s][:, :, :])
                        elif i == 3:
                            variance(number)
                        elif i == 5:
                            if layer == 1:
                                v.wait_ge(stored_h[s], 16 * h)
                            scale(H[s][:, :, 0:C], number, relu=True).then_inc(normed, 1)

                    def step(c, before=None, after=None):
                        v.wait_ge(stored_x[c[1]], 16 * c[2])
                        v.wait_ge(loaded[c[1]], 16 * in_loads * (c[2] + 1))
                        for i in range(SUBS):
                            evacuate(c, (c[0], c[1]), i, 0)
                            if before is not None:
                                norm_step(before, i)
                            if layer == 0 and after is not None and i == 4:
                                counts(after)
                            elif layer == 0 and after is not None and i == 6:
                                roots(after)
                        v.drain()
                        v.sem_inc(inputs_used, 1)
                    if layer == 0:
                        counts(at(0, 0))
                        roots(at(0, 0))
                    step(at(0, 0), after=at(0, 1))
                    with v.Fori(0, SUPER // 2 - 1) as t:
                        for d in (1, 2):
                            step(at(t, d), at(t, d - 1), at(t, d + 1))
                    step(at(0, LAST), at(0, LAST - 1))
                    for i in range(SUBS):
                        norm_step(at(0, LAST), i)
                else:
                    def attend(c, phase, x=None, t=None, y=None):
                        for i in range(SUBS):
                            if c is not None:
                                if i == 0:
                                    v.wait_ge(loaded[c[1]], 16 * in_loads * (c[2] + 1))
                                evacuate(c, phase, i, 0)
                            if x is not None and i == 0:
                                v.wait_ge(stored_h[x[1]], 16 * x[2])
                                nc.vector.memset(H[x[1]][:, :, C:C + 1], 0.0)
                                scale(H[x[1]][:, :, 0:C], 2 * x[0] + 1, 1, relu=True).then_inc(normed, 1)
                            elif t is not None and i == 1:
                                scale(T[t[1]][:, :, :], t[0]).then_inc(t_ready, 1)
                            elif y is not None and i == 2:
                                centre(Y[y[1]][:, :, :], 1)
                            elif y is not None and i == 5:
                                variance(2 * y[0], 1)
                        v.drain()
                        if c is not None:
                            v.sem_inc(inputs_used, 1)

                    def mlp(c, phase, t=None, y=None):
                        for i in range(SUBS):
                            if c is not None:
                                if i == 0:
                                    v.wait_ge(tg_ready, c[0] + 1)
                                evacuate(c, phase, i, 1)
                            if t is not None:
                                if i == 0:
                                    total(T[t[1]][:, :, :])
                                elif i == 1:
                                    centre(T[t[1]][:, :, :])
                                elif i == 3:
                                    variance(t[0])
                            if y is not None:
                                xs, ys = X[y[1]][:, :, :], Y[y[1]][:, :, :]
                                if i == 0:
                                    scale(ys, 2 * y[0], 1)
                                elif i == 1:
                                    v.drain()
                                    nc.vector.tensor_tensor(ys, ys, channels(net.norms[:, 2, :]), ALU.mult)
                                elif i == 2:
                                    v.drain()
                                    v.wait_ge(xa_ready, y[0] + 1)
                                    nc.vector.tensor_tensor(xs, xs, ys, ALU.add)
                                elif i == 3:
                                    v.drain()
                                    total(xs, 1)
                                elif i == 4:
                                    centre(xs, 1)
                                elif i == 5:
                                    variance(2 * y[0] + 1, 1)
                        v.drain()
                        if c is not None:
                            total(Y[c[1]][:, :, :], 1)
                    attend(at(0, 0), FIRST_PHASE)
                    mlp(None, None, t=at(0, 0))
                    attend(at(0, 1), attend_phase(at(0, 1)), t=at(0, 0))
                    mlp(at(0, 0), mlp_phase(at(0, 0)), t=at(0, 1))
                    attend(at(0, 2), attend_phase(at(0, 2)), None, at(0, 1), at(0, 0))
                    mlp(at(0, 1), mlp_phase(at(0, 1)), at(0, 2), at(0, 0))
                    attend(at(0, 3), attend_phase(at(0, 3)), at(0, 0), at(0, 2), at(0, 1))
                    mlp(at(0, 2), mlp_phase(at(0, 2)), at(0, 3), at(0, 1))
                    with v.Fori(0, SUPER // 2 - 2) as t:
                        for d in (4, 5):
                            attend(at(t, d), attend_phase(at(t, d)), at(t, d - 3), at(t, d - 1), at(t, d - 2))
                            mlp(at(t, d - 1), mlp_phase(at(t, d - 1)), at(t, d), at(t, d - 2))
                    attend(None, None, at(0, LAST - 2), at(0, LAST), at(0, LAST - 1))
                    mlp(at(0, LAST), LAST_PHASE, None, at(0, LAST - 1))
                    attend(None, None, at(0, LAST - 1), None, at(0, LAST))
                    mlp(None, None, None, at(0, LAST))
                    attend(None, None, at(0, LAST))

            @block.gpsimd
            def _(pool):
                if layer < 2:
                    with pool.Fori(0, SUPER // 2) as t:
                        for s in range(2):
                            pool.wait_ge(loaded[s], 16 * in_loads * (t + 1))
                            if layer == 0:
                                pool.wait_ge(deg_ready, 2 * t + s + 1)
                                nc.gpsimd.tensor_tensor(Z[s][:, :, C:P], A[s][:, :, 0:C],
                                                        inv_count[s][:, :].unsqueeze(2).to_broadcast([P, G, C]), ALU.mult).then_inc(z_ready, 1)
                            else:
                                nc.gpsimd.tensor_tensor(A[s][:, :, :], A[s][:, :, :], Z[s][:, :, C:C + 1].to_broadcast([P, G, C]), ALU.mult)
                                pool.drain()
                                nc.gpsimd.tensor_tensor(A[s][:, :, :], A[s][:, :, :], Z[s][:, :, 0:C], ALU.add).then_inc(z_ready, 1)
                else:
                    def channels(which):
                        return net.norms[:, which, :].unsqueeze(1).to_broadcast([P, G, C])

                    def gained(c):
                        pool.wait_ge(t_ready, c[0] + 1)
                        nc.gpsimd.tensor_tensor(TG[c[1]][:, :, :], T[c[1]][:, :, :], channels(0), ALU.mult).then_inc(tg_ready, 1)

                    def offset(c):
                        number, s, h = c
                        pool.wait_ge(loaded_x[s], 16 * (h + 1))
                        nc.gpsimd.tensor_tensor(X[s][:, :, :], X[s][:, :, :], channels(3), ALU.add).then_inc(xa_ready, 1)

                    def tail(c):
                        number, s, h = c
                        pool.wait_ge(normed, number + 1)
                        nc.gpsimd.tensor_tensor(X[s][:, :, :], X[s][:, :, :], H[s][:, :, 0:C], ALU.add).then_inc(tail_ready, 1)
                    offset(at(0, 0))
                    gained(at(0, 0))
                    offset(at(0, 1))
                    gained(at(0, 1))
                    with pool.Fori(0, SUPER // 2 - 1) as t:
                        for d in (2, 3):
                            gained(at(t, d))
                            tail(at(t, d - 2))
                            offset(at(t, d))
                    tail(at(0, LAST - 1))
                    tail(at(0, LAST))


T_ALL = EP // P
BLOCK = 10
DIGITS = 256
LIST_SPARE = 1 + EP + J
LIST_ROWS = LIST_SPARE + SPARE
LIST_CHUNKS = -(-EDGES // CH)


def sort_by_source(nc, net):
    with ExitStack() as ctx:
        ctx.callback(nc.all_engine_barrier)
        def sb(name, shape, dt=F32):
            return ctx.enter_context(nc.sbuf_tensor("s_" + name, shape, dt))

        def sem(name):
            return stage_semaphore(nc, ctx, "s_" + name)
        before_f = sb("before_f", [P, P])
        before = sb("before", [P, P], BF16)
        all_ones = sb("all_ones", [P, P], BF16)
        iota_f = sb("iota_f", [P, DIGITS])
        iota = sb("iota", [P, DIGITS], BF16)
        zero_row = sb("zero_row", [P, DIGITS], BF16)
        columns = [sb("col_src", [P, T_ALL], I32), sb("col_dst", [P, T_ALL], I32), sb("col_weight", [P, T_ALL])]
        rec = sb("rec", [P, T_ALL, 4], I32)
        part = sb("part", [P, T_ALL], I32)
        digit = sb("digit", [P, T_ALL])
        lane = sb("lane", [P, BLOCK])
        hots = [sb(f"hots{b}", [P, DIGITS], BF16) for b in range(4)]
        picked = sb("picked", [P, DIGITS])
        start_at = [sb(f"start_at{b}", [P, DIGITS]) for b in range(2)]
        rank = sb("rank", [P, BLOCK])
        ri = sb("ri", [P, BLOCK], I32)
        lo7 = sb("lo7", [P, BLOCK], I32)
        hi7 = sb("hi7", [P, BLOCK], I32)
        place = [sb(f"place{b}", [P, BLOCK], I32) for b in range(2)]
        recs = [sb(f"recs{b}", [P, BLOCK, 4], I32) for b in range(2)]
        none = sb("none", [1, 4], I32)
        blank = sb("blank", [P, 4 * T_ALL], I32)
        acc = [ctx.enter_context(nc.psum_tensor(f"s_acc{d}", [P, 512], F32)) for d in range(2)]
        within = ctx.enter_context(nc.psum_tensor("s_within", [P, 512], F32))
        names = ("loaded", "made", "hot", "freed", "counted", "ranked", "placed", "pool_turn", "reloaded", "filled", "summed", "based")
        (loaded, made, hot, freed, counted, ranked, placed, pool_turn, reloaded, filled, summed, based) = map(sem, names)
        scattered = [sem(f"scattered{b}") for b in range(2)]
        rounds = T_ALL // (2 * BLOCK)
        with nc.Block() as block:
            @block.sync
            def _(sp):
                sp.dma_start(before_f[:, :], net.dram["c_before"][:, :]).then_inc(loaded, 16)
                sp.dma_start(iota_f[:, :], net.dram["c_iota256"][:, :]).then_inc(loaded, 16)
                for tile, col in zip(columns, (net.src, net.dst_ext[1:1 + EP], net.dram["weight"])):
                    sp.dma_start(tile[:, :], col.rearrange("(p t) -> p t", p=P)).then_inc(loaded, 16)
                sp.wait_ge(made, 1)
                for n in range(2):
                    sp.dma_start(net.lists[n][0:1, :], none[:, :]).then_inc(filled, 16)
                    sp.dma_start(net.lists[n][1 + EP:1 + EP + J, :], blank[0:J, 0:4]).then_inc(filled, 16)
                sp.dma_start(net.lists[1][1:1 + EP, :].rearrange("(p t) c -> p (t c)", p=P), blank[:, :]).then_inc(filled, 16)
                for b in range(2):
                    sp.wait_ge(scattered[b], 16 * BLOCK * rounds)
                sp.dma_start(rec[:, :, :].rearrange("p t c -> p (t c)"),
                             net.half_sorted.rearrange("(p t) c -> p (t c)", p=P)).then_inc(reloaded, 16)
                sp.wait_ge(filled, 5 * 16)

            @block.vector
            def _(v):
                nc.vector.memset(none[:, :], -1)
                v.drain()
                nc.vector.memset(blank[:, :], 0).then_inc(made, 1)
                nc.vector.memset(all_ones[:, :], 1.0)
                nc.vector.memset(zero_row[:, :], 0.0)
                nc.vector.memset(rec[:, :, :], 0)
                v.wait_ge(loaded, 5 * 16)
                nc.vector.tensor_copy(before[:, :], before_f[:, :])
                nc.vector.tensor_copy(iota[:, :], iota_f[:, :])
                v.drain()
                for c in range(2):
                    nc.vector.tensor_copy(rec[:, :, c], columns[c][:, :])
                nc.vector.tensor_scalar(rec[:, :, 2], columns[2][:, :].bitcast(I32), 0, None, ALU.bitwise_or).then_inc(made, 1)
                v.drain()
                for d in range(2):
                    if d == 1:
                        v.wait_ge(reloaded, 16)
                    nc.vector.tensor_scalar(part[:, :], rec[:, :, 0], 255 if d == 0 else 8, None,
                                            ALU.bitwise_and if d == 0 else ALU.logical_shift_right)
                    v.drain()
                    nc.vector.tensor_copy(digit[:, :], part[:, :])
                    v.drain()
                    with v.Fori(0, rounds) as t:
                        for s in range(2):
                            nc.vector.tensor_copy(lane[:, :], digit[:, bass.ds(BLOCK * (2 * t + s), BLOCK)])
                            v.drain()
                            for q in range(BLOCK):
                                n = s * BLOCK + q
                                v.wait_ge(freed, T_ALL * d + 2 * BLOCK * t + n + 1)
                                nc.vector.tensor_scalar(hots[n % 4][:, :], iota[:, :], lane[:, q:q + 1], None, ALU.is_gt).then_inc(hot, 1)
                            v.drain()
                    v.wait_ge(freed, T_ALL * (d + 1) + 4)
                    with v.Fori(0, rounds) as t:
                        for s in range(2):
                            nc.vector.tensor_copy(lane[:, :], digit[:, bass.ds(BLOCK * (2 * t + s), BLOCK)])
                            v.drain()

                            def one_hot(q):
                                n = s * BLOCK + q
                                nc.vector.tensor_scalar(hots[n % 4][:, :], iota[:, :], lane[:, q:q + 1], None, ALU.is_equal).then_inc(hot, 1)
                            one_hot(0)
                            for q in range(BLOCK):
                                n = s * BLOCK + q
                                if q + 1 < BLOCK:
                                    one_hot(q + 1)
                                v.wait_ge(counted, T_ALL * d + 2 * BLOCK * t + n + 1)
                                nc.vector.tensor_tensor_reduce(out=picked[:, :], in0=within[:, 0:DIGITS], in1=hots[n % 4][:, :],
                                                               scale=1.0, scalar=0.0, op0=ALU.mult, op1=ALU.add,
                                                               accum_out=rank[:, q:q + 1]).then_inc(ranked, 1)
                            v.drain()
                            v.wait_ge(scattered[s], 16 * BLOCK * (rounds * d + t))
                            nc.vector.tensor_scalar(recs[s][:, :, :], rec[:, bass.ds(BLOCK * (2 * t + s), BLOCK), :], 0, None, ALU.bitwise_or)
                            if d == 0:
                                nc.vector.tensor_copy(ri[:, :], rank[:, :])
                                v.drain()
                                nc.vector.tensor_scalar(lo7[:, :], ri[:, :], P - 1, None, ALU.bitwise_and)
                                nc.vector.tensor_scalar(hi7[:, :], ri[:, :], 7, None, ALU.logical_shift_right)
                                v.drain()
                                nc.vector.scalar_tensor_tensor(place[s][:, :], lo7[:, :], float(T_ALL), hi7[:, :], ALU.mult, ALU.add).then_inc(placed, 1)
                            else:
                                nc.vector.tensor_scalar(place[s][:, :], rank[:, :], 1.0, None, ALU.add).then_inc(placed, 1)
                            v.drain()

            @block.tensor
            def _(pe):
                for _ in range(4):
                    pe.sem_inc(freed, 1)
                pe.wait_ge(made, 2)
                for d in range(2):
                    nc.tensor.matmul(acc[0][:, 0:DIGITS], all_ones[:, :], zero_row[:, :], start=True, stop=False)
                    with pe.Fori(0, rounds) as t:
                        for n in range(2 * BLOCK):
                            pe.wait_ge(hot, 2 * T_ALL * d + 2 * BLOCK * t + n + 1)
                            nc.tensor.matmul(acc[0][:, 0:DIGITS], all_ones[:, :], hots[n % 4][:, :], start=False, stop=False).then_inc(freed, 1)
                    nc.tensor.matmul(acc[0][:, 0:DIGITS], all_ones[:, :], zero_row[:, :], start=False, stop=True).then_inc(summed, 1)
                    with pe.Fori(0, rounds) as t:
                        for n in range(2 * BLOCK):
                            m = T_ALL * d + 2 * BLOCK * t + n
                            pe.wait_ge(hot, T_ALL * (2 * d + 1) + 2 * BLOCK * t + n + 1)
                            pe.wait_ge(based, m + d + 1)
                            nc.tensor.matmul(acc[n % 2][:, 0:DIGITS], net.ident[:, :], start_at[n % 2][:, :], start=True, stop=False)
                            nc.tensor.matmul(acc[n % 2][:, 0:DIGITS], all_ones[:, :], hots[n % 4][:, :], start=False, stop=True).then_inc(summed, 1)
                            pe.wait_ge(ranked, m)
                            nc.tensor.matmul(within[:, 0:DIGITS], net.ident[:, :], start_at[n % 2][:, :], start=True, stop=False)
                            nc.tensor.matmul(within[:, 0:DIGITS], before[:, :], hots[n % 4][:, :], start=False, stop=True).then_inc(counted, 1)

            @block.scalar
            def _(act):
                for d in range(2):
                    if d:
                        act.wait_ge(based, (T_ALL + 1) * d)
                    act.wait_ge(summed, (T_ALL + 1) * d + 1)
                    nc.scalar.activation(start_at[0][:, :], acc[0][:, 0:DIGITS], ACT.Copy).then_inc(based, 1)
                    with act.Fori(0, rounds) as t:
                        for n in range(2 * BLOCK):
                            m = T_ALL * d + 2 * BLOCK * t + n
                            act.wait_ge(summed, m + d + 2)
                            act.wait_ge(counted, m)
                            nc.scalar.activation(start_at[(n + 1) % 2][:, :], acc[n % 2][:, 0:DIGITS], ACT.Copy).then_inc(based, 1)

            @block.gpsimd
            def _(pool):
                for d in range(2):
                    table = (net.half_sorted, net.lists[0])[d]
                    with pool.Fori(0, rounds) as t:
                        for s in range(2):
                            pool.wait_ge(placed, 2 * rounds * d + 2 * t + s + 1)
                            pool.sem_inc(pool_turn, 1)
                            for q in range(BLOCK):
                                pool.indirect_dma_start(table[:, :], bass.IndirectOffsetOnAxis(ap=place[s][:, q:q + 1], axis=0),
                                                        recs[s][:, q, :], None).then_inc(scattered[s], 16)
                for s in range(2):
                    pool.wait_ge(scattered[s], 2 * 16 * BLOCK * rounds)


def diffuse(nc, net):
    W = C + 1
    with ExitStack() as ctx:
        ctx.callback(nc.all_engine_barrier)
        def sb(name, shape, dt=F32):
            return ctx.enter_context(nc.sbuf_tensor("d_" + name, shape, dt))

        def ps(name):
            return ctx.enter_context(nc.psum_tensor("d_" + name, [P, 512], F32))

        def sem(name):
            return stage_semaphore(nc, ctx, "d_" + name)
        before_f = sb("before_f", [P, P])
        before = sb("before", [P, P], BF16)
        all_ones = sb("all_ones", [P, P], BF16)
        ratios = sb("ratios", [P, STEPS])
        tcol = sb("tcol", [P, 1])
        pos0 = sb("pos0", [P, J + 2])
        node_spare = [sb(f"node_spare{s}", [P, J]) for s in range(2)]
        list_spare = [sb(f"list_spare{s}", [P, J]) for s in range(2)]
        last_step = sb("last_step", [P, 1])
        next_step = sb("next_step", [P, 1])
        coef = sb("coef", [P, 1])
        base = sb("base", [P, 1])
        have = sb("have", [P, 1])
        passed = sb("passed", [P, 1])
        have_i = sb("have_i", [P, 1], I32)
        rec = [sb(f"rec{s}", [P, J + 2, 4], I32) for s in range(2)]
        inside = sb("inside", [P, J + 2])
        srcs = sb("srcs", [P, J + 2])
        keep = sb("keep", [P, J], BF16)
        is_end = sb("is_end", [P, J])
        end_f = sb("end_f", [P, J])
        end = [sb(f"end{s}", [P, J], I32) for s in range(2)]
        near = [sb(f"near{s}", [P, J, W]) for s in range(2)]
        nonzero = sb("nonzero", [P, J, C])
        live = sb("live", [P, J])
        liveb = sb("liveb", [P, J], BF16)
        some = sb("some", [P, J])
        wl = sb("wl", [P, J])
        prod = sb("prod", [P, J, W])
        turned = sb("turned_sb", [W, CH])
        scan = sb("scan", [W, CH])
        carry = sb("carry", [W, 1])
        out = [sb(f"out{s}", [P, J, W]) for s in range(2)]
        counts = sb("counts", [P, 2 * J])
        ahead = sb("ahead", [P, 2])
        upto = sb("upto", [P, J])
        place_f = sb("place_f", [P, J])
        place = [sb(f"place{s}", [P, J], I32) for s in range(2)]
        pt, pk, pr, pc = ps("pt"), ps("pk"), ps("pr"), ps("pc")
        names = ("loaded", "set_up", "ready", "spread", "moved", "scanned", "back",
                 "out_ready", "placed", "stepped", "turn_pool", "turn_pe", "seen", "step_turn")
        (loaded, set_up, ready, spread, moved, scanned, back,
         out_ready, placed, stepped, turn_pool, turn_pe, seen, step_turn) = map(sem, names)
        rec_loaded, gathered, stored, passed_on = (
            [sem(f"{x}{s}") for s in range(2)] for x in ("rec_loaded", "gathered", "stored", "passed_on"))

        def chunks_of(engine):
            n = engine.value_load(have_i[0:1, 0:1], min_val=0, max_val=EDGES)
            return engine.snap((n + (CH - 1)) >> 9, min_val=0, max_val=LIST_CHUNKS)

        class Counts:
            def __init__(self, engine, name):
                self.engine = engine
                self.begun = [engine.alloc_register(f"begun{s}_{name}") for s in range(2)]
                self.done = [engine.alloc_register(f"done{s}_{name}") for s in range(2)]
                self.total = engine.alloc_register(f"total_{name}")
                for r in (*self.begun, *self.done, self.total):
                    engine.reg_mov(r, 0)

            def read(self, register):
                return self.engine.snap(register, min_val=0, max_val=STEPS * (CHUNKS + 1))

            def finished(self, s):
                self.engine.reg_add(self.done[s], self.done[s], 1)
                self.engine.reg_add(self.total, self.total, 1)

        def nothing(*_):
            pass

        def step_chunks(engine, n, begin, finish, parity):
            def start(c, s):
                begin(parity, c, s, n)
                engine.reg_add(n.begun[s], n.begun[s], 1)

            def end_of(s):
                finish(parity, s, n)
                n.finished(s)
            chunks = chunks_of(engine)
            pairs = engine.snap(chunks >> 1, min_val=0, max_val=LIST_CHUNKS // 2)
            odd = engine.snap(chunks - 2 * pairs, min_val=0, max_val=1)
            with engine.If(chunks > 0):
                start(0, 0)
                with engine.If(pairs > 0):
                    with engine.Fori(0, pairs) as t:
                        start(2 * t + 1, 1)
                        end_of(0)
                        start(2 * t + 2, 0)
                        end_of(1)
                with engine.If(odd > 0):
                    end_of(0)

        def steps(engine, name, begin, finish):
            n = Counts(engine, name)
            with engine.Fori(0, STEPS // 2) as t:
                for parity in (1, 0):
                    engine.wait_ge(stepped, 2 * t + 2 - parity)
                    engine.sem_inc(step_turn, 1)
                    step_chunks(engine, n, begin, finish, parity)
                    engine.sem_inc(seen, 1)

        with nc.Block() as block:
            @block.sync
            def _(sp):
                for dst, src in ((before_f, "c_before"), (ratios, "c_ratios"), (pos0, "c_pos0"),
                                 (node_spare[0], "c_node_spare"), (list_spare[0], "c_list_spare")):
                    sp.dma_start(dst[:, :], net.dram[src][:, :]).then_inc(loaded, 16)
                sp.dma_start(tcol[:, :], net.dram["L3_gnn_t"][None, :].to_broadcast([P, 1])).then_inc(loaded, 16)

                def begin(parity, c, s, n):
                    sp.wait_ge(gathered[s], n.read(n.begun[s]) * (16 * J))
                    sp.wait_ge(passed_on[s], n.read(n.done[s]) * (16 * J))
                    rows = net.lists[1 - parity]
                    sp.dma_start(rec[s][:, 0:J, :], rows[bass.ds(c * CH, CH), :].rearrange("(p j) c -> p j c", j=J)).then_inc(rec_loaded[s], 16)
                    sp.dma_start(rec[s][:, J:J + 2, :], rows[bass.ds(c * CH + J, CH), :].rearrange("(p j) c -> p j c", j=J)[:, 0:2, :]).then_inc(rec_loaded[s], 16)
                steps(sp, "sp", begin, nothing)

            @block.gpsimd
            def _(pool):
                def begin(parity, c, s, n):
                    pool.wait_ge(rec_loaded[s], n.read(n.begun[s]) * 32 + 32)
                    pool.sem_inc(turn_pool, 1)
                    for j in range(J):
                        pool.indirect_dma_start(near[s][:, j, :], None, net.term[1 - parity][:, :],
                                                bass.IndirectOffsetOnAxis(ap=rec[s][:, 1 + j, 1:2], axis=0)).then_inc(gathered[s], 16)

                def finish(parity, s, n):
                    k = n.read(n.total)
                    pool.wait_ge(placed, k + 1)
                    pool.sem_inc(turn_pool, 1)
                    for j in range(J):
                        pool.indirect_dma_start(net.lists[parity][:, :], bass.IndirectOffsetOnAxis(ap=place[s][:, j:j + 1], axis=0),
                                                rec[s][:, 1 + j, :], None).then_inc(passed_on[s], 16)
                    pool.wait_ge(out_ready, k + 1)
                    pool.sem_inc(turn_pool, 1)
                    for j in range(J):
                        pool.indirect_dma_start(net.term[parity][:, :], bass.IndirectOffsetOnAxis(ap=end[s][:, j:j + 1], axis=0),
                                                out[s][:, j, :], None).then_inc(stored[s], 16)
                        pool.indirect_dma_start(net.out[:, :], bass.IndirectOffsetOnAxis(ap=end[s][:, j:j + 1], axis=0),
                                                out[s][:, j, 0:C], None, compute_op=ALU.add).then_inc(stored[s], 16)
                steps(pool, "pool", begin, finish)

            @block.tensor
            def _(pe):
                pe.wait_ge(set_up, 1)

                def finish(parity, s, n):
                    k = n.read(n.total)
                    pe.wait_ge(ready, k + 1)
                    pe.sem_inc(turn_pe, 1)
                    nc.tensor.matmul(pc[:, 0:J], before[:, :], liveb[:, :], start=True, stop=True)
                    nc.tensor.matmul(pc[:, J:2 * J], all_ones[:, :], liveb[:, :], start=True, stop=True)
                    for j in range(J):
                        nc.tensor.matmul(pk[0:W, j:CH:J], keep[:, j:j + 1].to_broadcast([P, W]), net.identb[:, :], start=True, stop=True)
                    for j in range(J):
                        last = nc.tensor.transpose(pt[0:W, j:CH:J], prod[:, j, :], net.ident[:, :])
                    last.then_inc(spread, 1)
                    pe.wait_ge(scanned, k + 1)
                    pe.sem_inc(turn_pe, 1)
                    for j in range(J):
                        last = nc.tensor.transpose(pr[:, j * W:(j + 1) * W], scan[:, j:CH:J], net.ident[0:W, 0:W])
                    last.then_inc(back, 1)
                steps(pe, "pe", nothing, finish)

            @block.scalar
            def _(act):
                def finish(parity, s, n):
                    k = n.read(n.total)
                    act.wait_ge(spread, k + 1)
                    nc.scalar.activation(turned[:, :], pt[0:W, :], ACT.Copy).then_inc(moved, 1)
                steps(act, "act", nothing, finish)

            @block.vector
            def _(v):
                v.wait_ge(loaded, 6 * 16)
                nc.vector.tensor_copy(before[:, :], before_f[:, :])
                nc.vector.memset(all_ones[:, :], 1.0)
                for spare in (node_spare, list_spare):
                    nc.vector.tensor_scalar(spare[1][:, :], spare[0][:, :], float(CH), None, ALU.add)
                nc.vector.memset(carry[:, :], 0.0)
                nc.vector.tensor_scalar(tcol[:, :], tcol[:, :], 1e-8, -1.0 / N_SUB, ALU.max, ALU.mult)
                nc.vector.memset(last_step[:, :], 0.0)
                nc.vector.memset(next_step[:, :], 2.0)
                nc.vector.memset(base[:, :], 0.0)
                nc.vector.memset(passed[:, :], 0.0)
                nc.vector.memset(have[:, :], float(EDGES))
                nc.vector.memset(have_i[:, :], EDGES)
                v.drain()
                nc.vector.tensor_scalar(ratios[:, :], ratios[:, :], tcol[:, :], None, ALU.mult).then_inc(set_up, 1)
                v.drain()
                n = Counts(v, "v")

                def finish(parity, s, n):
                    k = n.read(n.total)
                    begun, done = n.read(n.begun[s]), n.read(n.done[s])
                    r = rec[s]
                    v.wait_ge(rec_loaded[s], begun * 32)
                    nc.vector.tensor_scalar(inside[:, :], pos0[:, :], base[:, :], have[:, :], ALU.add, ALU.is_lt)
                    v.drain()
                    nc.vector.scalar_tensor_tensor(srcs[:, :], r[:, :, 0], 1.0, inside[:, :], ALU.add, ALU.mult)
                    v.drain()
                    nc.vector.tensor_tensor(keep[:, :], srcs[:, 1:J + 1], srcs[:, 0:J], ALU.is_equal)
                    nc.vector.tensor_tensor(is_end[:, :], srcs[:, 1:J + 1], srcs[:, 2:J + 2], ALU.not_equal)
                    nc.vector.tensor_scalar(end_f[:, :], srcs[:, 1:J + 1], -1.0, None, ALU.add)
                    v.drain()
                    nc.vector.tensor_tensor(end_f[:, :], end_f[:, :], node_spare[s][:, :], ALU.subtract)
                    nc.vector.tensor_tensor(is_end[:, :], is_end[:, :], inside[:, 1:J + 1], ALU.mult)
                    v.drain()
                    nc.vector.tensor_tensor(end_f[:, :], end_f[:, :], is_end[:, :], ALU.mult)
                    v.drain()
                    v.wait_ge(stored[s], done * (32 * J))
                    v.wait_ge(passed_on[s], done * (16 * J))
                    nc.vector.tensor_tensor(end[s][:, :], end_f[:, :], node_spare[s][:, :], ALU.add)
                    v.wait_ge(gathered[s], begun * (16 * J))
                    nc.vector.tensor_scalar(nonzero[:, :, :], near[s][:, :, 0:C], 0.0, None, ALU.not_equal)
                    nc.vector.tensor_scalar(live[:, :], near[s][:, :, C], last_step[:, :], None, ALU.is_equal)
                    v.drain()
                    nc.vector.tensor_reduce(some[:, :], nonzero[:, :, :], AX.X, ALU.max)
                    nc.vector.tensor_tensor(live[:, :], live[:, :], inside[:, 1:J + 1], ALU.mult)
                    v.drain()
                    nc.vector.tensor_tensor(live[:, :], live[:, :], some[:, :], ALU.mult)
                    v.drain()
                    nc.vector.tensor_copy(liveb[:, :], live[:, :])
                    nc.vector.scalar_tensor_tensor(wl[:, :], r[:, 1:J + 1, 2].bitcast(F32), coef[:, :], live[:, :], ALU.mult, ALU.mult)
                    nc.vector.tensor_copy(prod[:, :, C], live[:, :])
                    v.drain()
                    nc.vector.tensor_tensor(prod[:, :, 0:C], near[s][:, :, 0:C], wl[:, :].unsqueeze(2).to_broadcast([P, J, C]),
                                            ALU.mult).then_inc(ready, 1)
                    nc.vector.tensor_tensor_scan(upto[:, :], all_ones[:, 0:J], live[:, :], 0.0, ALU.mult, ALU.add)
                    v.drain()
                    nc.vector.tensor_tensor(upto[:, :], upto[:, :], live[:, :], ALU.subtract)
                    v.wait_ge(spread, k + 1)
                    nc.vector.tensor_copy(counts[:, :], pc[:, 0:2 * J])
                    v.drain()
                    nc.vector.tensor_reduce(ahead[:, :], counts[:, :].rearrange("p (a j) -> p a j", a=2), AX.X, ALU.add)
                    v.drain()
                    nc.vector.tensor_scalar(place_f[:, :], upto[:, :], ahead[:, 0:1], passed[:, :], ALU.add, ALU.add)
                    v.drain()
                    nc.vector.scalar_tensor_tensor(place_f[:, :], place_f[:, :], 1.0, list_spare[s][:, :], ALU.add, ALU.subtract)
                    nc.vector.tensor_tensor(passed[:, :], passed[:, :], ahead[:, 1:2], ALU.add)
                    nc.vector.tensor_scalar(base[:, :], base[:, :], float(CH), None, ALU.add)
                    v.drain()
                    nc.vector.tensor_tensor(place_f[:, :], place_f[:, :], live[:, :], ALU.mult)
                    v.drain()
                    nc.vector.tensor_tensor(place[s][:, :], place_f[:, :], list_spare[s][:, :], ALU.add).then_inc(placed, 1)
                    v.wait_ge(moved, k + 1)
                    nc.vector.tensor_tensor_scan(scan[:, :], pk[0:W, :], turned[:, :], carry[:, :], ALU.mult, ALU.add).then_inc(scanned, 1)
                    v.drain()
                    nc.vector.tensor_copy(carry[:, :], scan[:, CH - 1:CH])
                    v.wait_ge(back, k + 1)
                    sums = pr[:, 0:J * W].rearrange("p (j c) -> p j c", c=W)
                    nc.vector.tensor_scalar(out[s][:, :, C], sums[:, :, C], 0.0, next_step[:, :], ALU.is_gt, ALU.mult)
                    nc.vector.tensor_copy(out[s][:, :, 0:C], sums[:, :, 0:C])
                    v.drain()
                    nc.vector.tensor_scalar(out[s][:, :, C], out[s][:, :, C], -1.0, None, ALU.add).then_inc(out_ready, 1)

                with v.Fori(0, STEPS // 2) as t:
                    for parity in (1, 0):
                        nc.vector.tensor_copy(coef[:, :], ratios[:, bass.ds(2 * t + (1 - parity), 1)])
                        v.drain()
                        v.sem_inc(stepped, 1)
                        step_chunks(v, n, nothing, finish, parity)
                        for s in range(2):
                            v.wait_ge(gathered[s], n.read(n.begun[s]) * (16 * J))
                            v.wait_ge(stored[s], n.read(n.done[s]) * (32 * J))
                            v.wait_ge(passed_on[s], n.read(n.done[s]) * (16 * J))
                        v.wait_ge(seen, 4 * (2 * t + (2 - parity)))
                        nc.vector.tensor_copy(have[:, :], passed[:, :])
                        nc.vector.tensor_copy(have_i[:, :], passed[:, :])
                        for x in (last_step, next_step):
                            nc.vector.tensor_scalar(x[:, :], x[:, :], 1.0, None, ALU.add)
                        nc.vector.memset(base[:, :], 0.0)
                        v.drain()
                        nc.vector.memset(passed[:, :], 0.0)
                        v.drain()


INPUTS = ["x", "src", "dst", "edge_type_8", "edge_weight", "L0_gnn_W_msg", "L0_gnn_b_msg", "L0_gnn_W_upd", "L0_gnn_b_upd",
          "L1_gnn_W", "L1_gnn_b", "L2_gnn_task_embedding", "L2_gnn_Wq", "L2_gnn_bq", "L2_gnn_Wk", "L2_gnn_bk", "L2_gnn_Wv",
          "L2_gnn_bv", "L2_gnn_ek_tab", "L2_gnn_ev_tab", "L2_gnn_es_tab", "L2_gnn_eg_tab", "L2_gnn_Wo", "L2_gnn_bo",
          "L2_gnn_ln1_g", "L2_gnn_ln1_b", "L2_gnn_W1", "L2_gnn_b1", "L2_gnn_W2", "L2_gnn_b2", "L2_gnn_ln2_g",
          "L2_gnn_ln2_b", "L2_gnn_Wf", "L2_gnn_bf", "L3_gnn_t"]


def host_layout(inputs):
    a = {k: np.ascontiguousarray(np.asarray(inputs[k])) for k in INPUTS}
    pad = EP - EDGES
    o = {k: v for k, v in a.items() if k not in ("x", "src", "dst", "edge_type_8", "edge_weight", "L1_gnn_W")}
    o["L1_gnn_WT"] = np.ascontiguousarray(a["L1_gnn_W"].T)
    o["x"] = np.concatenate([a["x"], np.zeros((NP - NODES, C), np.float32)])
    psrc = (NODES + np.arange(pad) % 128).astype(np.int32)
    pdst = np.full(pad, NP - 1, np.int32)
    o["src"] = np.concatenate([a["src"], psrc])
    one = np.full(1, -1, np.int32)
    o["dst_ext"] = np.concatenate([one, a["dst"], pdst, one, one, one])
    o["etype"] = np.concatenate([a["edge_type_8"], np.zeros(pad, np.int32)])
    o["weight"] = np.concatenate([a["edge_weight"], np.zeros(pad, np.float32)])
    o["c_before"] = np.triu(np.ones((P, P), np.float32), 1)
    o["c_iota256"] = np.broadcast_to(np.arange(DIGITS, dtype=np.float32), (P, DIGITS)).copy()
    o["c_ratios"] = np.broadcast_to(np.array(step_ratios(), np.float32), (P, STEPS)).copy()
    row = (np.arange(P)[:, None] * J + np.arange(J)[None, :]).astype(np.float32)
    o["c_pos0"] = (np.arange(P)[:, None] * J + np.arange(-1, J + 1)[None, :]).astype(np.float32)
    o["c_node_spare"] = row + np.float32(NP)
    o["c_list_spare"] = row + np.float32(LIST_SPARE)
    o["c_ident"] = np.eye(P, dtype=np.float32)
    o["c_ones"] = np.ones((1, P), np.float32)
    o["c_iota8"] = np.broadcast_to(np.arange(NET, dtype=np.float32), (P, J, NET)).copy()
    head = np.arange(C) // HD
    o["c_head_sum"] = np.where(head[:, None] == np.concatenate([head, np.arange(NH)])[None, :], HD ** -0.5, 0.0).astype(np.float32)
    return o


def program(nc, dram, out):
    net = Net()
    net.dram = dram
    net.x_in, net.src, net.dst_ext, net.etype, net.out = dram["x"], dram["src"], dram["dst_ext"], dram["etype"], out

    def table(name, rows, cols, dt=F32):
        return nc.dram_tensor(name, [rows, cols], dt, kind="Internal").ap()
    net.h0 = table("h0", NP, C)
    net.h1d = table("h1d", NP, C + 1)
    net.h2 = table("h2", NP, C)
    net.x1 = table("x1", NP, C)
    net.x2 = table("x2", NP, C)
    net.agg0 = table("agg0", NP, C + 1)
    net.agg1 = table("agg1", NP, C)
    net.agg2 = table("agg2", NP, C)
    net.term = [table(f"term{p}", NP + SPARE, C + 1) for p in range(2)]
    net.half_sorted = table("half_sorted", EP, 4, I32)
    net.lists = [table(f"list{p}", LIST_ROWS, 4, I32) for p in range(2)]
    with ExitStack() as ctx:
        allocate(nc, ctx, net)
        prepare(nc, net)
        sort_by_source(nc, net)
        first_norm(nc, net)
        for layer in range(3):
            edge_sums(nc, net, layer)
            node_update(nc, net, layer)
        diffuse(nc, net)


def kernel(**inputs):
    import concourse.bacc as bacc
    from concourse.bass_utils import run_bass_kernel_spmd
    nc = bacc.Bacc("TRN2", target_bir_lowering=False, num_devices=1)
    arrays = {f"in_{k}": v for k, v in host_layout(inputs).items()}
    dram = {k[3:]: nc.dram_tensor(k, v.shape, mybir.dt.from_np(v.dtype), kind="ExternalInput").ap() for k, v in arrays.items()}
    out = nc.dram_tensor("out", [NP + SPARE, C], F32, kind="ExternalOutput").ap()
    program(nc, dram, out)
    r = run_bass_kernel_spmd(nc, [arrays], core_ids=[0])
    return r.results[0]["out"][:NODES]
```

```python
import numpy as np
import concourse.bass as bass
from concourse import mybir
from contextlib import ExitStack

F32 = mybir.dt.float32
BF16 = mybir.dt.bfloat16
I32 = mybir.dt.int32
ALU = mybir.AluOpType
ACT = mybir.ActivationFunctionType
AX = mybir.AxisListType

P = 128
NODES, EDGES, C = 50000, 25000, 64
NH, HD, NET, FF = 4, 16, 8, 128
G = 28
J = 4
SUPER = -(-NODES // (P * G))
NP = SUPER * P * G
SUBS = G // J
CH = P * J
CHUNKS = 2 * -(-EDGES // (2 * CH))
EP = CHUNKS * CH
EPS = 1e-5
FAR = 1 << 17
NEG = -1e30
CV = C + NH
N_SUB, M_TERMS = 4, 20
STEPS = N_SUB * M_TERMS
SPARE = 2 * CH


def step_ratios():
    once = [1] * (M_TERMS + 1)
    for j in range(M_TERMS, 0, -1):
        once[j - 1] = once[j] * j
    poly = [1]
    for _ in range(N_SUB):
        new = [0] * (len(poly) + M_TERMS)
        for a, x in enumerate(poly):
            for b, y in enumerate(once):
                new[a + b] += x * y
        poly = new
    return [poly[k] / poly[k - 1] for k in range(1, len(poly))]


class Net:
    pass


def stage_semaphore(nc, ctx, name):
    s = nc.alloc_semaphore(name)
    ctx.callback(nc.clear_and_free_semaphores, [s])
    return s


def allocate(nc, ctx, net):
    def sb(name, shape, dt=F32):
        return ctx.enter_context(nc.sbuf_tensor(name, shape, dt))
    net.ident = sb("ident", [P, P])
    net.identb = sb("identb", [P, P], BF16)
    net.negidentb = sb("negidentb", [P, P], BF16)
    net.ones = sb("ones", [1, P])
    net.eps = sb("eps", [P, 1])
    net.iota8 = sb("iota8", [P, J, 3 * NET])
    net.w_msg = sb("w_msg", [P, C])
    net.b_msg = sb("b_msg", [C, 1])
    net.w_upd = sb("w_upd", [P, C])
    net.w_lin = sb("w_lin", [P, P])
    net.wq = sb("wq", [P, C])
    net.wk = sb("wk", [C, C])
    net.wv = sb("wv", [C, CV])
    net.bq = sb("bq", [C, 1])
    net.tabs = sb("tabs", [3 * NET, C + 2 * CV], BF16)
    net.tab_k, net.tab_v, net.tab_l = net.tabs[:, 0:C], net.tabs[:, C:C + CV], net.tabs[:, C + CV:C + 2 * CV]
    net.head_sum = sb("head_sum", [C, CV])
    net.w_out = sb("w_out", [P, P])
    net.w1 = sb("w1", [P, FF])
    net.b1 = sb("b1", [FF, 1])
    net.w2 = sb("w2", [FF, C])
    net.norms = sb("norms", [P, 4, C])
    net.bias_parts = sb("bias_parts", [3, 4, J, C], BF16)
    net.ones3 = sb("ones3", [3, P], BF16)


def prepare(nc, net):
    d = net.dram
    with ExitStack() as ctx:
        ctx.callback(nc.all_engine_barrier)
        def sb(name, shape, dt=F32):
            return ctx.enter_context(nc.sbuf_tensor(name, shape, dt))

        def sem(name):
            return stage_semaphore(nc, ctx, name)
        task = sb("task", [C, 1])
        wf = sb("wf", [C, 2 * C])
        bf_row = sb("bf_row", [1, 2 * C])
        bo_row = sb("bo_row", [1, C])
        wo = sb("wo", [P, C])
        g1 = sb("g1", [P, 1])
        a1 = sb("a1", [C, 1])
        a1_row = sb("a1_row", [1, C])
        rows = sb("rows", [1, 4, C])
        rest = sb("rest", [1, 4, C])
        parts = [sb(f"part{i}", [1, 4, C], BF16) for i in range(3)]
        repeated = [sb(f"repeated{i}", [1, 4, J, C], BF16) for i in range(3)]
        ek = sb("ek", [NET, C])
        bk = sb("bk", [NET, C])
        ev = sb("ev", [NET, C])
        bv = sb("bv", [NET, C])
        es = sb("es", [NET, NH])
        eg = sb("eg", [NET, NH])
        leg = sb("leg", [NET, NH])
        types = sb("types", [NET, C + 2 * CV])
        type_rest = sb("type_rest", [NET, C + 2 * CV])
        type_parts = [sb(f"type_part{i}", [NET, C + 2 * CV], BF16) for i in range(3)]
        gb = sb("gb", [1, 2 * C])
        gate = sb("gate", [1, C])
        gated = sb("gated", [1, C])
        ps = ctx.enter_context(nc.psum_tensor("ps_gate", [P, 512], F32))
        ps2 = ctx.enter_context(nc.psum_tensor("ps_gate2", [P, 512], F32))
        ps3 = ctx.enter_context(nc.psum_tensor("ps_up_bias", [P, 512], F32))
        loaded = sem("weights_loaded")
        parts_ready = sem("parts_ready")
        parts_placed = sem("parts_placed")
        corners_clear = sem("corners_clear")
        film_done = sem("film_done")
        up_bias_done = sem("up_bias_done")
        gb_ready = sem("gb_ready")
        tanh_done = sem("tanh_done")
        gate_ready = sem("gate_ready")
        spread_done = sem("spread_done")
        log_done = sem("log_done")
        with nc.Block() as block:
            loads = [
                (net.ident[:, :], d["c_ident"][:, :]), (net.ones[:, :], d["c_ones"][:, :]),
                (net.iota8[:, :, :], d["c_iota8"][:, :, :]), (net.head_sum[:, :], d["c_head_sum"][:, :]),
                (net.w_msg[:, :], d["L0_gnn_W_msg"][:, :]), (net.b_msg[:, :], d["L0_gnn_b_msg"][:, None]),
                (net.w_upd[:, :], d["L0_gnn_W_upd"][:, :]), (rows[:, 0, :], d["L0_gnn_b_upd"][None, :]),
                (net.w_lin[0:C, 0:C], d["L1_gnn_WT"][:, :]), (net.w_lin[C:P, C:P], d["L1_gnn_WT"][:, :]),
                (rows[:, 1, :], d["L1_gnn_b"][None, :]),
                (net.wq[C:, :], d["L2_gnn_Wq"][:, :]), (net.wk[:, :], d["L2_gnn_Wk"][:, :]),
                (net.wv[:, 0:C], d["L2_gnn_Wv"][:, :]),
                (net.bq[:, :], d["L2_gnn_bq"][:, None]),
                (bk[:, :], d["L2_gnn_bk"][None, :].to_broadcast([NET, C])),
                (bv[:, :], d["L2_gnn_bv"][None, :].to_broadcast([NET, C])),
                (ek[:, :], d["L2_gnn_ek_tab"][:, :]), (ev[:, :], d["L2_gnn_ev_tab"][:, :]),
                (es[:, :], d["L2_gnn_es_tab"][:, :]), (eg[:, :], d["L2_gnn_eg_tab"][:, :]),
                (task[:, :], d["L2_gnn_task_embedding"][:, None]), (wf[:, :], d["L2_gnn_Wf"][:, :]),
                (bf_row[:, :], d["L2_gnn_bf"][None, :]), (bo_row[:, :], d["L2_gnn_bo"][None, :]),
                (wo[0:C, :], d["L2_gnn_Wo"][:, :]), (wo[C:P, :], d["L2_gnn_Wo"][:, :]),
                (net.w1[0:C, :], d["L2_gnn_W1"][:, :]), (net.w1[C:P, :], d["L2_gnn_W1"][:, :]),
                (g1[0:C, :], d["L2_gnn_ln1_g"][:, None]), (g1[C:P, :], d["L2_gnn_ln1_g"][:, None]),
                (a1[:, :], d["L2_gnn_ln1_b"][:, None]), (a1_row[:, :], d["L2_gnn_ln1_b"][None, :]),
                (net.b1[:, :], d["L2_gnn_b1"][:, None]),
                (net.w2[:, :], d["L2_gnn_W2"][:, :]), (rows[:, 3, :], d["L2_gnn_b2"][None, :]),
                (net.norms[:, 0, :], d["L2_gnn_ln1_g"][None, :].to_broadcast([P, C])),
                (net.norms[:, 1, :], d["L2_gnn_ln1_b"][None, :].to_broadcast([P, C])),
                (net.norms[:, 2, :], d["L2_gnn_ln2_g"][None, :].to_broadcast([P, C])),
                (net.norms[:, 3, :], d["L2_gnn_ln2_b"][None, :].to_broadcast([P, C])),
            ]
            all_loaded = 16 * len(loads)

            @block.sync
            def _(sp):
                sp.wait_ge(corners_clear, 1)
                for dst, src in loads:
                    sp.dma_start(dst, src).then_inc(loaded, 16)
                sp.wait_ge(parts_ready, 1)
                for i in range(3):
                    sp.dma_start(net.bias_parts[i:i + 1, :, :, :], repeated[i][:, :, :, :]).then_inc(parts_placed, 16)
                    sp.dma_start(net.tabs[i * NET:(i + 1) * NET, :], type_parts[i][:, :]).then_inc(parts_placed, 16)
                sp.wait_ge(parts_placed, 6 * 16)

            @block.tensor
            def _(pe):
                pe.wait_ge(loaded, all_loaded)
                nc.tensor.matmul(ps[0:1, 0:2 * C], task[:, :], wf[:, :], start=True, stop=True).then_inc(film_done, 1)
                nc.tensor.matmul(ps3[:, 0:1], net.w1[0:C, :], a1[:, :], start=True, stop=True).then_inc(up_bias_done, 1)
                pe.wait_ge(gate_ready, 1)
                nc.tensor.matmul(ps2[:, 0:C], net.ones[:, :], gate[:, :], start=True, stop=True).then_inc(spread_done, 1)

            @block.scalar
            def _(act):
                act.wait_ge(gb_ready, 1)
                nc.scalar.activation(gate[:, :], gb[:, 0:C], ACT.Tanh).then_inc(tanh_done, 1)
                act.wait_ge(loaded, all_loaded)
                nc.scalar.activation(leg[:, :], eg[:, :], ACT.Ln).then_inc(log_done, 1)

            @block.vector
            def _(v):
                nc.vector.memset(net.w_lin[:, :], 0.0)
                nc.vector.memset(net.w_out[:, :], 0.0)
                nc.vector.memset(net.ones3[:, :], 1.0)
                v.drain()
                v.sem_inc(corners_clear, 1)
                v.wait_ge(loaded, all_loaded)
                nc.vector.tensor_copy(net.identb[:, :], net.ident[:, :])
                nc.vector.tensor_scalar(net.negidentb[:, :], net.ident[:, :], NEG, None, ALU.mult)
                nc.vector.memset(net.wv[:, C:CV], 0.0)
                nc.vector.memset(net.eps[:, :], EPS)
                nc.vector.memset(types[:, 2 * C:C + CV], 1.0)
                nc.vector.tensor_tensor(types[:, 0:C], ek[:, :], bk[:, :], ALU.add)
                nc.vector.tensor_tensor(types[:, C:2 * C], ev[:, :], bv[:, :], ALU.add)
                v.wait_ge(film_done, 1)
                nc.vector.tensor_tensor(gb[:, :], ps[0:1, 0:2 * C], bf_row[:, :], ALU.add).then_inc(gb_ready, 1)
                v.wait_ge(tanh_done, 1)
                nc.vector.tensor_scalar(gate[:, :], gate[:, :], 0.5, 1.0, ALU.mult, ALU.add).then_inc(gate_ready, 1)
                v.drain()
                nc.vector.tensor_tensor(gated[:, :], bo_row[:, :], gate[:, :], ALU.mult)
                v.drain()
                nc.vector.tensor_tensor(rows[:, 2, :], gated[:, :], gb[:, C:2 * C], ALU.add)
                nc.vector.tensor_tensor(rows[:, 3, :], rows[:, 3, :], a1_row[:, :], ALU.add)
                v.wait_ge(up_bias_done, 1)
                nc.vector.tensor_tensor(net.b1[:, :], net.b1[:, :], ps3[:, 0:1], ALU.add)
                nc.vector.tensor_scalar(net.w1[:, :], net.w1[:, :], g1[:, :], None, ALU.mult)
                v.wait_ge(spread_done, 1)
                for half in (slice(0, C), slice(C, P)):
                    nc.vector.tensor_tensor(net.w_out[half, half], wo[half, :], ps2[half, 0:C], ALU.mult)
                left = rows
                for i in range(3):
                    v.drain()
                    nc.vector.tensor_copy(parts[i][:, :, :], left[:, :, :])
                    v.drain()
                    nc.vector.tensor_copy(repeated[i][:, :, :, :], parts[i][:, :, :].unsqueeze(2).to_broadcast([1, 4, J, C]))
                    nc.vector.tensor_tensor(rest[:, :, :], left[:, :, :], parts[i][:, :, :], ALU.subtract)
                    left = rest
                v.wait_ge(log_done, 1)
                nc.vector.tensor_scalar(leg[:, :], leg[:, :], -10.0, 10.0, ALU.max, ALU.min)
                v.drain()
                nc.vector.tensor_tensor(es[:, :], es[:, :], leg[:, :], ALU.add)
                v.drain()
                nc.vector.tensor_copy(types[:, C + CV:2 * C + CV].rearrange("e (h d) -> e h d", d=HD),
                                      es[:, :].unsqueeze(2).to_broadcast([NET, NH, HD]))
                nc.vector.tensor_copy(types[:, 2 * C + CV:], es[:, :])
                left = types
                for i in range(3):
                    v.drain()
                    nc.vector.tensor_copy(type_parts[i][:, :], left[:, :])
                    v.drain()
                    nc.vector.tensor_tensor(type_rest[:, :], left[:, :], type_parts[i][:, :], ALU.subtract)
                    left = type_rest
                v.drain()
                v.sem_inc(parts_ready, 1)


def rows_of(table, chunk, rows):
    return table[bass.ds(chunk * (P * rows), P * rows), :].rearrange("(p g) c -> p g c", p=P)


def first_norm(nc, net):
    with ExitStack() as ctx:
        ctx.callback(nc.all_engine_barrier)
        def sb(name, shape, dt=F32):
            return ctx.enter_context(nc.sbuf_tensor(name, shape, dt))

        def sem(name):
            return stage_semaphore(nc, ctx, name)
        X = [sb(f"n_x{s}", [P, G, C]) for s in range(2)]
        XC = [sb(f"n_xc{s}", [P, G, C]) for s in range(2)]
        SQ = [sb(f"n_sq{s}", [P, G, C]) for s in range(2)]
        H = [sb(f"n_h{s}", [P, G, C]) for s in range(2)]
        mean = [sb(f"n_mean{s}", [P, G]) for s in range(2)]
        rstd = [sb(f"n_rstd{s}", [P, G]) for s in range(2)]
        loaded = [sem(f"n_loaded{s}") for s in range(2)]
        stored = [sem(f"n_stored{s}") for s in range(2)]
        centred, squared, var_ready, rstd_ready, normed = (
            sem(f"n_{x}") for x in ("centred", "squared", "var_ready", "rstd_ready", "normed"))
        with nc.Block() as block:
            @block.sync
            def _(sp):
                for s in range(2):
                    sp.dma_start(X[s][:, :, :], rows_of(net.x_in, s, G)).then_inc(loaded[s], 16)
                with sp.Fori(1, SUPER // 2) as t:
                    for s in range(2):
                        sp.wait_ge(centred, 2 * t + s - 1)
                        sp.dma_start(X[s][:, :, :], rows_of(net.x_in, 2 * t + s, G)).then_inc(loaded[s], 16)

            @block.vector
            def _(v):
                with v.Fori(0, SUPER // 2) as t:
                    for s in range(2):
                        v.wait_ge(loaded[s], 16 * t + 16)
                        nc.vector.tensor_reduce(mean[s][:, :], X[s][:, :, :], AX.X, ALU.add)
                        v.drain()
                        nc.vector.tensor_scalar(mean[s][:, :], mean[s][:, :], 1.0 / C, None, ALU.mult)
                        v.drain()
                        nc.vector.tensor_tensor(XC[s][:, :, :], X[s][:, :, :],
                                                mean[s][:, :].unsqueeze(2).to_broadcast([P, G, C]),
                                                ALU.subtract).then_inc(centred, 1)
                    for s in range(2):
                        v.wait_ge(squared, 2 * t + s + 1)
                        nc.vector.tensor_reduce(rstd[s][:, :], SQ[s][:, :, :], AX.X, ALU.add).then_inc(var_ready, 1)
                    for s in range(2):
                        v.wait_ge(rstd_ready, 2 * t + s + 1)
                        nc.vector.reciprocal(rstd[s][:, :], rstd[s][:, :])
                        v.drain()
                        v.wait_ge(stored[s], 16 * t)
                        nc.vector.scalar_tensor_tensor(H[s][:, :, :], XC[s][:, :, :], 0.0,
                                                       rstd[s][:, :].unsqueeze(2).to_broadcast([P, G, C]),
                                                       ALU.max, ALU.mult).then_inc(normed, 1)

            @block.scalar
            def _(act):
                with act.Fori(0, SUPER // 2) as t:
                    for s in range(2):
                        act.wait_ge(centred, 2 * t + s + 1)
                        nc.scalar.activation(SQ[s][:, :, :], XC[s][:, :, :], ACT.Square, scale=C ** -0.5).then_inc(squared, 1)
                    for s in range(2):
                        act.wait_ge(var_ready, 2 * t + s + 1)
                        nc.scalar.activation(rstd[s][:, :], rstd[s][:, :], ACT.Sqrt, bias=net.eps[:, :]).then_inc(rstd_ready, 1)
                    for s in range(2):
                        act.wait_ge(normed, 2 * t + s + 1)
                        act.dma_start(rows_of(net.h0, 2 * t + s, G), H[s][:, :, :]).then_inc(stored[s], 16)
                for s in range(2):
                    act.wait_ge(stored[s], 16 * (SUPER // 2))


def edge_sums(nc, net, layer):
    two = layer == 0
    table = (net.h0, net.h1d)[layer]
    agg = (net.agg0, net.agg1)[layer]
    wide = C + 1 if layer == 1 else C
    rows = (C + 1, C)[layer]
    outw = (C + 1, C)[layer]
    n_gather = 8 if two else 4
    n = f"e{layer}_"
    with ExitStack() as ctx:
        ctx.callback(nc.all_engine_barrier)
        def sb(name, shape, dt=F32):
            return ctx.enter_context(nc.sbuf_tensor(n + name, shape, dt))

        def ps(name):
            return ctx.enter_context(nc.psum_tensor(n + name, [P, 512], F32))

        def sem(name):
            return stage_semaphore(nc, ctx, n + name)
        src = [sb(f"src{s}", [P, J], I32) for s in range(2)]
        dst = [sb(f"dst{s}", [P, J + 2], I32) for s in range(2)]
        keep = [sb(f"keep{s}", [P, J], BF16) for s in range(2)]
        same = [sb(f"same{s}", [P, J]) for s in range(2)]
        end = [sb(f"end{s}", [P, J], I32) for s in range(2)]
        ends = [sb(f"ends{s}", [P, J, 2 * wide if two else wide]) for s in range(2)]
        out = [sb(f"out{s}", [P, J, outw]) for s in range(2)]
        scan = [sb(f"scan{s}", [rows, CH]) for s in range(2)]
        feat = sb("feat", [P if two else C, CH])
        msg = sb("msg", [rows, CH])
        y = sb("y", [P, J, C])
        pt = ps("pt")
        pk = ps("pk")
        pm = ps("pm")
        pr = ps("pr")
        loaded = [sem(f"loaded{s}") for s in range(2)]
        gathered = [sem(f"gathered{s}") for s in range(2)]
        scattered = [sem(f"scattered{s}") for s in range(2)]
        names = ("flags", "y_ready", "turned", "kept", "feat_ready", "msg_mm", "msg_ready", "scanned", "back", "out_ready",
                 "pool_turn", "pe_turn")
        (flags, y_ready, turned, kept, feat_ready, msg_mm, msg_ready, scanned, back, out_ready, pool_turn,
         pe_turn) = map(sem, names)

        def dst_rows(c):
            first = net.dst_ext[bass.ds(c * CH, CH)].rearrange("(p j) -> p j", j=J)
            last = net.dst_ext[bass.ds(c * CH + J, CH)].rearrange("(p j) -> p j", j=J)
            return first, last[:, 0:2]

        n_loads = 3
        with nc.Block() as block:
            @block.sync
            def _(sp):
                def load(c, s):
                    first, last = dst_rows(c)
                    sp.dma_start(src[s][:, :], net.src[bass.ds(c * CH, CH)].rearrange("(p j) -> p j", j=J)).then_inc(loaded[s], 16)
                    sp.dma_start(dst[s][:, 0:J], first).then_inc(loaded[s], 16)
                    sp.dma_start(dst[s][:, J:J + 2], last).then_inc(loaded[s], 16)
                for s in range(2):
                    load(s, s)
                with sp.Fori(1, CHUNKS // 2) as t:
                    for s in range(2):
                        sp.wait_ge(gathered[s], 16 * n_gather * t)
                        sp.wait_ge(flags, 2 * t + s - 1)
                        load(2 * t + s, s)

            @block.gpsimd
            def _(pool):
                def gather(t, s):
                    pool.wait_ge(loaded[s], 16 * n_loads * (t + 1))
                    pool.wait_ge(turned if two else y_ready, 2 * t + s + 1)
                    pool.sem_inc(pool_turn, 1)
                    for j in range(J):
                        pool.indirect_dma_start(ends[s][:, j, 0:wide], None, table[:, :],
                                                bass.IndirectOffsetOnAxis(ap=src[s][:, j:j + 1], axis=0)).then_inc(gathered[s], 16)
                        if two:
                            pool.indirect_dma_start(ends[s][:, j, wide:2 * wide], None, table[:, :],
                                                    bass.IndirectOffsetOnAxis(ap=dst[s][:, 1 + j:2 + j], axis=0)).then_inc(gathered[s], 16)

                def scatter(t, s):
                    pool.wait_ge(out_ready, 2 * t + s + 1)
                    pool.sem_inc(pool_turn, 1)
                    for j in range(J):
                        pool.indirect_dma_start(agg[:, :], bass.IndirectOffsetOnAxis(ap=end[s][:, j:j + 1], axis=0),
                                                out[s][:, j, :], None, bounds_check=NP - 1, oob_is_err=False).then_inc(scattered[s], 16)
                for s in range(2):
                    gather(0, s)
                with pool.Fori(0, CHUNKS // 2 - 1) as t:
                    for s in range(2):
                        gather(t + 1, s)
                        scatter(t, s)
                for s in range(2):
                    scatter(CHUNKS // 2 - 1, s)
                for s in range(2):
                    pool.wait_ge(scattered[s], 16 * J * (CHUNKS // 2))

            @block.vector
            def _(v):
                nc.vector.memset(scan[1][:, :], 0.0)
                if layer == 0:
                    nc.vector.memset(msg[C:C + 1, :], 1.0)
                if layer == 1:
                    for _ in range(2):
                        v.sem_inc(y_ready, 1)
                v.drain()

                def make_flags(t, s):
                    v.wait_ge(loaded[s], 16 * n_loads * (t + 1))
                    v.wait_ge(scattered[s], 16 * J * t)
                    nc.vector.tensor_tensor(keep[s][:, :], dst[s][:, 1:J + 1], dst[s][:, 0:J], ALU.is_equal)
                    nc.vector.tensor_tensor(same[s][:, :], dst[s][:, 1:J + 1], dst[s][:, 2:J + 2], ALU.is_equal)
                    v.drain()
                    nc.vector.scalar_tensor_tensor(end[s][:, :], same[s][:, :], float(FAR), dst[s][:, 1:J + 1],
                                                   ALU.mult, ALU.add).then_inc(flags, 1)

                def sums(t, s):
                    k = 2 * t + s + 1
                    if layer == 1:
                        v.wait_ge(gathered[s], 16 * n_gather * (t + 1))
                        v.wait_ge(turned, k - 1)
                        nc.vector.tensor_tensor(y[:, :, :], ends[s][:, :, 0:C],
                                                ends[s][:, :, C:C + 1].to_broadcast([P, J, C]), ALU.mult).then_inc(y_ready, 1)
                    v.wait_ge(msg_ready, k)
                    v.wait_ge(kept, k)
                    nc.vector.tensor_tensor_scan(scan[s][:, :], pk[0:rows, :], msg[:, :], scan[1 - s][:, CH - 1:CH],
                                                 ALU.mult, ALU.add).then_inc(scanned, 1)
                    v.wait_ge(back, k)
                    sums_rows = pr[:, 0:J * rows].rearrange("p (j c) -> p j c", c=rows)
                    nc.vector.tensor_copy(out[s][:, :, :], sums_rows).then_inc(out_ready, 1)

                with v.Fori(0, CHUNKS // 2) as t:
                    for s in range(2):
                        make_flags(t, s)
                        sums(t, s)

            @block.tensor
            def _(pe):
                if two:
                    for _ in range(2):
                        pe.sem_inc(turned, 1)
                with pe.Fori(0, CHUNKS // 2) as t:
                    for s in range(2):
                        k = 2 * t + s + 1
                        if two:
                            pe.wait_ge(gathered[s], 16 * n_gather * (t + 1))
                            pe.wait_ge(feat_ready, k - 1)
                            pe.sem_inc(pe_turn, 1)
                            for j in range(J):
                                last = nc.tensor.transpose(pt[:, j:CH:J], ends[s][:, j, :], net.ident[:, :])
                        else:
                            pe.wait_ge(y_ready, k + 2)
                            pe.wait_ge(feat_ready, k - 1)
                            pe.sem_inc(pe_turn, 1)
                            for j in range(J):
                                last = nc.tensor.transpose(pt[0:C, j:CH:J], y[:, j, :], net.ident[:, :])
                        last.then_inc(turned, 1)
                        pe.wait_ge(flags, k)
                        pe.wait_ge(scanned, k - 1)
                        for j in range(J):
                            last = nc.tensor.matmul(pk[0:rows, j:CH:J], keep[s][:, j:j + 1].to_broadcast([P, rows]),
                                                    net.identb[:, :], start=True, stop=True)
                        last.then_inc(kept, 1)
                        if layer == 0:
                            pe.wait_ge(feat_ready, k)
                            nc.tensor.matmul(pm[0:C, :], net.w_msg[:, :], feat[:, :], start=True, stop=True).then_inc(msg_mm, 1)
                        pe.wait_ge(scanned, k)
                        pe.wait_ge(out_ready, k - 1)
                        pe.sem_inc(pe_turn, 1)
                        for j in range(J):
                            last = nc.tensor.transpose(pr[:, j * rows:(j + 1) * rows], scan[s][:, j:CH:J], net.ident[0:rows, 0:rows])
                        last.then_inc(back, 1)

            @block.scalar
            def _(act):
                with act.Fori(0, CHUNKS // 2) as t:
                    for s in range(2):
                        k = 2 * t + s + 1
                        if layer == 0:
                            act.wait_ge(turned, k + 2)
                            nc.scalar.activation(feat[:, :], pt[:, :], ACT.Copy).then_inc(feat_ready, 1)
                            act.wait_ge(msg_mm, k)
                            act.wait_ge(scanned, k - 1)
                            nc.scalar.activation(msg[0:C, :], pm[0:C, :], ACT.Relu, bias=net.b_msg[:, :]).then_inc(msg_ready, 1)
                        else:
                            act.wait_ge(turned, k)
                            act.wait_ge(scanned, k - 1)
                            nc.scalar.activation(msg[:, :], pt[0:C, :], ACT.Copy)
                            act.drain()
                            act.sem_inc(feat_ready, 1)
                            act.sem_inc(msg_ready, 1)


def attention_sums(nc, net):
    with ExitStack() as ctx:
        ctx.callback(nc.all_engine_barrier)
        def sb(name, shape, dt=F32):
            return ctx.enter_context(nc.sbuf_tensor("a_" + name, shape, dt))

        def ps(name):
            return ctx.enter_context(nc.psum_tensor("a_" + name, [P, 512], F32))

        def sem(name):
            return stage_semaphore(nc, ctx, "a_" + name)
        T3 = 3 * NET
        LAST = CHUNKS // 2 - 1
        src = [sb(f"src{s}", [P, J], I32) for s in range(2)]
        dst = [sb(f"dst{s}", [P, J + 2], I32) for s in range(2)]
        etype = [sb(f"etype{s}", [P, J], I32) for s in range(2)]
        fresh = [sb(f"fresh{s}", [P, J], BF16) for s in range(2)]
        same = sb("same", [P, J])
        end = [sb(f"end{s}", [P, J], I32) for s in range(2)]
        ends = [sb(f"ends{s}", [P, J, 2 * C]) for s in range(2)]
        out = [sb(f"out{s}", [P, J, C]) for s in range(2)]
        onehot = sb("onehot", [P, J, T3], BF16)
        oht = sb("oht", [T3, CH], BF16)
        feat = sb("feat", [P, CH])
        qs = sb("qs", [C, CH])
        prod = sb("prod", [C, CH])
        mx = [sb(f"mx{s}", [CV, CH + 1]) for s in range(2)]
        lm = sb("lm", [CV, CH])
        dm = sb("dm", [CV, CH])
        pexp = sb("pexp", [CV, CH])
        rexp = sb("rexp", [CV, CH])
        negs = sb("negs", [CV, CH])
        msg = sb("msg", [CV, CH])
        scan = [sb(f"scan{s}", [CV, CH]) for s in range(2)]
        dsum = sb("dsum", [P, J, NH])
        pt, po, pg, pq, pk, pv, pl, pr = map(ps, (
            "features", "types", "starts", "queries", "keys", "values", "logit", "sums"))
        loaded = [sem(f"loaded{s}") for s in range(2)]
        gathered = [sem(f"gathered{s}") for s in range(2)]
        scattered = [sem(f"scattered{s}") for s in range(2)]
        names = ("flags", "turned", "feat_ready", "onehot_ready", "types_turned", "oht_ready", "projected", "qs_ready",
                 "prod_ready", "starts_spread", "values_done", "logits", "lm_ready", "dm_ready", "p_ready", "r_ready",
                 "msg_done", "scanned", "back", "out_ready", "pool_turn", "pe_turn")
        (flags, turned, feat_ready, onehot_ready, types_turned, oht_ready, projected, qs_ready,
         prod_ready, starts_spread, values_done, logits, lm_ready, dm_ready, p_ready, r_ready,
         msg_done, scanned, back, out_ready, pool_turn, pe_turn) = map(sem, names)

        def rows_4(column, c):
            return column[bass.ds(c * CH, CH)].rearrange("(p j) -> p j", j=J)

        with nc.Block() as block:
            @block.sync
            def _(sp):
                def load(c, s):
                    sp.dma_start(src[s][:, :], rows_4(net.src, c)).then_inc(loaded[s], 16)
                    sp.dma_start(dst[s][:, 0:J], rows_4(net.dst_ext, c)).then_inc(loaded[s], 16)
                    after = net.dst_ext[bass.ds(c * CH + J, CH)].rearrange("(p j) -> p j", j=J)
                    sp.dma_start(dst[s][:, J:J + 2], after[:, 0:2]).then_inc(loaded[s], 16)
                    sp.dma_start(etype[s][:, :], rows_4(net.etype, c)).then_inc(loaded[s], 16)
                for s in range(2):
                    load(s, s)
                with sp.Fori(1, CHUNKS // 2) as t:
                    for s in range(2):
                        sp.wait_ge(gathered[s], 16 * 2 * J * t)
                        sp.wait_ge(flags, 2 * t + s - 1)
                        sp.wait_ge(onehot_ready, 2 * t + s - 1)
                        load(2 * t + s, s)

            @block.gpsimd
            def _(pool):
                def gather(t, s):
                    pool.wait_ge(loaded[s], 16 * 4 * (t + 1))
                    pool.wait_ge(turned, 2 * t + s + 1)
                    pool.sem_inc(pool_turn, 1)
                    for j in range(J):
                        for half, rows in enumerate((src[s][:, j:j + 1], dst[s][:, 1 + j:2 + j])):
                            pool.indirect_dma_start(ends[s][:, j, half * C:(half + 1) * C], None, net.h2[:, :],
                                                    bass.IndirectOffsetOnAxis(ap=rows, axis=0)).then_inc(gathered[s], 16)

                def scatter(t, s):
                    pool.wait_ge(out_ready, 2 * t + s + 1)
                    pool.sem_inc(pool_turn, 1)
                    for j in range(J):
                        pool.indirect_dma_start(net.agg2[:, :], bass.IndirectOffsetOnAxis(ap=end[s][:, j:j + 1], axis=0),
                                                out[s][:, j, :], None, bounds_check=NP - 1, oob_is_err=False).then_inc(scattered[s], 16)
                for s in range(2):
                    gather(0, s)
                with pool.Fori(0, LAST) as t:
                    for s in range(2):
                        gather(t + 1, s)
                        scatter(t, s)
                for s in range(2):
                    scatter(LAST, s)
                for s in range(2):
                    pool.wait_ge(scattered[s], 16 * J * (CHUNKS // 2))

            @block.tensor
            def _(pe):
                def project(t, s):
                    k = 2 * t + s + 1
                    pe.wait_ge(gathered[s], 16 * 2 * J * (t + 1))
                    pe.wait_ge(feat_ready, k - 1)
                    pe.sem_inc(pe_turn, 1)
                    for j in range(J):
                        last = nc.tensor.transpose(pt[:, j:CH:J], ends[s][:, j, :], net.ident[:, :])
                    last.then_inc(turned, 1)
                    pe.wait_ge(onehot_ready, k)
                    pe.wait_ge(oht_ready, k - 1)
                    pe.sem_inc(pe_turn, 1)
                    for j in range(J):
                        last = nc.tensor.matmul(po[0:T3, j:CH:J], onehot[:, j, :], net.identb[:, :], start=True, stop=True)
                    last.then_inc(types_turned, 1)
                    pe.wait_ge(feat_ready, k)
                    pe.wait_ge(oht_ready, k)
                    pe.sem_inc(pe_turn, 1)
                    nc.tensor.matmul(pq[0:C, :], net.wq[C:P, :], feat[C:P, :], start=True, stop=True)
                    nc.tensor.matmul(pk[0:C, :], net.wk[:, :], feat[0:C, :], start=True, stop=False)
                    nc.tensor.matmul(pk[0:C, :], net.tab_k, oht[:, :], start=False, stop=True).then_inc(projected, 1)
                    pe.wait_ge(flags, k)
                    pe.wait_ge(msg_done, k - 1)
                    pe.sem_inc(pe_turn, 1)
                    for j in range(J):
                        last = nc.tensor.matmul(pg[0:CV, j:CH:J], fresh[s][:, j:j + 1].to_broadcast([P, CV]),
                                                net.negidentb[:, :], start=True, stop=True)
                    last.then_inc(starts_spread, 1)
                    nc.tensor.matmul(pv[0:CV, :], net.wv[:, :], feat[0:C, :], start=True, stop=False)
                    nc.tensor.matmul(pv[0:CV, :], net.tab_v, oht[:, :], start=False, stop=True).then_inc(values_done, 1)

                def logit(t, s):
                    k = 2 * t + s + 1
                    pe.wait_ge(prod_ready, k)
                    pe.wait_ge(lm_ready, k - 1)
                    pe.sem_inc(pe_turn, 1)
                    nc.tensor.matmul(pl[0:CV, :], net.head_sum[:, :], prod[:, :], start=True, stop=False)
                    nc.tensor.matmul(pl[0:CV, :], net.tab_l, oht[:, :], start=False, stop=True).then_inc(logits, 1)

                def turn_back(t, s):
                    k = 2 * t + s + 1
                    pe.wait_ge(scanned, k)
                    pe.wait_ge(out_ready, k - 1)
                    pe.sem_inc(pe_turn, 1)
                    for j in range(J):
                        last = nc.tensor.transpose(pr[:, j * CV:(j + 1) * CV], scan[s][:, j:CH:J], net.ident[0:CV, 0:CV])
                    last.then_inc(back, 1)
                for _ in range(2):
                    pe.sem_inc(turned, 1)
                project(0, 0)
                with pe.Fori(0, LAST) as t:
                    for s in range(2):
                        logit(t, s)
                        project(t + s, 1 - s)
                        turn_back(t, s)
                logit(LAST, 0)
                project(LAST, 1)
                turn_back(LAST, 0)
                logit(LAST, 1)
                turn_back(LAST, 1)

            @block.scalar
            def _(act):
                def copies(t, s):
                    k = 2 * t + s + 1
                    act.wait_ge(turned, k + 2)
                    act.wait_ge(values_done, k - 1)
                    nc.scalar.activation(feat[:, :], pt[:, :], ACT.Copy).then_inc(feat_ready, 1)
                    act.wait_ge(types_turned, k)
                    act.wait_ge(logits, k - 1)
                    nc.scalar.activation(oht[:, :], po[0:T3, :], ACT.Copy).then_inc(oht_ready, 1)

                def queries(t, s):
                    k = 2 * t + s + 1
                    act.wait_ge(projected, k)
                    act.wait_ge(prod_ready, k - 1)
                    nc.scalar.activation(qs[:, :], pq[0:C, :], ACT.Identity, bias=net.bq[:, :]).then_inc(qs_ready, 1)

                def exponentials(t, s):
                    k = 2 * t + s + 1
                    act.wait_ge(lm_ready, k)
                    nc.scalar.activation(pexp[:, :], lm[:, :], ACT.Exp).then_inc(p_ready, 1)
                    act.wait_ge(dm_ready, k)
                    nc.scalar.activation(rexp[:, :], dm[:, :], ACT.Exp).then_inc(r_ready, 1)

                copies(0, 0)
                queries(0, 0)
                with act.Fori(0, LAST) as t:
                    for s in range(2):
                        copies(t + s, 1 - s)
                        exponentials(t, s)
                        queries(t + s, 1 - s)
                copies(LAST, 1)
                exponentials(LAST, 0)
                queries(LAST, 1)
                exponentials(LAST, 1)

            @block.vector
            def _(v):
                def types(t, s):
                    k = 2 * t + s + 1
                    v.wait_ge(loaded[s], 16 * 4 * (t + 1))
                    v.wait_ge(types_turned, k - 1)
                    nc.vector.tensor_tensor(onehot[:, :, :], etype[s][:, :].unsqueeze(2).to_broadcast([P, J, T3]),
                                            net.iota8[:, :, :], ALU.is_equal).then_inc(onehot_ready, 1)

                def make_flags(t, s):
                    v.wait_ge(scattered[s], 16 * J * t)
                    nc.vector.tensor_tensor(fresh[s][:, :], dst[s][:, 1:J + 1], dst[s][:, 0:J], ALU.not_equal)
                    nc.vector.tensor_tensor(same[:, :], dst[s][:, 1:J + 1], dst[s][:, 2:J + 2], ALU.is_equal)
                    v.drain()
                    nc.vector.scalar_tensor_tensor(end[s][:, :], same[:, :], float(FAR), dst[s][:, 1:J + 1],
                                                   ALU.mult, ALU.add).then_inc(flags, 1)

                def products(t, s):
                    k = 2 * t + s + 1
                    v.wait_ge(qs_ready, k)
                    nc.vector.tensor_tensor(prod[:, :], qs[:, :], pk[0:C, :], ALU.mult).then_inc(prod_ready, 1)

                def softmax(t, s):
                    k = 2 * t + s + 1
                    v.wait_ge(starts_spread, k)
                    nc.vector.tensor_copy(negs[:, :], pg[0:CV, :])
                    nc.vector.tensor_copy(mx[s][:, 0:1], mx[1 - s][:, CH:CH + 1])
                    v.drain()
                    v.wait_ge(logits, k)
                    nc.vector.tensor_tensor_scan(mx[s][:, 1:CH + 1], negs[:, :], pl[0:CV, :], mx[1 - s][:, CH:CH + 1],
                                                 ALU.add, ALU.max)
                    v.drain()
                    nc.vector.tensor_tensor(lm[:, :], pl[0:CV, :], mx[s][:, 1:CH + 1], ALU.subtract).then_inc(lm_ready, 1)
                    nc.vector.tensor_tensor(dm[:, :], negs[:, :], mx[s][:, 0:CH], ALU.add)
                    v.drain()
                    nc.vector.tensor_tensor(dm[:, :], dm[:, :], mx[s][:, 1:CH + 1], ALU.subtract).then_inc(dm_ready, 1)

                def sums(t, s):
                    k = 2 * t + s + 1
                    v.wait_ge(p_ready, k)
                    v.wait_ge(values_done, k)
                    nc.vector.tensor_tensor(msg[:, :], pexp[:, :], pv[0:CV, :], ALU.mult).then_inc(msg_done, 1)
                    v.drain()
                    v.wait_ge(r_ready, k)
                    nc.vector.tensor_tensor_scan(scan[s][:, :], rexp[:, :], msg[:, :], scan[1 - s][:, CH - 1:CH],
                                                 ALU.mult, ALU.add).then_inc(scanned, 1)

                def divide(t, s):
                    k = 2 * t + s + 1
                    v.wait_ge(back, k)
                    sums_rows = pr[:, 0:J * CV].rearrange("p (j c) -> p j c", c=CV)
                    nc.vector.tensor_scalar(dsum[:, :, :], sums_rows[:, :, C:CV], 1e-12, None, ALU.max)
                    v.drain()
                    nc.vector.reciprocal(dsum[:, :, :], dsum[:, :, :])
                    v.drain()
                    for j in range(J):
                        last = nc.vector.tensor_tensor(
                            out[s][:, j, :].rearrange("p (h d) -> p h d", d=HD),
                            sums_rows[:, j, 0:C].rearrange("p (h d) -> p h d", d=HD),
                            dsum[:, j, :].unsqueeze(2).to_broadcast([P, NH, HD]), ALU.mult)
                    last.then_inc(out_ready, 1)

                nc.vector.memset(scan[1][:, :], 0.0)
                nc.vector.memset(mx[1][:, :], 0.0)
                types(0, 0)
                make_flags(0, 0)
                products(0, 0)
                with v.Fori(0, LAST) as t:
                    for s in range(2):
                        types(t + s, 1 - s)
                        softmax(t, s)
                        make_flags(t + s, 1 - s)
                        sums(t, s)
                        products(t + s, 1 - s)
                        divide(t, s)
                types(LAST, 1)
                softmax(LAST, 0)
                make_flags(LAST, 1)
                sums(LAST, 0)
                products(LAST, 1)
                divide(LAST, 0)
                softmax(LAST, 1)
                sums(LAST, 1)
                divide(LAST, 1)


def node_update(nc, net, layer):
    n = f"u{layer}_"
    TURNS = J if layer == 0 else J // 2
    aggw = C + 1 if layer == 0 else C
    hw = C + 1 if layer == 1 else C
    with ExitStack() as ctx:
        ctx.callback(nc.all_engine_barrier)
        def sb(name, shape, dt=F32):
            return ctx.enter_context(nc.sbuf_tensor(n + name, shape, dt))

        def ps(name):
            return ctx.enter_context(nc.psum_tensor(n + name, [P, 512], F32))

        def sem(name):
            return stage_semaphore(nc, ctx, n + name)
        X = [sb(f"x{s}", [P, G, C]) for s in range(2)]
        A = [sb(f"a{s}", [P, G, aggw]) for s in range(2)]
        Z = [sb(f"z{s}", [P, G, P if layer == 0 else hw]) for s in range(2)]
        T = [sb(f"t{s}", [P, G, C]) for s in range(2)]
        H = [sb(f"h{s}", [P, G, C if layer == 1 else C + 1]) for s in range(2)]
        chains = 2 if layer == 2 else 1
        XC = [sb(f"xc{n}", [P, G, C]) for n in range(chains)]
        SQ = [sb(f"sq{n}", [P, G, C]) for n in range(chains)]
        mean = [sb(f"mean{n}", [P, G]) for n in range(chains)]
        rstd = [sb(f"rstd{n}", [P, G]) for n in range(chains)]
        centred, squared, var_ready, rstd_ready = (
            [sem(f"{x}{n}") for n in range(chains)] for x in ("centred", "squared", "var_ready", "rstd_ready"))
        zt = [sb(f"zt{b}", [P, TURNS * P]) for b in range(2)]
        pt = [ps(f"pt{b}") for b in range(2)]
        po = [ps(f"po{b}") for b in range(2)]
        loaded = [sem(f"loaded{s}") for s in range(2)]
        stored_x = [sem(f"stored_x{s}") for s in range(2)]
        stored_h = [sem(f"stored_h{s}") for s in range(2)]
        names = ("z_ready", "turned", "zt_ready", "mm_done", "evacuated", "inputs_used", "normed", "pe_turn")
        (z_ready, turned, zt_ready, mm_done, evacuated, inputs_used, normed, pe_turn) = map(sem, names)
        if layer == 0:
            inv_count = [sb(f"inv_count{s}", [P, G]) for s in range(2)]
            dinv = [sb(f"dinv{s}", [P, G]) for s in range(2)]
            deg_ready, dinv_ready = map(sem, ("deg_ready", "dinv_ready"))
        if layer == 2:
            Y = [sb(f"y{s}", [P, G, C]) for s in range(2)]
            TG = [sb(f"tg{s}", [P, G, C]) for s in range(2)]
            u = [sb(f"u{b}", [FF, 2, CH // 2]) for b in range(2)]
            pf = [ctx.enter_context(nc.psum_tensor(f"{n}pf{b}", [P, 2, 512], F32)) for b in range(2)]
            loaded_x = [sem(f"loaded_x{s}") for s in range(2)]
            up_done, gelu_done, t_ready, tg_ready, xa_ready, tail_ready = map(
                sem, ("up_done", "gelu_done", "t_ready", "tg_ready", "xa_ready", "tail_ready"))
        weight = (net.w_upd, net.w_lin, net.w_out)[layer]
        x_in = (net.x_in, net.x1, net.x2)[layer]
        h_in = (net.h0, net.h1d, net.h2)[layer]
        agg = (net.agg0, net.agg1, net.agg2)[layer]
        x_out = (net.x1, net.x2, net.out)[layer]
        h_out = (net.h1d, net.h2, net.term[0])[layer]
        LAST = SUPER - 1
        in_loads = 2 if layer == 2 else 3

        def at(t, d):
            return 2 * t + d, d % 2, t + d // 2

        def attend_phase(j):
            return (2 * j[0] - 1, 1)

        def mlp_phase(j):
            return (2 * j[0] + 2, 0)
        FIRST_PHASE, LAST_PHASE = (0, 0), (2 * LAST + 1, 1)

        with nc.Block() as block:
            @block.sync
            def _(sp):
                def load(c):
                    number, s, _ = c
                    sp.dma_start(A[s][:, :, :], rows_of(agg, number, G)).then_inc(loaded[s], 16)
                    sp.dma_start(Z[s][:, :, 0:hw], rows_of(h_in, number, G)).then_inc(loaded[s], 16)
                    if layer < 2:
                        sp.dma_start(X[s][:, :, :], rows_of(x_in, number, G)).then_inc(loaded[s], 16)

                def load_x(c):
                    number, s, _ = c
                    sp.dma_start(X[s][:, :, :], rows_of(x_in, number, G)).then_inc(loaded_x[s], 16)

                def store_x(c, tile):
                    number, s, _ = c
                    sp.dma_start(rows_of(x_out, number, G), tile[s][:, :, :]).then_inc(stored_x[s], 16)
                load(at(0, 0))
                load(at(0, 1))

                def store_h(c):
                    number, s, _ = c
                    sp.dma_start(rows_of(h_out, number, G), H[s][:, :, :]).then_inc(stored_h[s], 16)
                if layer < 2:
                    def step(c, after=None, before=None):
                        sp.wait_ge(inputs_used, c[0] + 1)
                        if after is not None:
                            load(after)
                        store_x(c, T)
                        if before is not None:
                            sp.wait_ge(normed, before[0] + 1)
                            store_h(before)
                    step(at(0, 0), at(0, 2))
                    step(at(0, 1), at(0, 3), at(0, 0))
                    with sp.Fori(0, SUPER // 2 - 2) as t:
                        for d in (2, 3):
                            step(at(t, d), at(t, d + 2), at(t, d - 1))
                    for d in (LAST - 1, LAST):
                        step(at(0, d), None, at(0, d - 1))
                    sp.wait_ge(normed, SUPER)
                    store_h(at(0, LAST))
                else:
                    load_x(at(0, 0))
                    load_x(at(0, 1))
                    for d in range(2):
                        sp.wait_ge(inputs_used, d + 1)
                        load(at(0, d + 2))

                    def swap_x(t, d):
                        sp.wait_ge(tail_ready, at(t, d)[0] + 1)
                        store_h(at(t, d))
                        store_x(at(t, d), X)
                        sp.wait_ge(stored_x[d % 2], 16 * (at(t, d)[2] + 1))
                        load_x(at(t, d + 2))
                    with sp.Fori(0, SUPER // 2 - 2) as t:
                        for d in range(2):
                            sp.wait_ge(inputs_used, at(t, d + 2)[0] + 1)
                            load(at(t, d + 4))
                            swap_x(t, d)
                    for d in (LAST - 3, LAST - 2):
                        swap_x(0, d)
                    for d in (LAST - 1, LAST):
                        sp.wait_ge(tail_ready, d + 1)
                        store_h(at(0, d))
                        store_x(at(0, d), X)
                for s in range(2):
                    sp.wait_ge(stored_x[s], 16 * (SUPER // 2))
                    sp.wait_ge(stored_h[s], 16 * (SUPER // 2))

            @block.tensor
            def _(pe):
                def turn(source, phase, i, start):
                    q, b = phase[0] * SUBS + i, (phase[1] + i) % 2
                    if not start or i > 1:
                        pe.wait_ge(zt_ready, q - 1)
                    pe.sem_inc(pe_turn, 1)
                    per = J // TURNS
                    for n in range(TURNS):
                        first = i * J + n * per
                        last = nc.tensor.transpose(pt[b][:, n * P:(n + 1) * P],
                                                   source[:, first:first + per, :].rearrange("p j c -> p (j c)"), net.ident[:, :])
                    last.then_inc(turned, 1)

                def set_bias(b, which):
                    nc.tensor.matmul(po[b][:, 0:J * C], net.ones3[:, :],
                                     net.bias_parts[:, which, :, :].rearrange("k j c -> k (j c)"), start=True, stop=False)

                def products(source, phase, start=False):
                    turn(source, phase, 0, start)
                    for i in range(SUBS):
                        q, b = phase[0] * SUBS + i, (phase[1] + i) % 2
                        if i + 1 < SUBS:
                            turn(source, phase, i + 1, start)
                        pe.wait_ge(zt_ready, q + 1)
                        if not start or i > 1:
                            pe.wait_ge(evacuated, q - 1)
                        pe.sem_inc(pe_turn, 1)
                        width = J * C // TURNS
                        set_bias(b, layer)
                        for n in range(TURNS):
                            last = nc.tensor.matmul(po[b][:, n * width:(n + 1) * width], zt[b][:, n * P:(n + 1) * P], weight[:, :],
                                                    start=False, stop=n == TURNS - 1)
                        last.then_inc(mm_done, 1)

                def mlp(c, phase):
                    number, s, _ = c
                    pe.wait_ge(t_ready, number + 1)

                    def up(i):
                        b = (phase[1] + i) % 2
                        pe.wait_ge(zt_ready, phase[0] * SUBS + i + 1)
                        pe.sem_inc(pe_turn, 1)
                        for half in range(2):
                            lanes = slice(half * C, (half + 1) * C)
                            last = nc.tensor.matmul(pf[b][:, half, 0:CH // 2], net.w1[lanes, :], zt[b][lanes, :], start=True, stop=True)
                        last.then_inc(up_done, 1)

                    def down(i):
                        b = (phase[1] + i) % 2
                        pe.wait_ge(gelu_done, number * SUBS + i + 1)
                        pe.wait_ge(evacuated, phase[0] * SUBS + i - 1)
                        pe.sem_inc(pe_turn, 1)
                        set_bias(b, 3)
                        for j in range(J):
                            half, pair = j % 2, j // 2
                            last = nc.tensor.matmul(po[b][:, j * C:(j + 1) * C], u[b][:, half, pair * P:(pair + 1) * P], net.w2[:, :],
                                                    start=False, stop=j == J - 1)
                        last.then_inc(mm_done, 1)
                    turn(T[s], phase, 0, False)
                    turn(T[s], phase, 1, False)
                    up(0)
                    for i in range(SUBS):
                        if i + 1 < SUBS:
                            up(i + 1)
                        if i + 2 < SUBS:
                            turn(T[s], phase, i + 2, False)
                        down(i)
                if layer < 2:
                    def step(c, start=False):
                        pe.wait_ge(z_ready, c[0] + 1)
                        products((Z if layer == 0 else A)[c[1]], (c[0], c[1]), start)
                    step(at(0, 0), True)
                    with pe.Fori(0, SUPER // 2 - 1) as t:
                        step(at(t, 1))
                        step(at(t, 2))
                    step(at(0, LAST))
                else:
                    def attend(c, phase, start=False):
                        pe.wait_ge(loaded[c[1]], 16 * in_loads * (c[2] + 1))
                        products(A[c[1]], phase, start)
                    attend(at(0, 0), FIRST_PHASE, True)
                    attend(at(0, 1), attend_phase(at(0, 1)))
                    mlp(at(0, 0), mlp_phase(at(0, 0)))
                    with pe.Fori(0, SUPER // 2 - 1) as t:
                        for d in (2, 3):
                            attend(at(t, d), attend_phase(at(t, d)))
                            mlp(at(t, d - 1), mlp_phase(at(t, d - 1)))
                    mlp(at(0, LAST), LAST_PHASE)

            @block.scalar
            def _(act):
                def copy(phase, i, start, after_up=False):
                    q, b = phase[0] * SUBS + i, (phase[1] + i) % 2
                    act.wait_ge(turned, q + 1)
                    if not after_up and (not start or i > 1):
                        act.wait_ge(mm_done, q - 1)
                    nc.scalar.activation(zt[b][:, :], pt[b][:, 0:TURNS * P], ACT.Copy).then_inc(zt_ready, 1)

                def gelu(c, phase, i):
                    q, b = phase[0] * SUBS + i, (phase[1] + i) % 2
                    act.wait_ge(up_done, c[0] * SUBS + i + 1)
                    act.wait_ge(mm_done, q - 1)
                    nc.scalar.activation(u[b][:, :, :], pf[b][:, :, 0:CH // 2], ACT.Gelu, bias=net.b1[:, :]).then_inc(gelu_done, 1)

                def square(r, n=0):
                    act.wait_ge(centred[n], r + 1)
                    nc.scalar.activation(SQ[n][:, :, :], XC[n][:, :, :], ACT.Square, scale=C ** -0.5).then_inc(squared[n], 1)

                def root(r, n=0):
                    act.wait_ge(var_ready[n], r + 1)
                    nc.scalar.activation(rstd[n][:, :], rstd[n][:, :], ACT.Sqrt, bias=net.eps[:, :]).then_inc(rstd_ready[n], 1)

                def degree_root(c):
                    act.wait_ge(deg_ready, c[0] + 1)
                    nc.scalar.activation(dinv[c[1]][:, :], dinv[c[1]][:, :], ACT.Sqrt).then_inc(dinv_ready, 1)
                if layer < 2:
                    def step(c, before=None, after=None):
                        for i in range(SUBS):
                            copy((c[0], c[1]), i, before is None)
                            if before is not None:
                                if i == 2:
                                    square(before[0])
                                elif i == 4:
                                    root(before[0])
                            if layer == 0 and after is not None and i == 5:
                                degree_root(after)
                    if layer == 0:
                        degree_root(at(0, 0))
                    step(at(0, 0), after=at(0, 1))
                    with act.Fori(0, SUPER // 2 - 1) as t:
                        for d in (1, 2):
                            step(at(t, d), at(t, d - 1), at(t, d + 1))
                    step(at(0, LAST), at(0, LAST - 1))
                    square(LAST)
                    root(LAST)
                else:
                    def attend(phase, start=False, y=None):
                        for i in range(SUBS):
                            if phase is not None:
                                copy(phase, i, start)
                            if y is not None and i == 5:
                                square(2 * y[0], 1)
                            elif y is not None and i == 6:
                                root(2 * y[0], 1)

                    def mlp(c, phase, t=None, y=None):
                        if c is not None:
                            copy(phase, 0, False)
                        for i in range(SUBS):
                            if c is not None:
                                if i + 1 < SUBS:
                                    copy(phase, i + 1, False, i + 1 > 1)
                                gelu(c, phase, i)
                            if t is not None and i == 2:
                                square(t[0])
                            elif y is not None and i == 5:
                                square(2 * y[0] + 1, 1)
                        if t is not None:
                            root(t[0])
                        if y is not None:
                            root(2 * y[0] + 1, 1)
                    attend(FIRST_PHASE, True)
                    mlp(None, None, t=at(0, 0))
                    attend(attend_phase(at(0, 1)))
                    mlp(at(0, 0), mlp_phase(at(0, 0)), t=at(0, 1))
                    for d in (2, 3):
                        attend(attend_phase(at(0, d)), y=at(0, d - 2))
                        mlp(at(0, d - 1), mlp_phase(at(0, d - 1)), at(0, d), at(0, d - 2))
                    with act.Fori(0, SUPER // 2 - 2) as t:
                        for d in (4, 5):
                            attend(attend_phase(at(t, d)), y=at(t, d - 2))
                            mlp(at(t, d - 1), mlp_phase(at(t, d - 1)), at(t, d), at(t, d - 2))
                    attend(None, y=at(0, LAST - 1))
                    mlp(at(0, LAST), LAST_PHASE, y=at(0, LAST - 1))
                    attend(None, y=at(0, LAST))
                    mlp(None, None, y=at(0, LAST))

            @block.vector
            def _(v):
                def spread(x):
                    return x.unsqueeze(2).to_broadcast([P, G, C])

                def channels(x):
                    return x.unsqueeze(1).to_broadcast([P, G, C])

                def total(x, n=0):
                    nc.vector.tensor_reduce(mean[n][:, :], x, AX.X, ALU.add)

                def centre(x, n=0):
                    v.drain()
                    nc.vector.tensor_scalar(mean[n][:, :], mean[n][:, :], 1.0 / C, None, ALU.mult)
                    v.drain()
                    nc.vector.tensor_tensor(XC[n][:, :, :], x, spread(mean[n][:, :]), ALU.subtract).then_inc(centred[n], 1)

                def variance(r, n=0):
                    v.wait_ge(squared[n], r + 1)
                    nc.vector.tensor_reduce(rstd[n][:, :], SQ[n][:, :, :], AX.X, ALU.add).then_inc(var_ready[n], 1)

                def scale(y, r, n=0, relu=False):
                    v.wait_ge(rstd_ready[n], r + 1)
                    nc.vector.reciprocal(rstd[n][:, :], rstd[n][:, :])
                    v.drain()
                    if relu:
                        return nc.vector.scalar_tensor_tensor(y, XC[n][:, :, :], 0.0, spread(rstd[n][:, :]), ALU.max, ALU.mult)
                    return nc.vector.tensor_tensor(y, XC[n][:, :, :], spread(rstd[n][:, :]), ALU.mult)

                def evacuate(c, phase, i, m):
                    q, b, s = phase[0] * SUBS + i, (phase[1] + i) % 2, c[1]
                    rows = slice(i * J, (i + 1) * J)
                    got = po[b][:, 0:J * C].rearrange("p (j c) -> p j c", c=C)
                    v.wait_ge(mm_done, q + 1)
                    if layer == 0:
                        nc.vector.scalar_tensor_tensor(T[s][:, rows, :], got, 0.0, X[s][:, rows, :], ALU.max, ALU.add).then_inc(evacuated, 1)
                    elif layer == 1:
                        nc.vector.tensor_tensor(T[s][:, rows, :], got, X[s][:, rows, :], ALU.add).then_inc(evacuated, 1)
                    elif m == 0:
                        nc.vector.tensor_tensor(T[s][:, rows, :], got, Z[s][:, rows, :], ALU.add).then_inc(evacuated, 1)
                    else:
                        nc.vector.tensor_tensor(Y[s][:, rows, :], got, TG[s][:, rows, :], ALU.add).then_inc(evacuated, 1)

                def counts(c):
                    number, s, h = c
                    v.wait_ge(loaded[s], 16 * in_loads * (h + 1))
                    nc.vector.tensor_scalar(dinv[s][:, :], A[s][:, :, C], 1.0, None, ALU.max)
                    v.drain()
                    nc.vector.reciprocal(inv_count[s][:, :], dinv[s][:, :]).then_inc(deg_ready, 1)

                def roots(c):
                    v.wait_ge(dinv_ready, c[0] + 1)
                    nc.vector.reciprocal(dinv[c[1]][:, :], dinv[c[1]][:, :])

                if layer < 2:
                    def norm_step(c, i):
                        number, s, h = c
                        if i == 0:
                            total(T[s][:, :, :])
                            if layer == 0:
                                v.wait_ge(stored_h[s], 16 * h)
                                nc.vector.tensor_copy(H[s][:, :, C], dinv[s][:, :])
                        elif i == 1:
                            centre(T[s][:, :, :])
                        elif i == 3:
                            variance(number)
                        elif i == 5:
                            if layer == 1:
                                v.wait_ge(stored_h[s], 16 * h)
                            scale(H[s][:, :, 0:C], number, relu=True).then_inc(normed, 1)

                    def step(c, before=None, after=None):
                        v.wait_ge(stored_x[c[1]], 16 * c[2])
                        v.wait_ge(loaded[c[1]], 16 * in_loads * (c[2] + 1))
                        for i in range(SUBS):
                            evacuate(c, (c[0], c[1]), i, 0)
                            if before is not None:
                                norm_step(before, i)
                            if layer == 0 and after is not None and i == 4:
                                counts(after)
                            elif layer == 0 and after is not None and i == 6:
                                roots(after)
                        v.drain()
                        v.sem_inc(inputs_used, 1)
                    if layer == 0:
                        counts(at(0, 0))
                        roots(at(0, 0))
                    step(at(0, 0), after=at(0, 1))
                    with v.Fori(0, SUPER // 2 - 1) as t:
                        for d in (1, 2):
                            step(at(t, d), at(t, d - 1), at(t, d + 1))
                    step(at(0, LAST), at(0, LAST - 1))
                    for i in range(SUBS):
                        norm_step(at(0, LAST), i)
                else:
                    def attend(c, phase, x=None, t=None, y=None):
                        for i in range(SUBS):
                            if c is not None:
                                if i == 0:
                                    v.wait_ge(loaded[c[1]], 16 * in_loads * (c[2] + 1))
                                evacuate(c, phase, i, 0)
                            if x is not None and i == 0:
                                v.wait_ge(stored_h[x[1]], 16 * x[2])
                                nc.vector.memset(H[x[1]][:, :, C:C + 1], 0.0)
                                scale(H[x[1]][:, :, 0:C], 2 * x[0] + 1, 1, relu=True).then_inc(normed, 1)
                            elif t is not None and i == 1:
                                scale(T[t[1]][:, :, :], t[0]).then_inc(t_ready, 1)
                            elif y is not None and i == 2:
                                centre(Y[y[1]][:, :, :], 1)
                            elif y is not None and i == 5:
                                variance(2 * y[0], 1)
                        v.drain()
                        if c is not None:
                            v.sem_inc(inputs_used, 1)

                    def mlp(c, phase, t=None, y=None):
                        for i in range(SUBS):
                            if c is not None:
                                if i == 0:
                                    v.wait_ge(tg_ready, c[0] + 1)
                                evacuate(c, phase, i, 1)
                            if t is not None:
                                if i == 0:
                                    total(T[t[1]][:, :, :])
                                elif i == 1:
                                    centre(T[t[1]][:, :, :])
                                elif i == 3:
                                    variance(t[0])
                            if y is not None:
                                xs, ys = X[y[1]][:, :, :], Y[y[1]][:, :, :]
                                if i == 0:
                                    scale(ys, 2 * y[0], 1)
                                elif i == 1:
                                    v.drain()
                                    nc.vector.tensor_tensor(ys, ys, channels(net.norms[:, 2, :]), ALU.mult)
                                elif i == 2:
                                    v.drain()
                                    v.wait_ge(xa_ready, y[0] + 1)
                                    nc.vector.tensor_tensor(xs, xs, ys, ALU.add)
                                elif i == 3:
                                    v.drain()
                                    total(xs, 1)
                                elif i == 4:
                                    centre(xs, 1)
                                elif i == 5:
                                    variance(2 * y[0] + 1, 1)
                        v.drain()
                        if c is not None:
                            total(Y[c[1]][:, :, :], 1)
                    attend(at(0, 0), FIRST_PHASE)
                    mlp(None, None, t=at(0, 0))
                    attend(at(0, 1), attend_phase(at(0, 1)), t=at(0, 0))
                    mlp(at(0, 0), mlp_phase(at(0, 0)), t=at(0, 1))
                    attend(at(0, 2), attend_phase(at(0, 2)), None, at(0, 1), at(0, 0))
                    mlp(at(0, 1), mlp_phase(at(0, 1)), at(0, 2), at(0, 0))
                    attend(at(0, 3), attend_phase(at(0, 3)), at(0, 0), at(0, 2), at(0, 1))
                    mlp(at(0, 2), mlp_phase(at(0, 2)), at(0, 3), at(0, 1))
                    with v.Fori(0, SUPER // 2 - 2) as t:
                        for d in (4, 5):
                            attend(at(t, d), attend_phase(at(t, d)), at(t, d - 3), at(t, d - 1), at(t, d - 2))
                            mlp(at(t, d - 1), mlp_phase(at(t, d - 1)), at(t, d), at(t, d - 2))
                    attend(None, None, at(0, LAST - 2), at(0, LAST), at(0, LAST - 1))
                    mlp(at(0, LAST), LAST_PHASE, None, at(0, LAST - 1))
                    attend(None, None, at(0, LAST - 1), None, at(0, LAST))
                    mlp(None, None, None, at(0, LAST))
                    attend(None, None, at(0, LAST))

            @block.gpsimd
            def _(pool):
                if layer < 2:
                    with pool.Fori(0, SUPER // 2) as t:
                        for s in range(2):
                            pool.wait_ge(loaded[s], 16 * in_loads * (t + 1))
                            if layer == 0:
                                pool.wait_ge(deg_ready, 2 * t + s + 1)
                                nc.gpsimd.tensor_tensor(Z[s][:, :, C:P], A[s][:, :, 0:C],
                                                        inv_count[s][:, :].unsqueeze(2).to_broadcast([P, G, C]), ALU.mult).then_inc(z_ready, 1)
                            else:
                                nc.gpsimd.tensor_tensor(A[s][:, :, :], A[s][:, :, :], Z[s][:, :, C:C + 1].to_broadcast([P, G, C]), ALU.mult)
                                pool.drain()
                                nc.gpsimd.tensor_tensor(A[s][:, :, :], A[s][:, :, :], Z[s][:, :, 0:C], ALU.add).then_inc(z_ready, 1)
                else:
                    def channels(which):
                        return net.norms[:, which, :].unsqueeze(1).to_broadcast([P, G, C])

                    def gained(c):
                        pool.wait_ge(t_ready, c[0] + 1)
                        nc.gpsimd.tensor_tensor(TG[c[1]][:, :, :], T[c[1]][:, :, :], channels(0), ALU.mult).then_inc(tg_ready, 1)

                    def offset(c):
                        number, s, h = c
                        pool.wait_ge(loaded_x[s], 16 * (h + 1))
                        nc.gpsimd.tensor_tensor(X[s][:, :, :], X[s][:, :, :], channels(3), ALU.add).then_inc(xa_ready, 1)

                    def tail(c):
                        number, s, h = c
                        pool.wait_ge(normed, number + 1)
                        nc.gpsimd.tensor_tensor(X[s][:, :, :], X[s][:, :, :], H[s][:, :, 0:C], ALU.add).then_inc(tail_ready, 1)
                    offset(at(0, 0))
                    gained(at(0, 0))
                    offset(at(0, 1))
                    gained(at(0, 1))
                    with pool.Fori(0, SUPER // 2 - 1) as t:
                        for d in (2, 3):
                            gained(at(t, d))
                            tail(at(t, d - 2))
                            offset(at(t, d))
                    tail(at(0, LAST - 1))
                    tail(at(0, LAST))


T_ALL = EP // P
BLOCK = 10
DIGITS = 256
LIST_SPARE = 1 + EP + J
LIST_ROWS = LIST_SPARE + SPARE
GROUP = 3
assert (STEPS // 2 - 1) % GROUP == 0 and T_ALL % (4 * BLOCK) == 0
LIST_CHUNKS = -(-EDGES // CH)


def sort_by_source(nc, net):
    with ExitStack() as ctx:
        ctx.callback(nc.all_engine_barrier)
        def sb(name, shape, dt=F32):
            return ctx.enter_context(nc.sbuf_tensor("s_" + name, shape, dt))

        def sem(name):
            return stage_semaphore(nc, ctx, "s_" + name)
        before_f = sb("before_f", [P, P])
        before = sb("before", [P, P], BF16)
        all_ones = sb("all_ones", [P, P], BF16)
        iota_f = sb("iota_f", [P, DIGITS])
        iota = sb("iota", [P, DIGITS], BF16)
        columns = [sb("col_src", [P, T_ALL], I32), sb("col_dst", [P, T_ALL], I32), sb("col_weight", [P, T_ALL])]
        rec = sb("rec", [P, T_ALL, 4], I32)
        part = sb("part", [P, T_ALL], I32)
        digit = sb("digit", [P, T_ALL])
        lane = sb("lane", [P, BLOCK])
        block_hots = [sb(f"block_hots{b}", [P, BLOCK, DIGITS], BF16) for b in range(2)]
        hots = [sb(f"hots{b}", [P, DIGITS], BF16) for b in range(4)]
        picked = [sb(f"picked{b}", [P, DIGITS]) for b in range(2)]
        ones_f = sb("ones_f", [P, T_ALL])
        upto = [sb(f"upto{h}", [P, T_ALL]) for h in range(2)]
        first = [sb(f"first{h}", [P, T_ALL]) for h in range(2)]
        below = sb("below", [P, 2])
        first_hi = [sb(f"first_hi{g}", [T_ALL // 2, DIGITS], BF16) for g in range(2)]
        first_lo = [sb(f"first_lo{g}", [T_ALL // 2, DIGITS], BF16) for g in range(2)]
        rank = sb("rank", [P, BLOCK])
        ri = sb("ri", [P, BLOCK], I32)
        lo7 = sb("lo7", [P, BLOCK], I32)
        hi7 = sb("hi7", [P, BLOCK], I32)
        place = [sb(f"place{b}", [P, BLOCK], I32) for b in range(2)]
        recs = [sb(f"recs{b}", [P, BLOCK, 4], I32) for b in range(2)]
        none = sb("none", [1, 4], I32)
        blank = sb("blank", [P, 4 * T_ALL], I32)
        zeros = sb("zeros", [P, G * (C + 1)])
        cleared = sem("tables_cleared")
        def ps(name):
            return ctx.enter_context(nc.psum_tensor("s_" + name, [P, 512], F32))
        tile_counts = [ps(f"tile_counts{h}") for h in range(2)]
        smaller = ps("smaller")
        by_tile = [ps(f"by_tile{g}") for g in range(2)]
        within = [ps(f"within{b}") for b in range(2)]
        names = ("loaded", "made", "hot", "block_hot", "block_counted", "counted", "ranked", "placed", "pool_turn", "pe_turn", "reloaded", "filled",
                 "summed", "below_ready", "first_ready", "turned", "table_ready")
        (loaded, made, hot, block_hot, block_counted, counted, ranked, placed, pool_turn, pe_turn, reloaded, filled,
         summed, below_ready, first_ready, turned, table_ready) = map(sem, names)
        scattered = [sem(f"scattered{b}") for b in range(2)]
        rounds = T_ALL // (2 * BLOCK)
        with nc.Block() as block:
            @block.sync
            def _(sp):
                sp.dma_start(before_f[:, :], net.dram["c_before"][:, :]).then_inc(loaded, 16)
                sp.dma_start(iota_f[:, :], net.dram["c_iota256"][:, :]).then_inc(loaded, 16)
                for tile, col in zip(columns, (net.src, net.dst_ext[1:1 + EP], net.dram["weight"])):
                    sp.dma_start(tile[:, :], col.rearrange("(p t) -> p t", p=P)).then_inc(loaded, 16)
                sp.wait_ge(made, 1)
                for n in range(2):
                    sp.dma_start(net.lists[n][0:1, :], none[:, :]).then_inc(filled, 16)
                    sp.dma_start(net.lists[n][1 + EP:1 + EP + J, :], blank[0:J, 0:4]).then_inc(filled, 16)
                sp.dma_start(net.lists[1][1:1 + EP, :].rearrange("(p t) c -> p (t c)", p=P), blank[:, :]).then_inc(filled, 16)
                for table in (net.agg0, net.agg1, net.agg2, net.term[1]):
                    wide = table.shape[1]
                    for i in range(SUPER):
                        rows = table[i * P * G:(i + 1) * P * G, :].rearrange("(p g) c -> p (g c)", p=P)
                        sp.dma_start(rows, zeros[:, 0:G * wide]).then_inc(cleared, 16)
                for table in (net.out, *net.term):
                    wide = table.shape[1]
                    rows = table[NP:NP + SPARE, :].rearrange("(p g) c -> p (g c)", p=P)
                    sp.dma_start(rows, zeros[:, 0:SPARE // P * wide]).then_inc(cleared, 16)
                for b in range(2):
                    sp.wait_ge(scattered[b], 16 * BLOCK * rounds)
                sp.dma_start(rec[:, :, :].rearrange("p t c -> p (t c)"),
                             net.half_sorted.rearrange("(p t) c -> p (t c)", p=P)).then_inc(reloaded, 16)
                sp.wait_ge(filled, 5 * 16)
                sp.wait_ge(cleared, (4 * SUPER + 3) * 16)

            @block.vector
            def _(v):
                nc.vector.memset(none[:, :], -1)
                nc.vector.memset(zeros[:, :], 0.0)
                v.drain()
                nc.vector.memset(blank[:, :], 0).then_inc(made, 1)
                nc.vector.memset(all_ones[:, :], 1.0)
                nc.vector.memset(ones_f[:, :], 1.0)
                nc.vector.memset(rec[:, :, :], 0)
                v.wait_ge(loaded, 5 * 16)
                nc.vector.tensor_copy(before[:, :], before_f[:, :])
                nc.vector.tensor_copy(iota[:, :], iota_f[:, :])
                v.drain()
                for c in range(2):
                    nc.vector.tensor_copy(rec[:, :, c], columns[c][:, :])
                nc.vector.tensor_scalar(rec[:, :, 2], columns[2][:, :].bitcast(I32), 0, None, ALU.bitwise_or).then_inc(made, 1)
                v.drain()
                for d in range(2):
                    if d == 1:
                        v.wait_ge(reloaded, 16)
                    nc.vector.tensor_scalar(part[:, :], rec[:, :, 0], 255 if d == 0 else 8, None,
                                            ALU.bitwise_and if d == 0 else ALU.logical_shift_right)
                    v.drain()
                    nc.vector.tensor_copy(digit[:, :], part[:, :])
                    v.drain()
                    with v.Fori(0, rounds) as t:
                        for s in range(2):
                            nc.vector.tensor_copy(lane[:, :], digit[:, bass.ds(BLOCK * (2 * t + s), BLOCK)])
                            v.drain()
                            v.wait_ge(block_counted, 2 * (rounds * d + t) + s + 1)
                            for q in range(BLOCK):
                                last = nc.vector.tensor_scalar(block_hots[s][:, q, :], iota[:, :], lane[:, q:q + 1], None, ALU.is_equal)
                            last.then_inc(block_hot, 1)
                            v.drain()
                    v.wait_ge(block_counted, 2 * rounds * (d + 1) + 2)
                    for h in range(2):
                        nc.vector.tensor_tensor_scan(upto[h][:, :], ones_f[:, :], tile_counts[h][:, 0:T_ALL], 0.0, ALU.mult, ALU.add)
                    v.drain()
                    v.sem_inc(summed, 1)
                    for h in range(2):
                        nc.vector.tensor_tensor(first[h][:, :], upto[h][:, :], tile_counts[h][:, 0:T_ALL], ALU.subtract)
                    v.wait_ge(below_ready, d + 1)
                    nc.vector.tensor_copy(below[:, :], smaller[:, 0:2])
                    v.drain()
                    for h in range(2):
                        last = nc.vector.tensor_scalar(first[h][:, :], first[h][:, :], below[:, h:h + 1], None, ALU.add)
                    last.then_inc(first_ready, 1)
                    v.wait_ge(turned, d + 1)
                    for g in range(2):
                        nc.vector.tensor_copy(first_hi[g][:, :], by_tile[g][0:T_ALL // 2, 0:DIGITS])
                    v.drain()
                    for g in range(2):
                        last = nc.vector.tensor_tensor(first_lo[g][:, :], by_tile[g][0:T_ALL // 2, 0:DIGITS], first_hi[g][:, :], ALU.subtract)
                    last.then_inc(table_ready, 1)
                    with v.Fori(0, rounds) as t:
                        for s in range(2):
                            nc.vector.tensor_copy(lane[:, :], digit[:, bass.ds(BLOCK * (2 * t + s), BLOCK)])
                            v.drain()

                            def one_hot(q):
                                n = s * BLOCK + q
                                nc.vector.tensor_scalar(hots[n % 4][:, :], iota[:, :], lane[:, q:q + 1], None, ALU.is_equal).then_inc(hot, 1)
                            one_hot(0)
                            for q in range(BLOCK):
                                n = s * BLOCK + q
                                if q + 1 < BLOCK:
                                    one_hot(q + 1)
                                v.wait_ge(counted, T_ALL * d + 2 * BLOCK * t + n + 1)
                                nc.vector.tensor_tensor_reduce(out=picked[n % 2][:, :], in0=within[n % 2][:, 0:DIGITS], in1=hots[n % 4][:, :],
                                                               scale=1.0, scalar=0.0, op0=ALU.mult, op1=ALU.add,
                                                               accum_out=rank[:, q:q + 1]).then_inc(ranked, 1)
                            v.drain()
                            v.wait_ge(scattered[s], 16 * BLOCK * (rounds * d + t))
                            nc.vector.tensor_scalar(recs[s][:, :, :], rec[:, bass.ds(BLOCK * (2 * t + s), BLOCK), :], 0, None, ALU.bitwise_or)
                            if d == 0:
                                nc.vector.tensor_copy(ri[:, :], rank[:, :])
                                v.drain()
                                nc.vector.tensor_scalar(lo7[:, :], ri[:, :], P - 1, None, ALU.bitwise_and)
                                nc.vector.tensor_scalar(hi7[:, :], ri[:, :], 7, None, ALU.logical_shift_right)
                                v.drain()
                                nc.vector.scalar_tensor_tensor(place[s][:, :], lo7[:, :], float(T_ALL), hi7[:, :], ALU.mult, ALU.add).then_inc(placed, 1)
                            else:
                                nc.vector.tensor_scalar(place[s][:, :], rank[:, :], 1.0, None, ALU.add).then_inc(placed, 1)
                            v.drain()

            @block.tensor
            def _(pe):
                for _ in range(2):
                    pe.sem_inc(block_counted, 1)
                pe.wait_ge(made, 2)
                HALF = DIGITS // 2
                for d in range(2):
                    with pe.Fori(0, rounds) as t:
                        for s in range(2):
                            pe.wait_ge(block_hot, 2 * (rounds * d + t) + s + 1)
                            pe.sem_inc(pe_turn, 1)
                            for q in range(BLOCK):
                                for h in range(2):
                                    last = nc.tensor.matmul(tile_counts[h][:, bass.ds(BLOCK * (2 * t + s) + q, 1)],
                                                            block_hots[s][:, q, h * HALF:(h + 1) * HALF], all_ones[:, 0:1], start=True, stop=True)
                            last.then_inc(block_counted, 1)
                    pe.wait_ge(summed, d + 1)
                    pe.sem_inc(pe_turn, 1)
                    all_of = [upto[h][:, T_ALL - 1:T_ALL] for h in range(2)]
                    nc.tensor.matmul(smaller[:, 0:1], before_f[:, :], all_of[0], start=True, stop=True)
                    nc.tensor.matmul(smaller[:, 1:2], ones_f[:, 0:P], all_of[0], start=True, stop=False)
                    nc.tensor.matmul(smaller[:, 1:2], before_f[:, :], all_of[1], start=False, stop=True).then_inc(below_ready, 1)
                    pe.wait_ge(first_ready, d + 1)
                    pe.sem_inc(pe_turn, 1)
                    for g in range(2):
                        for h in range(2):
                            last = nc.tensor.transpose(by_tile[g][0:T_ALL // 2, h * P:(h + 1) * P],
                                                       first[h][:, g * (T_ALL // 2):(g + 1) * (T_ALL // 2)], net.ident[:, :])
                    last.then_inc(turned, 1)
                    pe.wait_ge(table_ready, d + 1)
                    pe.sem_inc(pe_turn, 1)
                    for g in range(2):
                        with pe.Fori(0, rounds // 2) as t:
                            for n in range(2 * BLOCK):
                                m = T_ALL * d + T_ALL // 2 * g + 2 * BLOCK * t + n
                                pe.wait_ge(hot, m + 1)
                                pe.wait_ge(ranked, m - 1 if d or g or n > 1 else m - n)
                                pe.sem_inc(pe_turn, 1)
                                row = net.identb[0:T_ALL // 2, bass.ds(2 * BLOCK * t + n, 1)].to_broadcast([T_ALL // 2, P])
                                nc.tensor.matmul(within[n % 2][:, 0:DIGITS], row, first_hi[g][:, :], start=True, stop=False)
                                nc.tensor.matmul(within[n % 2][:, 0:DIGITS], row, first_lo[g][:, :], start=False, stop=False)
                                nc.tensor.matmul(within[n % 2][:, 0:DIGITS], before[:, :], hots[n % 4][:, :], start=False, stop=True).then_inc(counted, 1)

            @block.gpsimd
            def _(pool):
                for d in range(2):
                    table = (net.half_sorted, net.lists[0])[d]
                    with pool.Fori(0, rounds) as t:
                        for s in range(2):
                            pool.wait_ge(placed, 2 * rounds * d + 2 * t + s + 1)
                            pool.sem_inc(pool_turn, 1)
                            for q in range(BLOCK):
                                pool.indirect_dma_start(table[:, :], bass.IndirectOffsetOnAxis(ap=place[s][:, q:q + 1], axis=0),
                                                        recs[s][:, q, :], None).then_inc(scattered[s], 16)
                for s in range(2):
                    pool.wait_ge(scattered[s], 2 * 16 * BLOCK * rounds)


def diffuse(nc, net):
    W = C + 1
    with ExitStack() as ctx:
        ctx.callback(nc.all_engine_barrier)
        def sb(name, shape, dt=F32):
            return ctx.enter_context(nc.sbuf_tensor("d_" + name, shape, dt))

        def ps(name):
            return ctx.enter_context(nc.psum_tensor("d_" + name, [P, 512], F32))

        def sem(name):
            return stage_semaphore(nc, ctx, "d_" + name)
        before_f = sb("before_f", [P, P])
        before = sb("before", [P, P], BF16)
        all_ones = sb("all_ones", [P, P], BF16)
        ratios = sb("ratios", [P, STEPS])
        tcol = sb("tcol", [P, 1])
        pos0 = sb("pos0", [P, J + 2])
        pos0_short = sb("pos0_short", [P, 3])
        node_spare = [sb(f"node_spare{s}", [P, J]) for s in range(2)]
        list_spare = [sb(f"list_spare{s}", [P, J]) for s in range(2)]
        last_step = sb("last_step", [P, 1])
        next_step = sb("next_step", [P, 1])
        coef = sb("coef", [P, 1])
        base = sb("base", [P, 1])
        have = sb("have", [P, 1])
        passed = sb("passed", [P, 1])
        have_i = sb("have_i", [P, 1], I32)
        rec = [sb(f"rec{s}", [P, J + 2, 4], I32) for s in range(2)]
        inside = sb("inside", [P, J + 2])
        srcs = sb("srcs", [P, J + 2])
        keep = sb("keep", [P, J], BF16)
        is_end = sb("is_end", [P, J])
        end_f = sb("end_f", [P, J])
        end = [sb(f"end{s}", [P, J], I32) for s in range(2)]
        near = [sb(f"near{s}", [P, J, W]) for s in range(2)]
        nonzero = sb("nonzero", [P, J, C])
        live = sb("live", [P, J])
        liveb = sb("liveb", [P, J], BF16)
        some = sb("some", [P, J])
        wl = sb("wl", [P, J])
        prod = sb("prod", [P, J, W])
        turned = sb("turned_sb", [W, CH])
        scan = sb("scan", [W, CH])
        carry = sb("carry", [W, 1])
        out = [sb(f"out{s}", [P, J, W]) for s in range(2)]
        counts = sb("counts", [P, 2 * J])
        ahead = sb("ahead", [P, 2])
        upto = sb("upto", [P, J])
        place_f = sb("place_f", [P, J])
        place = [sb(f"place{s}", [P, J], I32) for s in range(2)]
        pt, pk, pr, pc = ps("pt"), ps("pk"), ps("pr"), ps("pc")
        names = ("loaded", "set_up", "ready", "spread", "moved", "scanned", "back",
                 "out_ready", "placed", "stepped", "turn_sp", "turn_pool", "turn_pe", "seen", "step_turn")
        (loaded, set_up, ready, spread, moved, scanned, back,
         out_ready, placed, stepped, turn_sp, turn_pool, turn_pe, seen, step_turn) = map(sem, names)
        rec_loaded, gathered, stored, passed_on = (
            [sem(f"{x}{s}") for s in range(3)] for x in ("rec_loaded", "gathered", "stored", "passed_on"))
        SHORT = 2

        class Counts:
            def __init__(self, engine, name):
                self.engine = engine
                self.begun = [engine.alloc_register(f"begun{s}_{name}") for s in range(3)]
                self.done = [engine.alloc_register(f"done{s}_{name}") for s in range(3)]
                self.passed = [engine.alloc_register(f"passed{s}_{name}") for s in range(3)]
                self.total = engine.alloc_register(f"total_{name}")
                self.meetings = engine.alloc_register(f"meetings_{name}")
                for r in (*self.begun, *self.done, *self.passed, self.total, self.meetings):
                    engine.reg_mov(r, 0)

            def read(self, register):
                return self.engine.snap(register, min_val=0, max_val=STEPS * (CHUNKS + 1))

            def finished(self, s, first):
                self.engine.reg_add(self.done[s], self.done[s], 1)
                if not first:
                    self.engine.reg_add(self.passed[s], self.passed[s], 1)
                self.engine.reg_add(self.total, self.total, 1)

        def rows_per_partition(s):
            return 1 if s == SHORT else J

        def nothing(*_):
            pass

        def list_length(engine):
            return engine.value_load(have_i[0:1, 0:1], min_val=0, max_val=EDGES)

        def step_chunks(engine, n, edges, begin, finish, parity, first):
            def start(c, s):
                begin(parity, first, c, s, n)
                engine.reg_add(n.begun[s], n.begun[s], 1)

            def end_of(s):
                finish(parity, first, s, n)
                n.finished(s, first)
            tiles = engine.snap((edges + (P - 1)) >> 7, min_val=0, max_val=-(-EDGES // P))
            chunks = engine.snap((edges + (CH - 1)) >> 9, min_val=0, max_val=LIST_CHUNKS)
            pairs = engine.snap(chunks >> 1, min_val=0, max_val=LIST_CHUNKS // 2)
            odd = engine.snap(chunks - 2 * pairs, min_val=0, max_val=1)
            with engine.If(tiles > 1):
                start(0, 0)
                with engine.If(pairs > 0):
                    with engine.Fori(0, pairs) as t:
                        start(2 * t + 1, 1)
                        end_of(0)
                        start(2 * t + 2, 0)
                        end_of(1)
                with engine.If(odd > 0):
                    end_of(0)
            if not first:
                with engine.If(tiles == 1):
                    start(0, SHORT)
                    end_of(SHORT)

        def all_steps(engine, one_step, length):
            one_step(1, 1, True)
            with engine.Fori(0, (STEPS // 2 - 1) // GROUP) as g:
                with engine.If(length() > 0):
                    with engine.Fori(0, GROUP) as t:
                        one_step(2 * GROUP * g + 2 * t + 2, 0, False)
                        one_step(2 * GROUP * g + 2 * t + 3, 1, False)
            one_step(STEPS, 0, False)

        def steps(engine, name, begin, finish):
            n = Counts(engine, name)

            def meet():
                engine.reg_add(n.meetings, n.meetings, 1)
                engine.wait_ge(stepped, n.read(n.meetings))
                engine.sem_inc(step_turn, 1)
                return list_length(engine)

            def one_step(k, parity, first):
                step_chunks(engine, n, meet(), begin, finish, parity, first)
                engine.sem_inc(seen, 1)

            def length():
                edges = meet()
                engine.sem_inc(seen, 1)
                return edges
            all_steps(engine, one_step, length)

        with nc.Block() as block:
            @block.sync
            def _(sp):
                for dst, src in ((before_f, "c_before"), (ratios, "c_ratios"), (pos0, "c_pos0"), (pos0_short, "c_pos0_short"),
                                 (node_spare[0], "c_node_spare"), (list_spare[0], "c_list_spare")):
                    sp.dma_start(dst[:, :], net.dram[src][:, :]).then_inc(loaded, 16)
                sp.dma_start(tcol[:, :], net.dram["L3_gnn_t"][None, :].to_broadcast([P, 1])).then_inc(loaded, 16)

                def begin(parity, first, c, s, n):
                    for x in range(3):
                        if x % 2 == s % 2:
                            sp.wait_ge(gathered[x], n.read(n.begun[x]) * (16 * rows_per_partition(x)))
                            sp.sem_inc(turn_sp, 1)
                            sp.wait_ge(passed_on[x], n.read(n.passed[x]) * (16 * rows_per_partition(x)))
                            sp.sem_inc(turn_sp, 1)
                    sp.wait_ge(placed, n.read(n.total))
                    sp.sem_inc(turn_sp, 1)
                    rows = net.lists[0 if first else parity]
                    if s == SHORT:
                        for i in range(3):
                            sp.dma_start(rec[0][:, i, :], rows[i:P + i, :]).then_inc(rec_loaded[s], 16)
                    else:
                        sp.dma_start(rec[s][:, 0:J, :], rows[bass.ds(c * CH, CH), :].rearrange("(p j) c -> p j c", j=J)).then_inc(rec_loaded[s], 16)
                        sp.dma_start(rec[s][:, J:J + 2, :], rows[bass.ds(c * CH + J, CH), :].rearrange("(p j) c -> p j c", j=J)[:, 0:2, :]).then_inc(rec_loaded[s], 16)
                steps(sp, "sp", begin, nothing)

            @block.gpsimd
            def _(pool):
                def begin(parity, first, c, s, n):
                    loads = 3 if s == SHORT else 2
                    pool.wait_ge(rec_loaded[s], n.read(n.begun[s]) * (16 * loads) + 16 * loads)
                    pool.sem_inc(turn_pool, 1)
                    for j in range(rows_per_partition(s)):
                        pool.indirect_dma_start(near[s % 2][:, j, :], None, net.term[1 - parity][:, :],
                                                bass.IndirectOffsetOnAxis(ap=rec[s % 2][:, 1 + j, 1:2], axis=0)).then_inc(gathered[s], 16)

                def finish(parity, first, s, n):
                    k = n.read(n.total)
                    tile = s % 2
                    pool.wait_ge(placed, k + 1)
                    pool.sem_inc(turn_pool, 1)
                    if not first:
                        for j in range(rows_per_partition(s)):
                            pool.indirect_dma_start(net.lists[1 - parity][:, :], bass.IndirectOffsetOnAxis(ap=place[tile][:, j:j + 1], axis=0),
                                                    rec[tile][:, 1 + j, :], None).then_inc(passed_on[s], 16)
                    pool.wait_ge(out_ready, k + 1)
                    pool.sem_inc(turn_pool, 1)
                    for j in range(rows_per_partition(s)):
                        pool.indirect_dma_start(net.term[parity][:, :], bass.IndirectOffsetOnAxis(ap=end[tile][:, j:j + 1], axis=0),
                                                out[tile][:, j, :], None).then_inc(stored[s], 16)
                        pool.indirect_dma_start(net.out[:, :], bass.IndirectOffsetOnAxis(ap=end[tile][:, j:j + 1], axis=0),
                                                out[tile][:, j, 0:C], None, compute_op=ALU.add).then_inc(stored[s], 16)
                steps(pool, "pool", begin, finish)

            @block.tensor
            def _(pe):
                pe.wait_ge(set_up, 1)

                def finish(parity, first, s, n):
                    k = n.read(n.total)
                    rows = rows_per_partition(s)
                    pe.wait_ge(ready, k + 1)
                    pe.sem_inc(turn_pe, 1)
                    nc.tensor.matmul(pc[:, 0:rows], before[:, :], liveb[:, 0:rows], start=True, stop=True)
                    nc.tensor.matmul(pc[:, J:J + rows], all_ones[:, :], liveb[:, 0:rows], start=True, stop=True)
                    for j in range(rows):
                        nc.tensor.matmul(pk[0:W, j:P * rows:rows], keep[:, j:j + 1].to_broadcast([P, W]), net.identb[:, :], start=True, stop=True)
                    for j in range(rows):
                        last = nc.tensor.transpose(pt[0:W, j:P * rows:rows], prod[:, j, :], net.ident[:, :])
                    last.then_inc(spread, 1)
                    pe.wait_ge(scanned, k + 1)
                    pe.sem_inc(turn_pe, 1)
                    for j in range(rows):
                        last = nc.tensor.transpose(pr[:, j * W:(j + 1) * W], scan[:, j:P * rows:rows], net.ident[0:W, 0:W])
                    last.then_inc(back, 1)
                steps(pe, "pe", nothing, finish)

            @block.scalar
            def _(act):
                def finish(parity, first, s, n):
                    k = n.read(n.total)
                    edges = P * rows_per_partition(s)
                    act.wait_ge(spread, k + 1)
                    nc.scalar.activation(turned[:, 0:edges], pt[0:W, 0:edges], ACT.Copy).then_inc(moved, 1)
                steps(act, "act", nothing, finish)

            @block.vector
            def _(v):
                v.wait_ge(loaded, 7 * 16)
                nc.vector.tensor_copy(before[:, :], before_f[:, :])
                nc.vector.memset(all_ones[:, :], 1.0)
                for spare in (node_spare, list_spare):
                    nc.vector.tensor_scalar(spare[1][:, :], spare[0][:, :], float(CH), None, ALU.add)
                nc.vector.memset(carry[:, :], 0.0)
                nc.vector.tensor_scalar(tcol[:, :], tcol[:, :], 1e-8, -1.0 / N_SUB, ALU.max, ALU.mult)
                nc.vector.memset(last_step[:, :], 0.0)
                nc.vector.memset(next_step[:, :], 2.0)
                nc.vector.memset(base[:, :], 0.0)
                nc.vector.memset(passed[:, :], 0.0)
                nc.vector.memset(have[:, :], float(EDGES))
                nc.vector.memset(have_i[:, :], EDGES)
                v.drain()
                nc.vector.tensor_scalar(ratios[:, :], ratios[:, :], tcol[:, :], None, ALU.mult).then_inc(set_up, 1)
                v.drain()
                n = Counts(v, "v")

                def finish(parity, first, s, n):
                    k = n.read(n.total)
                    begun, done = n.read(n.begun[s]), n.read(n.done[s])
                    J = rows_per_partition(s)
                    edges, tile = P * J, s % 2
                    by_partition = pc[:, 0:8].rearrange("p (a j) -> p a j", a=2)
                    positions = pos0_short if s == SHORT else pos0
                    r, node, spare = rec[tile][:, 0:J + 2, :], node_spare[tile][:, 0:J], list_spare[tile][:, 0:J]
                    v.wait_ge(rec_loaded[s], begun * (16 * (3 if s == SHORT else 2)))
                    nc.vector.tensor_scalar(inside[:, 0:J + 2], positions[:, :], base[:, :], have[:, :], ALU.add, ALU.is_lt)
                    v.drain()
                    nc.vector.scalar_tensor_tensor(srcs[:, 0:J + 2], r[:, :, 0], 1.0, inside[:, 0:J + 2], ALU.add, ALU.mult)
                    v.drain()
                    nc.vector.tensor_tensor(keep[:, 0:J], srcs[:, 1:J + 1], srcs[:, 0:J], ALU.is_equal)
                    nc.vector.tensor_tensor(is_end[:, 0:J], srcs[:, 1:J + 1], srcs[:, 2:J + 2], ALU.not_equal)
                    nc.vector.tensor_scalar(end_f[:, 0:J], srcs[:, 1:J + 1], -1.0, None, ALU.add)
                    v.drain()
                    nc.vector.tensor_tensor(end_f[:, 0:J], end_f[:, 0:J], node, ALU.subtract)
                    nc.vector.tensor_tensor(is_end[:, 0:J], is_end[:, 0:J], inside[:, 1:J + 1], ALU.mult)
                    v.drain()
                    nc.vector.tensor_tensor(end_f[:, 0:J], end_f[:, 0:J], is_end[:, 0:J], ALU.mult)
                    v.drain()
                    if s != SHORT:
                        v.wait_ge(stored[s], done * (32 * J))
                        v.wait_ge(passed_on[s], n.read(n.passed[s]) * (16 * J))
                    nc.vector.tensor_tensor(end[tile][:, 0:J], end_f[:, 0:J], node, ALU.add)
                    v.wait_ge(gathered[s], begun * (16 * J))
                    nc.vector.tensor_scalar(nonzero[:, 0:J, :], near[tile][:, 0:J, 0:C], 0.0, None, ALU.not_equal)
                    nc.vector.tensor_scalar(live[:, 0:J], near[tile][:, 0:J, C], last_step[:, :], None, ALU.is_equal)
                    v.drain()
                    nc.vector.tensor_reduce(some[:, 0:J], nonzero[:, 0:J, :], AX.X, ALU.max)
                    nc.vector.tensor_tensor(live[:, 0:J], live[:, 0:J], inside[:, 1:J + 1], ALU.mult)
                    v.drain()
                    nc.vector.tensor_tensor(live[:, 0:J], live[:, 0:J], some[:, 0:J], ALU.mult)
                    v.drain()
                    nc.vector.tensor_copy(liveb[:, 0:J], live[:, 0:J])
                    nc.vector.scalar_tensor_tensor(wl[:, 0:J], r[:, 1:J + 1, 2].bitcast(F32), coef[:, :], live[:, 0:J], ALU.mult, ALU.mult)
                    nc.vector.tensor_copy(prod[:, 0:J, C], live[:, 0:J])
                    v.drain()
                    nc.vector.tensor_tensor(prod[:, 0:J, 0:C], near[tile][:, 0:J, 0:C], wl[:, 0:J].unsqueeze(2).to_broadcast([P, J, C]),
                                            ALU.mult).then_inc(ready, 1)
                    nc.vector.tensor_tensor_scan(upto[:, 0:J], all_ones[:, 0:J], live[:, 0:J], 0.0, ALU.mult, ALU.add)
                    v.drain()
                    nc.vector.tensor_tensor(upto[:, 0:J], upto[:, 0:J], live[:, 0:J], ALU.subtract)
                    v.wait_ge(spread, k + 1)
                    nc.vector.tensor_copy(counts[:, 0:2 * J].rearrange("p (a j) -> p a j", a=2), by_partition[:, :, 0:J])
                    v.drain()
                    nc.vector.tensor_reduce(ahead[:, :], counts[:, 0:2 * J].rearrange("p (a j) -> p a j", a=2), AX.X, ALU.add)
                    v.drain()
                    nc.vector.tensor_scalar(place_f[:, 0:J], upto[:, 0:J], ahead[:, 0:1], passed[:, :], ALU.add, ALU.add)
                    v.drain()
                    nc.vector.scalar_tensor_tensor(place_f[:, 0:J], place_f[:, 0:J], 1.0, spare, ALU.add, ALU.subtract)
                    nc.vector.tensor_tensor(passed[:, :], passed[:, :], ahead[:, 1:2], ALU.add)
                    nc.vector.tensor_scalar(base[:, :], base[:, :], float(CH), None, ALU.add)
                    v.drain()
                    nc.vector.tensor_tensor(place_f[:, 0:J], place_f[:, 0:J], live[:, 0:J], ALU.mult)
                    v.drain()
                    nc.vector.tensor_tensor(place[tile][:, 0:J], place_f[:, 0:J], spare, ALU.add).then_inc(placed, 1)
                    v.wait_ge(moved, k + 1)
                    nc.vector.tensor_tensor_scan(scan[:, 0:edges], pk[0:W, 0:edges], turned[:, 0:edges], carry[:, :], ALU.mult, ALU.add).then_inc(scanned, 1)
                    v.drain()
                    nc.vector.tensor_copy(carry[:, :], scan[:, edges - 1:edges])
                    v.wait_ge(back, k + 1)
                    sums = pr[:, 0:J * W].rearrange("p (j c) -> p j c", c=W)
                    nc.vector.tensor_scalar(out[tile][:, 0:J, C], sums[:, :, C], 0.0, next_step[:, :], ALU.is_gt, ALU.mult)
                    nc.vector.tensor_copy(out[tile][:, 0:J, 0:C], sums[:, :, 0:C])
                    v.drain()
                    nc.vector.tensor_scalar(out[tile][:, 0:J, C], out[tile][:, 0:J, C], -1.0, None, ALU.add).then_inc(out_ready, 1)

                def length():
                    v.reg_add(n.meetings, n.meetings, 1)
                    v.drain()
                    v.sem_inc(stepped, 1)
                    return list_length(v)

                def one_step(k, parity, first):
                    nc.vector.tensor_copy(coef[:, :], ratios[:, bass.ds(k - 1, 1)])
                    step_chunks(v, n, length(), nothing, finish, parity, first)
                    for s in range(3):
                        rows = rows_per_partition(s)
                        v.wait_ge(gathered[s], n.read(n.begun[s]) * (16 * rows))
                        v.wait_ge(stored[s], n.read(n.done[s]) * (32 * rows))
                        v.wait_ge(passed_on[s], n.read(n.passed[s]) * (16 * rows))
                    v.wait_ge(seen, n.read(n.meetings) * 4)
                    if not first:
                        nc.vector.tensor_copy(have[:, :], passed[:, :])
                        nc.vector.tensor_copy(have_i[:, :], passed[:, :])
                    for x in (last_step, next_step):
                        nc.vector.tensor_scalar(x[:, :], x[:, :], 1.0, None, ALU.add)
                    nc.vector.memset(base[:, :], 0.0)
                    v.drain()
                    nc.vector.memset(passed[:, :], 0.0)
                    v.drain()
                all_steps(v, one_step, length)


INPUTS = ["x", "src", "dst", "edge_type_8", "edge_weight", "L0_gnn_W_msg", "L0_gnn_b_msg", "L0_gnn_W_upd", "L0_gnn_b_upd",
          "L1_gnn_W", "L1_gnn_b", "L2_gnn_task_embedding", "L2_gnn_Wq", "L2_gnn_bq", "L2_gnn_Wk", "L2_gnn_bk", "L2_gnn_Wv",
          "L2_gnn_bv", "L2_gnn_ek_tab", "L2_gnn_ev_tab", "L2_gnn_es_tab", "L2_gnn_eg_tab", "L2_gnn_Wo", "L2_gnn_bo",
          "L2_gnn_ln1_g", "L2_gnn_ln1_b", "L2_gnn_W1", "L2_gnn_b1", "L2_gnn_W2", "L2_gnn_b2", "L2_gnn_ln2_g",
          "L2_gnn_ln2_b", "L2_gnn_Wf", "L2_gnn_bf", "L3_gnn_t"]


def host_layout(inputs):
    a = {k: np.ascontiguousarray(np.asarray(inputs[k])) for k in INPUTS}
    pad = EP - EDGES
    o = {k: v for k, v in a.items() if k not in ("x", "src", "dst", "edge_type_8", "edge_weight", "L1_gnn_W")}
    o["L1_gnn_WT"] = np.ascontiguousarray(a["L1_gnn_W"].T)
    o["x"] = np.concatenate([a["x"], np.zeros((NP - NODES, C), np.float32)])
    psrc = (NODES + np.arange(pad) % 128).astype(np.int32)
    pdst = np.full(pad, NP - 1, np.int32)
    o["src"] = np.concatenate([a["src"], psrc])
    one = np.full(1, -1, np.int32)
    o["dst_ext"] = np.concatenate([one, a["dst"], pdst, one, one, one])
    o["etype"] = np.concatenate([a["edge_type_8"], np.zeros(pad, np.int32)])
    o["weight"] = np.concatenate([a["edge_weight"], np.zeros(pad, np.float32)])
    o["c_before"] = np.triu(np.ones((P, P), np.float32), 1)
    o["c_iota256"] = np.broadcast_to(np.arange(DIGITS, dtype=np.float32), (P, DIGITS)).copy()
    o["c_ratios"] = np.broadcast_to(np.array(step_ratios(), np.float32), (P, STEPS)).copy()
    row = (np.arange(P)[:, None] * J + np.arange(J)[None, :]).astype(np.float32)
    o["c_pos0"] = (np.arange(P)[:, None] * J + np.arange(-1, J + 1)[None, :]).astype(np.float32)
    o["c_pos0_short"] = (np.arange(P)[:, None] + np.arange(-1, 2)[None, :]).astype(np.float32)
    o["c_node_spare"] = row + np.float32(NP)
    o["c_list_spare"] = row + np.float32(LIST_SPARE)
    o["c_ident"] = np.eye(P, dtype=np.float32)
    o["c_ones"] = np.ones((1, P), np.float32)
    o["c_iota8"] = np.broadcast_to(np.arange(3 * NET, dtype=np.float32) % NET, (P, J, 3 * NET)).copy()
    head = np.arange(C) // HD
    o["c_head_sum"] = np.where(head[:, None] == np.concatenate([head, np.arange(NH)])[None, :], HD ** -0.5, 0.0).astype(np.float32)
    return o


def program(nc, dram, out):
    net = Net()
    net.dram = dram
    net.x_in, net.src, net.dst_ext, net.etype, net.out = dram["x"], dram["src"], dram["dst_ext"], dram["etype"], out

    def table(name, rows, cols, dt=F32):
        return nc.dram_tensor(name, [rows, cols], dt, kind="Internal").ap()
    net.h0 = table("h0", NP, C)
    net.h1d = table("h1d", NP, C + 1)
    net.h2 = table("h2", NP, C)
    net.x1 = table("x1", NP, C)
    net.x2 = table("x2", NP, C)
    net.agg0 = table("agg0", NP, C + 1)
    net.agg1 = table("agg1", NP, C)
    net.agg2 = table("agg2", NP, C)
    net.term = [table(f"term{p}", NP + SPARE, C + 1) for p in range(2)]
    net.half_sorted = table("half_sorted", EP, 4, I32)
    net.lists = [table(f"list{p}", LIST_ROWS, 4, I32) for p in range(2)]
    with ExitStack() as ctx:
        allocate(nc, ctx, net)
        prepare(nc, net)
        sort_by_source(nc, net)
        first_norm(nc, net)
        for layer in range(3):
            if layer < 2:
                edge_sums(nc, net, layer)
            else:
                attention_sums(nc, net)
            node_update(nc, net, layer)
        diffuse(nc, net)


def kernel(**inputs):
    import concourse.bacc as bacc
    from concourse.bass_utils import run_bass_kernel_spmd
    nc = bacc.Bacc("TRN2", target_bir_lowering=False, num_devices=1)
    arrays = {f"in_{k}": v for k, v in host_layout(inputs).items()}
    dram = {k[3:]: nc.dram_tensor(k, v.shape, mybir.dt.from_np(v.dtype), kind="ExternalInput").ap() for k, v in arrays.items()}
    out = nc.dram_tensor("out", [NP + SPARE, C], F32, kind="ExternalOutput").ap()
    program(nc, dram, out)
    r = run_bass_kernel_spmd(nc, [arrays], core_ids=[0])
    return r.results[0]["out"][:NODES]
```
